# Optimizing a Trainium2 kernel written in Bass

```python
import numpy as np
import jax
import jax.numpy as jnp

def _softmax(x, axis=-1):
    return jax.nn.softmax(x, axis=axis)

def _gelu(x):
    return jax.nn.gelu(x, approximate=True)

def _silu(x):
    return jax.nn.silu(x)

def _sigmoid(x):
    return jax.nn.sigmoid(x)

def _layernorm(x, axis=-1, eps=1e-05):
    m = jnp.mean(x, axis=axis, keepdims=True)
    v = jnp.var(x, axis=axis, keepdims=True)
    return (x - m) / jnp.sqrt(v + eps)

def _scatter_add(tgt, idx, src, axis=0):
    return tgt.at[idx].add(src)

def _segment_sum(src, seg, n):
    return jax.ops.segment_sum(src, seg, n)
kernel_name = 'mk_audio_tower_d1_tok_audfeat512_r4_056e57'

def setup_inputs(seed: int=0):
    np.random.seed(seed)
    _w = jnp.asarray

    def _rec_inputs():
        import jax
        import jax.numpy as jnp
        _rk = jax.random.key(seed)
        x = -0.00190633 + 1.00279 * jax.random.normal(jax.random.fold_in(_rk, 1), (64, 64, 7), jnp.float32)
        return x
    x = _rec_inputs()

    def _L0_tok_setup():
        import jax, jax.numpy as jnp
        import numpy as np
        SIG_DEPTH = 4

        def _outer(a, b):
            return (a[:, :, None] * b[:, None, :]).reshape(a.shape[0], -1)
        key = jax.random.key(seed)
        k1, k2 = jax.random.split(key)
        B, L, Cin = (64, 64, 7)
        out_dim = 128
        C = Cin + 1
        sig_channels = sum((C ** k for k in range(1, SIG_DEPTH + 1)))
        inp = jax.random.normal(k1, (B, L, Cin), dtype=jnp.float32)
        W = jax.random.normal(k2, (out_dim, sig_channels), dtype=jnp.float32) * 0.02
        b = jnp.zeros((out_dim,), dtype=jnp.float32)
        return {'inp': inp, 'W': W, 'b': b}
    _L0_tok_all = _L0_tok_setup()
    _L0_tok_in = {k: v for k, v in _L0_tok_all.items() if k in ('W', 'b')}
    del _L0_tok_all

    def _L0_attn_setup():
        import jax, jax.numpy as jnp
        import numpy as np
        HEADS = 8
        DIM_HEAD = 64
        NEG_MAX = -jnp.finfo(jnp.float32).max

        def _sn_weight(W, u, sigma):
            v = jax.lax.stop_gradient(W @ u)
            v = v / jnp.linalg.norm(v)
            u2 = jax.lax.stop_gradient(W.T @ v)
            u2 = u2 / jnp.linalg.norm(u2)
            v = jax.lax.stop_gradient(v)
            u2 = jax.lax.stop_gradient(u2)
            sig = jnp.einsum('c,cd,d->', v, W, u2)
            return W / sig * sigma
        key = jax.random.key(seed)
        ks = jax.random.split(key, 5)
        dim, inner = (128, HEADS * DIM_HEAD)
        x = jax.random.normal(ks[0], (4, 512, dim), dtype=jnp.float32)
        w_qkv = 0.02 * jax.random.normal(ks[1], (3 * inner, dim), dtype=jnp.float32)
        u_qkv = jax.random.normal(ks[2], (dim,), dtype=jnp.float32)
        u_qkv = u_qkv / jnp.linalg.norm(u_qkv)
        w_out = 0.02 * jax.random.normal(ks[3], (dim, inner), dtype=jnp.float32)
        b_out = jnp.zeros((dim,), dtype=jnp.float32)
        u_out = jax.random.normal(ks[4], (inner,), dtype=jnp.float32)
        u_out = u_out / jnp.linalg.norm(u_out)
        sigma_qkv = jnp.array(1.0, dtype=jnp.float32)
        sigma_out = jnp.array(1.0, dtype=jnp.float32)
        temperature = jnp.log(jnp.array(DIM_HEAD ** (-0.5), dtype=jnp.float32))
        return {'x': x, 'w_qkv': w_qkv, 'u_qkv': u_qkv, 'sigma_qkv': sigma_qkv, 'w_out': w_out, 'b_out': b_out, 'u_out': u_out, 'sigma_out': sigma_out, 'temperature': temperature}
    _L0_attn_all = _L0_attn_setup()
    _L0_attn_in = {k: v for k, v in _L0_attn_all.items() if k in ('w_qkv', 'u_qkv', 'sigma_qkv', 'w_out', 'b_out', 'u_out', 'sigma_out', 'temperature')}
    del _L0_attn_all

    def _L0_ffn_setup():
        import jax, jax.numpy as jnp
        import numpy as np
        E = 8
        K = 1
        D = 128
        I = 512
        B, T = (2, 512)
        key = jax.random.key(seed)
        ks = jax.random.split(key, 7)
        s = 0.02
        x = jax.random.normal(ks[0], (B, T, D), jnp.float32)
        gate_w = jax.random.normal(ks[1], (E, D), jnp.float32) * s
        w1 = jax.random.normal(ks[2], (E, I, D), jnp.float32) * s
        w2 = jax.random.normal(ks[3], (E, D, I), jnp.float32) * s
        w3 = jax.random.normal(ks[4], (E, I, D), jnp.float32) * s
        sw1 = jax.random.normal(ks[5], (I, D), jnp.float32) * s
        sw2 = jax.random.normal(ks[6], (D, I), jnp.float32) * s
        return {'x': x, 'gate_w': gate_w, 'w1': w1, 'w2': w2, 'w3': w3, 'sw1': sw1, 'sw2': sw2}
    _L0_ffn_all = _L0_ffn_setup()
    _L0_ffn_in = {k: v for k, v in _L0_ffn_all.items() if k in ('gate_w', 'w1', 'w2', 'w3', 'sw1', 'sw2')}
    del _L0_ffn_all
    return {'x': x, 'L0_tok_W': _L0_tok_in['W'], 'L0_tok_b': _L0_tok_in['b'], 'L0_attn_w_qkv': _L0_attn_in['w_qkv'], 'L0_attn_u_qkv': _L0_attn_in['u_qkv'], 'L0_attn_sigma_qkv': _L0_attn_in['sigma_qkv'], 'L0_attn_w_out': _L0_attn_in['w_out'], 'L0_attn_b_out': _L0_attn_in['b_out'], 'L0_attn_u_out': _L0_attn_in['u_out'], 'L0_attn_sigma_out': _L0_attn_in['sigma_out'], 'L0_attn_temperature': _L0_attn_in['temperature'], 'L0_ffn_gate_w': _L0_ffn_in['gate_w'], 'L0_ffn_w1': _L0_ffn_in['w1'], 'L0_ffn_w2': _L0_ffn_in['w2'], 'L0_ffn_w3': _L0_ffn_in['w3'], 'L0_ffn_sw1': _L0_ffn_in['sw1'], 'L0_ffn_sw2': _L0_ffn_in['sw2']}

def reference(x, L0_tok_W, L0_tok_b, L0_attn_w_qkv, L0_attn_u_qkv, L0_attn_sigma_qkv, L0_attn_w_out, L0_attn_b_out, L0_attn_u_out, L0_attn_sigma_out, L0_attn_temperature, L0_ffn_gate_w, L0_ffn_w1, L0_ffn_w2, L0_ffn_w3, L0_ffn_sw1, L0_ffn_sw2):
    import jax
    import jax.numpy as jnp

    def _L0_tok_ref(inp, W, b):
        import jax, jax.numpy as jnp
        import numpy as np
        SIG_DEPTH = 4

        def _outer(a, b):
            return (a[:, :, None] * b[:, None, :]).reshape(a.shape[0], -1)
        B, L, Cin = inp.shape
        t = jnp.broadcast_to(jnp.linspace(0.0, 1.0, L, dtype=inp.dtype)[None, :, None], (B, L, 1))
        x = jnp.concatenate([t, inp], axis=-1)
        C = Cin + 1
        d = SIG_DEPTH
        dx = jnp.transpose(x[:, 1:] - x[:, :-1], (1, 0, 2))
        init = tuple((jnp.zeros((B, C ** (k + 1)), x.dtype) for k in range(d)))

        def step(levels, v):
            e = [v]
            for k in range(1, d):
                e.append(_outer(e[-1], v) / (k + 1))
            new = []
            for k in range(d):
                acc = levels[k] + e[k]
                for i in range(k):
                    acc = acc + _outer(levels[i], e[k - 1 - i])
                new.append(acc)
            sig = jnp.concatenate(new, axis=-1)
            return (tuple(new), sig)
        _, sigs = jax.lax.scan(step, init, dx)
        sigs = jnp.transpose(sigs, (1, 0, 2))
        return sigs @ W.T + b

    def _L0_attn_ref(x, w_qkv, u_qkv, sigma_qkv, w_out, b_out, u_out, sigma_out, temperature):
        import jax, jax.numpy as jnp
        import numpy as np
        HEADS = 8
        DIM_HEAD = 64
        NEG_MAX = -jnp.finfo(jnp.float32).max

        def _sn_weight(W, u, sigma):
            v = jax.lax.stop_gradient(W @ u)
            v = v / jnp.linalg.norm(v)
            u2 = jax.lax.stop_gradient(W.T @ v)
            u2 = u2 / jnp.linalg.norm(u2)
            v = jax.lax.stop_gradient(v)
            u2 = jax.lax.stop_gradient(u2)
            sig = jnp.einsum('c,cd,d->', v, W, u2)
            return W / sig * sigma
        b, n, _ = x.shape
        Wq = _sn_weight(w_qkv, u_qkv, sigma_qkv)
        qkv = x @ Wq.T
        q, k, v = jnp.split(qkv, 3, axis=-1)

        def heads(t):
            return t.reshape(b, n, HEADS, DIM_HEAD).transpose(0, 2, 1, 3)
        q, k, v = (heads(q), heads(k), heads(v))
        dots = jnp.einsum('bhid,bhjd->bhij', q, k) * jnp.exp(temperature)
        eye = jnp.eye(n, dtype=bool)
        dots = jnp.where(eye, NEG_MAX, dots)
        attn = jax.nn.softmax(dots, axis=-1)
        out = jnp.einsum('bhij,bhjd->bhid', attn, v)
        out = out.transpose(0, 2, 1, 3).reshape(b, n, HEADS * DIM_HEAD)
        Wo = _sn_weight(w_out, u_out, sigma_out)
        return out @ Wo.T + b_out

    def _L0_ffn_ref(x, gate_w, w1, w2, w3, sw1, sw2):
        import jax, jax.numpy as jnp
        import numpy as np
        E = 8
        K = 1
        D = 128
        I = 512
        B, T = (2, 512)
        xf = x.reshape(-1, D)
        logits = xf @ gate_w.T
        wts, idx = jax.lax.top_k(logits, K)
        wts = jax.nn.softmax(wts, axis=-1)
        comb = jnp.einsum('nke,nk->ne', jax.nn.one_hot(idx, E, dtype=xf.dtype), wts)
        h = jax.nn.silu(jnp.einsum('nd,eid->nei', xf, w1)) * jnp.einsum('nd,eid->nei', xf, w3)
        y = jnp.einsum('nei,edi->nd', h * comb[:, :, None], w2)
        y = y + jax.nn.gelu(xf @ sw1.T, approximate=False) @ sw2.T
        return y.reshape(x.shape)
    h = _L0_tok_ref(x, L0_tok_W, L0_tok_b)
    h = h + _L0_attn_ref(_layernorm(h, axis=-1), L0_attn_w_qkv, L0_attn_u_qkv, L0_attn_sigma_qkv, L0_attn_w_out, L0_attn_b_out, L0_attn_u_out, L0_attn_sigma_out, L0_attn_temperature)
    h = h + _L0_ffn_ref(_layernorm(h, axis=-1), L0_ffn_gate_w, L0_ffn_w1, L0_ffn_w2, L0_ffn_w3, L0_ffn_sw1, L0_ffn_sw2)
    return h

_drawn_inputs = setup_inputs


def setup_inputs(seed=0):
    import zlib

    import numpy as np

    out = dict(_drawn_inputs(seed))
    spreads = {'L0_tok_b': (0.0, 0.8), 'L0_attn_b_out': (0.0, 0.8)}
    factors = {'L0_attn_w_qkv': 4.773,
     'L0_attn_u_qkv': 8.0,
     'L0_attn_w_out': 4.83,
     'L0_attn_u_out': 8.0,
     'L0_ffn_gate_w': 8.0,
     'L0_ffn_w1': 8.0,
     'L0_ffn_w2': 8.0,
     'L0_ffn_w3': 8.0,
     'L0_ffn_sw1': 8.0,
     'L0_ffn_sw2': 8.0}
    for name, (base, spread) in spreads.items():
        noise = np.random.default_rng([zlib.crc32(name.encode()), seed]).standard_normal(out[name].shape)
        drawn = base * np.exp(spread * noise) if base else spread * noise
        out[name] = jnp.asarray(drawn.astype(out[name].dtype))
    for name, factor in factors.items():
        out[name] = (out[name] * factor).astype(out[name].dtype)
    return out
```

```python
from contextlib import ExitStack

import concourse.bass as bass
from concourse import mybir

F32 = mybir.dt.float32
BF16 = mybir.dt.bfloat16
I32 = mybir.dt.int32
U32 = mybir.dt.uint32
ALU = mybir.AluOpType
ACT = mybir.ActivationFunctionType
AX = mybir.AxisListType.X

P = 128
SEQS, LEN, CHANNELS = 64, 64, 8
TILES = SEQS * LEN // P
DIM = 128
HEADS, HEAD_DIM = 8, 64
PAIRS = HEADS // 2
INNER = HEADS * HEAD_DIM
EXPERTS, HIDDEN = 8, 512
HC = HIDDEN // P
SORTED = TILES + EXPERTS - 1
ROW = DIM + 1
C2 = CHANNELS * CHANNELS
C3 = C2 * CHANNELS
LOW = 1 + CHANNELS + C2
UC = C3 // P
EPS = 1e-5
NO_TOKEN = 1 << 20
GROUP = 4
GROUPS = TILES // GROUP
FILL = SORTED // 3
SMALL_STEPS, NORM_STEPS, ROUTE_STEPS = 15, 11, 21
SQUARED_STEP = 7


def spread(ap, axis, shape):
    return ap.unsqueeze(axis).to_broadcast(shape)


def build(nc, x_next, x_prev, w_low, w_high, tok_b, wqkv_t, wqkv, u_qkv, wout_t, wout, u_out, b_out,
          scalars, gate_t, w13_t, w2_t, sw1_t, sw2_t, square, mask_c, steps, out):
    with ExitStack() as ctx:
        def sb(name, shape, dt=F32):
            return ctx.enter_context(nc.sbuf_tensor(name, shape, dt))

        def sem(name):
            return ctx.enter_context(nc.semaphore(name))

        sorted_rows = nc.dram_tensor("sorted_rows", [SORTED * P, ROW], F32, kind="Internal").ap()

        xn_in = sb("xn_in", [P, TILES, CHANNELS])
        xp_in = sb("xp_in", [P, TILES, CHANNELS])
        wlow = sb("wlow", [LOW, CHANNELS * DIM])
        whigh = sb("whigh", [P, UC, CHANNELS * DIM])
        tokb = sb("tokb", [P, DIM])
        wqkvT = sb("wqkvT", [P, 3 * INNER])
        wqkv_sb = sb("wqkv_sb", [P, 3 * INNER // P, DIM])
        uq = sb("uq", [P, 1])
        woutT = sb("woutT", [P, PAIRS, DIM])
        wout_sb = sb("wout_sb", [P, INNER])
        uo = sb("uo", [P, PAIRS])
        bout = sb("bout", [P, DIM])
        scal = sb("scal", [P, 3])
        gateT = sb("gateT", [P, EXPERTS])
        w13 = sb("w13", [P, EXPERTS, 2 * HIDDEN])
        w2 = sb("w2", [P, EXPERTS, HC, DIM])
        sw1 = sb("sw1", [P, HIDDEN])
        sw2 = sb("sw2", [P, HC, DIM])
        sq = sb("sq", [P, 5, P])
        ident, before, upto, below, ones = (sq[:, n, :] for n in range(5))
        ident_b = sb("ident_b", [P, P], BF16)
        mask = sb("mask", [P, C3], BF16)
        stepc = sb("stepc", [P, EXPERTS + TILES + SORTED])
        rev_expert = stepc[:, 0:EXPERTS]
        tile_edges = stepc[:, EXPERTS:EXPERTS + TILES]
        tile_index = stepc[:, EXPERTS + TILES:]

        v = sb("v", [P, TILES, CHANNELS])
        vh = sb("vh", [P, TILES, CHANNELS])
        t3 = sb("t3", [P, TILES, CHANNELS])
        t4 = sb("t4", [P, TILES, CHANNELS])
        low = sb("low", [P, TILES, LOW])
        e2 = sb("e2", [P, TILES, C2])
        g3 = sb("g3", [P, TILES, C2])

        e3 = sb("e3", [P, C3])
        g4 = sb("g4", [P, C3])
        low_tile = sb("low_tile", [P, LOW])
        ut = sb("ut", [P, UC, P])
        lowt = sb("lowt", [LOW, P])
        z = sb("z", [P, CHANNELS, DIM])
        maskf = z[:].rearrange("p c d -> p (c d)")[:, 0:C3]

        h = sb("h", [P, TILES, DIM])
        hb = sb("hb", [P, DIM])
        xn = sb("xn", [P, DIM])
        xT = sb("xT", [P, P])
        qz = sb("qz", [P, PAIRS, 2, 2, LEN])
        kT = sb("kT", [P, PAIRS, P])
        vv = sb("vv", [P, INNER])
        rowmax = sb("rowmax", [P, HEADS])
        prob = sb("prob", [P, HEADS, LEN])
        rowsum = sb("rowsum", [P, HEADS])
        rinv = sb("rinv", [P, HEADS])
        pn = sb("pn", [P, HEADS, LEN])
        pz = sb("pz", [P, PAIRS, 2, 2, LEN])
        oT = sb("oT", [P, PAIRS, P])
        stats = sb("stats", [P, 2, 6])
        meanvar = sb("meanvar", [P, 2, 2])
        rstd = sb("rstd", [P, 2, 2])
        powers = sb("powers", [P, 2])
        scrap = sb("scrap", [P, 1])
        x2 = sb("x2", [P, TILES, ROW])
        x2T = sb("x2T", [P, TILES * P])
        x2t = sb("x2t", [P, P])
        x2n = sb("x2n", [P, DIM])
        logits = sb("logits", [P, TILES, EXPERTS])

        wu = sb("wu", [P, 3 * INNER // P + 1])
        wtwu = sb("wtwu", [P, 1 + PAIRS])
        sqs = sb("sqs", [P, 32])
        nrm = sb("nrm", [P, 4])
        fac = sb("fac", [P, 8])

        def taker(*hosts):
            parts = [[t[:].rearrange("p a b -> p (a b)"), 0] for t in hosts]

            def take(*shape):
                size = 1
                for n in shape:
                    size *= n
                for part in parts:
                    flat, at = part
                    if at + size <= flat.shape[1]:
                        part[1] = at + size
                        ap = flat[:, at:at + size]
                        names = "abcd"[:len(shape)]
                        if len(shape) == 1:
                            return ap
                        return ap.rearrange(f"p ({' '.join(names)}) -> p {' '.join(names)}",
                                            **dict(zip(names, shape)))
                raise AssertionError("no room")
            return take

        late = taker(wqkv_sb, low, e2, g3)

        oh = late(TILES, EXPERTS)
        pick = late(TILES, EXPERTS)
        best = sb("best", [P, 2, TILES])
        tot = late(EXPERTS, TILES)
        incl = late(EXPERTS, TILES)
        zeros = late(EXPERTS * TILES)
        rt = sb("rt", [P, 8, EXPERTS])
        off = late(EXPERTS, TILES)
        over = late(EXPERTS, TILES)
        pos_f = late(TILES)
        pos = sb("pos", [P, TILES], U32)
        upt = late(SORTED, EXPERTS)
        exp_f = late(SORTED)
        exp_i = sb("exp_i", [P, SORTED], I32)

        gh = taker(whigh)(2, HC, GROUP * P)
        rows = late(2, ROW)
        ids = sb("ids", [P, SORTED], U32)
        rowsT = late(2, P)
        act = late(2, HIDDEN)
        hid = late(2, HIDDEN)
        hidT = late(2, HC, P)
        y = late(2, DIM)
        fill = w2[:].rearrange("p e c d -> p (e c d)")[:, 0:FILL * ROW].rearrange("p (t r) -> p t r", r=ROW)

        B = [ctx.enter_context(nc.psum_tensor(f"bank{n}", [P, 512], F32)) for n in range(8)]

        ld_x, ld_c, ld_sn, ld_sig, ld_att, ld_ffn = (sem(f"loaded_{n}") for n in
                                                     ("x", "const", "norms", "signature", "attention", "ffn"))
        filled, fill_sent = sem("fill_written"), sem("fill_sent")
        consts_cast = sem("consts_cast")
        pads_zeroed = sem("pads_zeroed")
        ids_written = sem("ids_written")
        small, s1_psum, s2_psum = sem("small_levels"), sem("s1_psum"), sem("s2_psum")
        norm_root, norm_mm, norm_step, exp_temp = sem("norm_root"), sem("norm_matmul"), sem("norm_step"), sem("exp_temperature")
        e3_ready, u4_psum, u4_sb = sem("e3_ready"), sem("u4_psum"), sem("u4_sb")
        y_psum, z_sb, h_psum, h_read = sem("y_psum"), sem("z_sb"), sem("h_psum"), sem("h_read")
        ln1, ln2, xn_ready, xT_psum, xT_sb = sem("ln1"), sem("ln2"), sem("xn_ready"), sem("xT_psum"), sem("xT_sb")
        q_psum, k_psum, v_psum = sem("q_psum"), sem("k_psum"), sem("v_psum")
        q_sb, k_sb, v_sb = sem("q_sb"), sem("k_sb"), sem("v_sb")
        s_psum, soft, exp_done = sem("scores_psum"), sem("softmax_step"), sem("exp_done")
        shifted, sum_inv, pn_ready = sem("shifted"), sem("sum_inverse"), sem("pn_ready")
        p_psum, pA_sb, pB_sb = sem("probT_psum"), sem("probT_first_seq"), sem("probT_second_seq")
        o_psum, o_sb, att_psum, h2_done = sem("o_psum"), sem("o_sb"), sem("attention_psum"), sem("h2_done")
        x2_ready, x2T_psum, x2T_sb = sem("x2_ready"), sem("x2T_psum"), sem("x2T_sb")
        lg_psum, lg_sb = sem("logits_psum"), sem("logits_sb")
        x2_kept = sem("x2_kept")
        rooted = [sem("ln1_rooted"), sem("ln2_rooted")]
        powers_set = sem("powers_set")
        route, rank_psum, pos_ready, scattered = sem("route_step"), sem("rank_psum"), sem("pos_ready"), sem("scattered")
        up_psum, gelu_done, down_psum, added = sem("up_psum"), sem("gelu_done"), sem("down_psum"), sem("added")
        out_sent = [sem(f"out_sent{n}") for n in range(GROUPS)]
        rows_in = [sem(f"rows_in{n}") for n in range(2)]
        id_kept = sem("id_kept")
        rT_psum, rT_sb = sem("rowsT_psum"), sem("rowsT_sb")
        eu_psum, silu_done, hid_done = sem("expert_up_psum"), sem("silu_done"), sem("hid_done")
        hT_psum, hT_sb, ed_psum, y_done = sem("hidT_psum"), sem("hidT_sb"), sem("expert_down_psum"), sem("y_done")
        y_sent = [sem(f"y_sent{n}") for n in range(2)]

        nc_block = ctx.enter_context(nc.Block())
        block = nc_block

        @block.sync
        def _(sp):
            sp.dma_start(xn_in[:], x_next).then_inc(ld_x, 16)
            sp.dma_start(xp_in[:], x_prev).then_inc(ld_x, 16)
            sp.dma_start(sq[:], square).then_inc(ld_c, 16)
            sp.dma_start(maskf[:], mask_c).then_inc(ld_c, 16)
            sp.dma_start(stepc[:], steps).then_inc(ld_c, 16)
            sp.dma_start(tokb[:], tok_b).then_inc(ld_c, 16)
            sp.dma_start(whigh[:], w_high).then_inc(ld_sig, 16)
            sp.dma_start(wlow[:], w_low).then_inc(ld_sig, 16)
            sp.dma_start(wqkvT[:], wqkv_t).then_inc(ld_att, 16)
            sp.dma_start(woutT[:], wout_t).then_inc(ld_att, 16)
            sp.dma_start(bout[:], b_out).then_inc(ld_att, 16)
            sp.dma_start(gateT[:], gate_t).then_inc(ld_att, 16)
            sp.dma_start(wqkv_sb[:], wqkv).then_inc(ld_sn, 16)
            sp.dma_start(wout_sb[:], wout).then_inc(ld_sn, 16)
            sp.dma_start(uq[:], u_qkv).then_inc(ld_sn, 16)
            sp.dma_start(uo[:], u_out).then_inc(ld_sn, 16)
            sp.dma_start(scal[:], scalars).then_inc(ld_sn, 16)
            sp.dma_start(sw1[:], sw1_t).then_inc(ld_ffn, 16)
            sp.dma_start(sw2[:], sw2_t).then_inc(ld_ffn, 16)
            sp.dma_start(w13[:], w13_t).then_inc(ld_ffn, 16)
            sp.wait_ge(filled, 1)
            for n in range(SORTED // FILL):
                sp.dma_start(sorted_rows[n * FILL * P:(n + 1) * FILL * P, :].rearrange("(t p) r -> p t r", p=P),
                             fill[:]).then_inc(fill_sent, 16)
            sp.wait_ge(fill_sent, 16 * (SORTED // FILL))
            sp.dma_start(w2[:], w2_t).then_inc(ld_ffn, 16)
            for g in range(GROUPS):
                sp.wait_ge(added, g + 1)
                sp.dma_start(out[g * GROUP * P:(g + 1) * GROUP * P, :].rearrange("(t p) d -> p t d", p=P),
                             h[:, g * GROUP:(g + 1) * GROUP, :]).then_inc(out_sent[g], 16)
                if g == 0:
                    sp.wait_ge(scattered, 16 * TILES)
                    for j in range(2):
                        sp.dma_start(rows[:, j, :], sorted_rows[j * P:(j + 1) * P, :]).then_inc(rows_in[j], 16)
            with sp.Fori(2, SORTED - 2, 2) as j:
                for k in range(2):
                    sp.wait_ge(rT_psum, j + (k - 1))
                    sp.wait_ge(id_kept, j + (k - 1))
                    sp.dma_start(rows[:, k, :], sorted_rows[bass.ds((j + k) * P, P), :]).then_inc(rows_in[k], 16)
            sp.wait_ge(rT_psum, SORTED - 2)
            sp.wait_ge(id_kept, SORTED - 2)
            sp.dma_start(rows[:, 0, :], sorted_rows[(SORTED - 1) * P:SORTED * P, :]).then_inc(rows_in[0], 16)

        @block.gpsimd
        def _(pool):
            nc.gpsimd.memset(fill[:, :, 0:DIM], 0.0)
            nc.gpsimd.memset(fill[:, :, DIM:ROW].bitcast(I32), NO_TOKEN).then_inc(filled, 1)
            nc.gpsimd.memset(powers[:, 0:1], -0.5).then_inc(powers_set, 1)
            nc.gpsimd.memset(powers[:, 1:2], 0.5).then_inc(powers_set, 1)
            pool.wait_ge(powers_set, 2)
            nc.gpsimd.memset(qz[:], 0.0).then_inc(pads_zeroed, 1)
            nc.gpsimd.memset(pz[:], 0.0).then_inc(pads_zeroed, 1)
            nc.gpsimd.iota(x2[:, :, DIM:ROW].bitcast(I32), pattern=[[P, TILES], [1, 1]], base=0,
                           channel_multiplier=1).then_inc(ids_written, 1)

            def level3(s, first=False):
                if not first:
                    pool.wait_ge(u4_psum, s)
                shape = [P, 1, C2, CHANNELS]
                def by3(t):
                    return t[:].rearrange("p (o a c) -> p o a c", o=1, c=CHANNELS)
                nc.gpsimd.tensor_tensor(by3(e3), spread(low[:, bass.ds(s, 1), 1 + CHANNELS:LOW], 3, shape),
                                        spread(v[:, bass.ds(s, 1), :], 2, shape), ALU.mult)
                nc.gpsimd.tensor_tensor(by3(g4), spread(g3[:, bass.ds(s, 1), :], 3, shape),
                                        spread(vh[:, bass.ds(s, 1), :], 2, shape), ALU.mult)
                nc.gpsimd.tensor_copy(low_tile[:], low[:, bass.ds(s, 1), :].rearrange("p o a -> p (o a)")) \
                    .then_inc(e3_ready, 1)

            def root(n, done, t):
                pool.wait_ge(done, 3 * t + 3)
                nc.gpsimd.tensor_tensor(rstd[:, n, 1:2], rstd[:, n, 0:1], powers[:, 0:1], ALU.pow) \
                    .then_inc(rooted[n], 1)

            def normalise(t):
                pool.wait_ge(sum_inv, t + 1)
                nc.gpsimd.tensor_tensor(pn[:], prob[:], spread(rinv[:], 2, [P, HEADS, LEN]), ALU.mult) \
                    .then_inc(pn_ready, 1)
                root(1, ln2, t)
                pool.wait_ge(x2_ready, t + 1)
                nc.gpsimd.tensor_copy(x2[:, bass.ds(t, 1), 0:DIM], x2n[:].unsqueeze(1)).then_inc(x2_kept, 1)

            pool.wait_ge(small, SMALL_STEPS)
            level3(0, True)
            pool.wait_ge(norm_step, SQUARED_STEP)
            nc.gpsimd.tensor_tensor(fac[:, 2:4], fac[:, 2:4], powers[:, 1:2].to_broadcast([P, 2]), ALU.pow) \
                .then_inc(norm_root, 1)
            level3(1)
            with pool.Fori(0, TILES - 2) as i:
                root(0, ln1, i)
                level3(i + 2)
                normalise(i)
            for t in range(TILES - 2, TILES):
                root(0, ln1, t)
                normalise(t)

            pool.wait_ge(pos_ready, 1)
            pool.wait_ge(x2_kept, TILES)
            pool.wait_ge(ids_written, 1)
            pool.wait_ge(fill_sent, 16 * (SORTED // FILL))
            for t in range(TILES):
                nc.gpsimd.indirect_dma_start(
                    out=sorted_rows[:, :], out_offset=bass.IndirectOffsetOnAxis(ap=pos[:, t:t + 1], axis=0),
                    in_=x2[:, t, :], in_offset=None).then_inc(scattered, 16)
            for g in range(GROUPS):
                pool.wait_ge(out_sent[g], 16)
            for j in range(SORTED):
                pool.wait_ge(y_done, j + 1)
                nc.gpsimd.indirect_dma_start(
                    out=out[:, :], out_offset=bass.IndirectOffsetOnAxis(ap=ids[:, j:j + 1], axis=0),
                    in_=y[:, j % 2, :], in_offset=None, bounds_check=TILES * P - 1, oob_is_err=False,
                    compute_op=ALU.add).then_inc(y_sent[j % 2], 16)
            pool.wait_ge(y_sent[0], 16 * ((SORTED + 1) // 2))
            pool.wait_ge(y_sent[1], 16 * (SORTED // 2))

        @block.scalar
        def _(a):
            a.wait_ge(ld_sn, 80)
            nc.scalar.activation(fac[:, 0:1], scal[:, 2:3], ACT.Exp).then_inc(exp_temp, 1)
            a.wait_ge(norm_step, NORM_STEPS)
            a.wait_ge(pads_zeroed, 2)

            def signature(s):
                a.wait_ge(u4_psum, s + 1)
                nc.scalar.copy(ut[:].rearrange("p c t -> p (c t)"), B[0][:]).then_inc(u4_sb, 1)
                nc.scalar.copy(lowt[:], B[3][0:LOW, 0:P]).then_inc(u4_sb, 1)

            def attention(t):
                a.wait_ge(xT_psum, t + 1)
                nc.scalar.copy(xT[:], B[4][:, 0:P]).then_inc(xT_sb, 1)
                a.wait_ge(q_psum, t + 1)
                for half in range(2):
                    part = slice(half * HEAD_DIM, (half + 1) * HEAD_DIM)
                    nc.scalar.activation(qz[part, :, :, half, :],
                                         B[5][part, :].rearrange("p (c s q) -> p c s q", c=PAIRS, s=2),
                                         ACT.Copy, scale=fac[part, 1:2]).then_inc(q_sb, 1)
                a.wait_ge(v_psum, t + 1)
                nc.scalar.copy(vv[:], B[7][:]).then_inc(v_sb, 1)
                a.wait_ge(shifted, t + 1)
                nc.scalar.activation(prob[:], prob[:], ACT.Exp).then_inc(exp_done, 1)
                a.wait_ge(p_psum, t + 1)
                nc.scalar.copy(pz[0:LEN, :, 0, :, :],
                               B[5][0:LEN, :].rearrange("k (c h q) -> k c h q", c=PAIRS, h=2)).then_inc(pA_sb, 1)
                a.wait_ge(o_psum, t + 1)
                nc.scalar.copy(oT[:].rearrange("p c t -> p (c t)"), B[6][:]).then_inc(o_sb, 1)
                a.wait_ge(x2T_psum, t + 1)
                nc.scalar.copy(x2t[:], B[4][:, 0:P]).then_inc(x2T_sb, 1)
                a.wait_ge(x2T_sb, 2 * t + 1)
                nc.scalar.copy(x2T[:, bass.ds(t * P, P)], x2t[:]).then_inc(x2T_sb, 1)

            signature(0)
            with a.Fori(0, TILES - 1) as i:
                signature(i + 1)
                attention(i)
            attention(TILES - 1)

            with a.Fori(0, GROUPS - 1, 2) as g:
                for k in range(2):
                    for c in range(HC):
                        a.wait_ge(up_psum, (g + k) * HC + (c + 1))
                        nc.scalar.activation(gh[:, k, c, :], B[c][:], ACT.Gelu).then_inc(gelu_done, 1)

            def silu(j, k):
                a.wait_ge(eu_psum, j + 1)
                nc.scalar.activation(act[:, k, :], B[1 + 2 * k][:], ACT.Silu).then_inc(silu_done, 1)

            def rows_transposed(j, k):
                a.wait_ge(rT_psum, j + 1)
                nc.scalar.copy(rowsT[:, k, :], B[0][:, 0:P]).then_inc(rT_sb, 1)

            def result(j, k, reused=True):
                a.wait_ge(ed_psum, j + 1)
                if reused:
                    a.wait_ge(y_sent[k], (j - k) * 8)
                nc.scalar.copy(y[:, k, :], B[6][:, 0:DIM]).then_inc(y_done, 1)

            rows_transposed(0, 0)
            rows_transposed(1, 1)
            silu(0, 0)
            for j in range(3):
                silu(j + 1, (j + 1) % 2)
                rows_transposed(j + 2, j % 2)
                if j >= 1:
                    result(j - 1, (j - 1) % 2, False)
            with a.Fori(3, SORTED - 3, 2) as i:
                for k in range(2):
                    silu(i + (k + 1), k)
                    rows_transposed(i + (k + 2), 1 - k)
                    result(i + (k - 1), k)
            silu(SORTED - 1, 0)
            for j in range(SORTED - 3, SORTED):
                result(j, j % 2)

        @block.vector
        def _(d):
            V = nc.vector
            d.wait_ge(ld_x, 32)
            n_small = 0

            def step(ins):
                nonlocal n_small
                ins.then_inc(small, 1)
                n_small += 1
                d.wait_ge(small, n_small)

            lev = [P, TILES, CHANNELS, CHANNELS]

            def outer(out_, left, right):
                return V.tensor_tensor(out_.rearrange("p t (a c) -> p t a c", c=CHANNELS), spread(left, 3, lev),
                                       spread(right, 2, lev), ALU.mult)

            s1 = B[1][:, 0:TILES * CHANNELS].rearrange("p (t c) -> p t c", c=CHANNELS)
            step(V.tensor_tensor(v[:], xn_in[:], xp_in[:], ALU.subtract))
            V.memset(low[:, :, 0:1], 1.0)
            V.tensor_scalar(vh[:], v[:], 0.5, None, ALU.mult)
            d.wait_ge(s1_psum, 1)
            f2 = low[:, :, 1:1 + CHANNELS]
            step(V.scalar_tensor_tensor(f2, v[:], 0.5, s1, ALU.mult, ALU.add))
            step(outer(e2[:], f2, v[:]))
            V.scalar_tensor_tensor(t3[:], v[:], 1.0 / 3.0, s1, ALU.mult, ALU.add)
            step(V.scalar_tensor_tensor(t4[:], v[:], 0.25, s1, ALU.mult, ALU.add))
            step(outer(low[:, :, 1 + CHANNELS:LOW], t3[:], vh[:]))
            step(V.tensor_scalar(t3[:], v[:], 1.0 / 3.0, None, ALU.mult))
            step(outer(g3[:], t4[:], t3[:]))
            d.wait_ge(s2_psum, 1)
            per = 512 // C2
            for n in range(TILES // per):
                s2 = B[2 + n][:].rearrange("p (t c) -> p t c", c=C2)
                ts = slice(n * per, (n + 1) * per)
                for into in (low[:, ts, 1 + CHANNELS:LOW], g3[:, ts, :]):
                    step(V.tensor_tensor(into, into, s2, ALU.add))
            assert n_small == SMALL_STEPS

            d.wait_ge(ld_c, 64)
            V.tensor_copy(ident_b[:], ident).then_inc(consts_cast, 1)
            V.tensor_copy(mask[:], maskf[:]).then_inc(consts_cast, 1)
            nq = 3 * INNER // P
            n_norm = 0

            def nstep(ins):
                nonlocal n_norm
                ins.then_inc(norm_step, 1)
                n_norm += 1
                d.wait_ge(norm_step, n_norm)

            d.wait_ge(norm_mm, 1)
            nstep(V.tensor_copy(wu[:], B[6][:, 0:nq + 1]))
            d.wait_ge(norm_mm, 2)
            nstep(V.tensor_copy(wtwu[:], B[7][:, 0:1 + PAIRS]))
            V.tensor_tensor(sqs[:, 0:nq], wu[:, 0:nq], wu[:, 0:nq], ALU.mult)
            V.tensor_tensor(sqs[:, nq:nq + 1], wu[:, nq:nq + 1], wu[:, nq:nq + 1], ALU.mult)
            nstep(V.tensor_tensor(sqs[:, 16:17 + PAIRS], wtwu[:], wtwu[:], ALU.mult))
            V.reduce_sum(nrm[:, 0:1], sqs[:, 0:nq], axis=AX)
            V.tensor_copy(nrm[:, 1:2], sqs[:, 16:17])
            V.tensor_copy(nrm[:, 2:3], sqs[:, nq:nq + 1])
            nstep(V.reduce_sum(nrm[:, 3:4], sqs[:, 17:17 + PAIRS], axis=AX))
            d.wait_ge(norm_mm, 3)
            nstep(V.tensor_copy(sqs[:, 0:4], B[6][:, 32:36]))
            nstep(V.reciprocal(fac[:, 6:8], sqs[:, 1:4:2]))
            nstep(V.tensor_tensor(fac[:, 2:4], sqs[:, 0:4:2], fac[:, 6:8], ALU.mult))
            d.wait_ge(norm_root, 1)
            nstep(V.tensor_tensor(fac[:, 4:6], fac[:, 2:4], scal[:, 0:2], ALU.mult))
            d.wait_ge(exp_temp, 1)
            nstep(V.tensor_tensor(fac[:, 1:2], fac[:, 4:5], fac[:, 4:5], ALU.mult))
            nstep(V.tensor_tensor(fac[:, 1:2], fac[:, 1:2], fac[:, 0:1], ALU.mult))
            nstep(V.tensor_tensor(fac[:, 6:7], fac[:, 4:5], fac[:, 5:6], ALU.mult))
            assert n_norm == NORM_STEPS

            def one(ap):
                return ap.rearrange("p o c -> p (o c)")

            def carry():
                V.tensor_copy(scrap[:], ones[:, 0:1])

            def layer_norm(n, done, t, src, dst):
                V.bn_stats(stats[:, n, :], src).then_inc(done, 1)
                d.wait_ge(done, 3 * t + 1)
                carry()
                V.bn_aggr(meanvar[:, n, :], stats[:, n, :]).then_inc(done, 1)
                d.wait_ge(done, 3 * t + 2)
                V.tensor_scalar(rstd[:, n, 0:1], meanvar[:, n, 1:2], EPS, None, ALU.add).then_inc(done, 1)
                d.wait_ge(rooted[n], t + 1)
                return V.tensor_scalar(dst, src, meanvar[:, n, 0:1], rstd[:, n, 1:2], ALU.subtract, ALU.mult)

            def weigh(s, half):
                cs = slice(half * 4, half * 4 + 4)
                d.wait_ge(y_psum, 2 * s + (half + 1))
                V.tensor_tensor(z[:, cs, :], B[1 + half][:].rearrange("p (c d) -> p c d", c=4),
                                spread(v[:, bass.ds(s, 1), cs].rearrange("p o c -> p (o c)"), 2, [P, 4, DIM]),
                                ALU.mult).then_inc(z_sb, 1)

            def iteration(t, sig, kept=True):
                d.wait_ge(h_psum, t + 1)
                ht = one(h[:, bass.ds(t, 1), :])
                V.tensor_tensor(ht, B[3][:, P:P + DIM], tokb[:], ALU.add).then_inc(h_read, 1)
                d.wait_ge(h_read, t + 1)
                V.tensor_tensor(hb[:], ht, bout[:], ALU.add)
                layer_norm(0, ln1, t, ht, xn[:]).then_inc(xn_ready, 1)
                if sig:
                    weigh(t + 1, 0)
                d.wait_ge(k_psum, t + 1)
                V.tensor_copy(kT[:].rearrange("p c t -> p (c t)"), B[6][:]).then_inc(k_sb, 1)
                d.wait_ge(s_psum, t + 1)
                sc = B[4][:].rearrange("p (c k) -> p c k", k=LEN)
                V.tensor_reduce(rowmax[:], sc, AX, ALU.max).then_inc(soft, 1)
                d.wait_ge(soft, 2 * t + 1)
                V.tensor_tensor(prob[:], sc, spread(rowmax[:], 2, [P, HEADS, LEN]), ALU.subtract) \
                    .then_inc(shifted, 1)
                if sig:
                    weigh(t + 1, 1)
                d.wait_ge(exp_done, t + 1)
                V.reduce_sum(rowsum[:], prob[:], axis=AX).then_inc(soft, 1)
                d.wait_ge(soft, 2 * t + 2)
                V.reciprocal(rinv[:], rowsum[:]).then_inc(sum_inv, 1)
                d.wait_ge(p_psum, t + 1)
                V.tensor_copy(pz[LEN:P, :, 1, :, :],
                              B[5][LEN:P, :].rearrange("k (c h q) -> k c h q", c=PAIRS, h=2)).then_inc(pB_sb, 1)
                if kept:
                    d.wait_ge(x2_kept, t)
                d.wait_ge(att_psum, t + 1)
                V.scalar_tensor_tensor(ht, B[7][:, 0:DIM], fac[:, 6:7], hb[:], ALU.mult, ALU.add) \
                    .then_inc(h2_done, 1)
                d.wait_ge(h2_done, t + 1)
                carry()
                layer_norm(1, ln2, t, ht, x2n[:]).then_inc(x2_ready, 1)
                d.wait_ge(lg_psum, t + 1)
                V.tensor_copy(one(logits[:, bass.ds(t, 1), :]), B[5][:, 0:EXPERTS]).then_inc(lg_sb, 1)

            weigh(0, 0)
            weigh(0, 1)
            iteration(0, True, False)
            with d.Fori(1, TILES - 1) as i:
                iteration(i, True)
            iteration(TILES - 1, False)

            n_route = 0

            def rstep(ins):
                nonlocal n_route
                ins.then_inc(route, 1)
                n_route += 1
                d.wait_ge(route, n_route)

            te = [P, TILES, EXPERTS]
            d.wait_ge(lg_sb, TILES)
            V.memset(zeros[:], 0.0)
            rstep(V.tensor_reduce(best[:, 0, :], logits[:], AX, ALU.max))
            rstep(V.tensor_tensor(pick[:], logits[:], spread(best[:, 0, :], 2, te), ALU.is_equal))
            rstep(V.tensor_tensor(pick[:], pick[:], spread(rev_expert, 1, te), ALU.mult))
            rstep(V.tensor_reduce(best[:, 1, :], pick[:], AX, ALU.max))
            rstep(V.tensor_tensor(oh[:], spread(rev_expert, 1, te), spread(best[:, 1, :], 2, te), ALU.is_equal))
            d.wait_ge(rank_psum, 1)
            te_bank = B[7][:, 0:TILES * EXPERTS].rearrange("p (t e) -> p e t", e=EXPERTS)
            rstep(V.tensor_copy(tot[:], te_bank))
            rstep(V.tensor_tensor_scan(incl[:].rearrange("p e t -> p (e t)"),
                                       tot[:].rearrange("p e t -> p (e t)"), zeros[:], 0.0, ALU.add, ALU.add))
            last = incl[:, :, TILES - 1]
            start, count, ntiles, end_t, base = (rt[:, n, :] for n in range(5))
            V.memset(start[:, 0:1], 0.0)
            rstep(V.tensor_copy(start[:, 1:EXPERTS], last[:, 0:EXPERTS - 1]))
            rstep(V.tensor_tensor(count, last, start, ALU.subtract))
            rstep(V.tensor_tensor(over[:], spread(count, 2, [P, EXPERTS, TILES]),
                                  spread(tile_edges, 1, [P, EXPERTS, TILES]), ALU.is_gt))
            rstep(V.reduce_sum(ntiles, over[:], axis=AX))
            rstep(V.tensor_tensor_scan(end_t, ntiles, zeros[:, 0:EXPERTS], 0.0, ALU.add, ALU.add))
            rstep(V.tensor_tensor(base, end_t, ntiles, ALU.subtract))
            rstep(V.scalar_tensor_tensor(base, base, float(P), start, ALU.mult, ALU.subtract))
            rstep(V.tensor_tensor(off[:], incl[:], tot[:], ALU.subtract))
            rstep(V.tensor_tensor(off[:], off[:], spread(base, 2, [P, EXPERTS, TILES]), ALU.add))
            rstep(V.tensor_tensor(pick[:], off[:].rearrange("p e t -> p t e"),
                                  B[6][:, 0:TILES * EXPERTS].rearrange("p (t e) -> p t e", e=EXPERTS), ALU.add))
            rstep(V.tensor_tensor(pick[:], pick[:], oh[:], ALU.mult))
            rstep(V.reduce_sum(pos_f[:], pick[:], axis=AX))
            V.tensor_copy(pos[:], pos_f[:]).then_inc(pos_ready, 1)
            se = [P, SORTED, EXPERTS]
            rstep(V.tensor_tensor(upt[:], spread(end_t, 1, se), spread(tile_index, 2, se), ALU.is_le))
            rstep(V.reduce_sum(exp_f[:], upt[:], axis=AX))
            V.tensor_scalar(exp_i[:], exp_f[:], float(EXPERTS - 1), None, ALU.min).then_inc(pos_ready, 1)
            assert n_route == ROUTE_STEPS

            with d.Fori(0, GROUPS - 1, 2) as g:
                for k in range(2):
                    d.wait_ge(down_psum, g + (k + 1))
                    hg = h[:, bass.ds((g + k) * GROUP, GROUP), :].rearrange("p t d -> p (t d)")
                    V.tensor_tensor(hg, hg, B[4 + k][:], ALU.add).then_inc(added, 1)

            def keep_ids(j, k):
                d.wait_ge(rows_in[k], (j - k) * 8 + 16)
                V.tensor_copy(ids[:, bass.ds(j, 1)], rows[:, k, DIM:ROW].bitcast(U32)).then_inc(id_kept, 1)

            def gate(j, k):
                d.wait_ge(silu_done, j + 1)
                V.tensor_tensor(hid[:, k, :], act[:, k, :], B[2 + 2 * k][:], ALU.mult).then_inc(hid_done, 1)

            def hidden_transposed(j, k):
                d.wait_ge(hT_psum, j + 1)
                V.tensor_copy(hidT[:, k, :, :].rearrange("p c t -> p (c t)"), B[5][:]).then_inc(hT_sb, 1)

            keep_ids(0, 0)
            keep_ids(1, 1)
            gate(0, 0)
            hidden_transposed(0, 0)
            gate(1, 1)
            keep_ids(2, 0)
            with d.Fori(1, SORTED - 3, 2) as i:
                for k in range(2):
                    hidden_transposed(i + k, 1 - k)
                    gate(i + (k + 1), k)
                    keep_ids(i + (k + 2), 1 - k)
            hidden_transposed(SORTED - 2, 1)
            gate(SORTED - 1, 0)
            hidden_transposed(SORTED - 1, 0)

        @block.tensor
        def _(pe):
            T = nc.tensor

            def mm(out_, lhsT, rhs, start=True, stop=True):
                return T.matmul(out_, lhsT, rhs, start=start, stop=stop)

            def col(c, n=P):
                return slice(c * n, (c + 1) * n)

            pe.wait_ge(ld_c, 64)
            pe.wait_ge(small, 1)
            mm(B[1][:, 0:TILES * CHANNELS], before, v[:].rearrange("p t c -> p (t c)")).then_inc(s1_psum, 1)
            pe.wait_ge(small, 3)
            per = 512 // C2
            for n in range(TILES // per):
                last = mm(B[2 + n][:], before, e2[:, n * per:(n + 1) * per, :].rearrange("p t c -> p (t c)"))
            last.then_inc(s2_psum, 1)

            pe.wait_ge(ld_sn, 80)
            pe.wait_ge(ld_att, 64)
            nq = 3 * INNER // P
            for c in range(nq):
                mm(B[6][:, c:c + 1], wqkvT[:, col(c)], uq[:])
            for c in range(PAIRS):
                last = mm(B[6][:, nq:nq + 1], woutT[:, c, :], uo[:, c:c + 1], c == 0, c == PAIRS - 1)
            last.then_inc(norm_mm, 1)
            pe.wait_ge(norm_step, 1)
            for c in range(nq):
                mm(B[7][:, 0:1], wqkv_sb[:, c, :], wu[:, c:c + 1], c == 0, c == nq - 1)
            for c in range(PAIRS):
                last = mm(B[7][:, 1 + c:2 + c], wout_sb[:, col(c)], wu[:, nq:nq + 1])
            last.then_inc(norm_mm, 1)
            pe.wait_ge(norm_step, 4)
            mm(B[6][:, 32:36], ones, nrm[:]).then_inc(norm_mm, 1)

            def features(s, first=False):
                pe.wait_ge(e3_ready, s + 1)
                for c in range(UC):
                    mm(B[0][:, col(c)], e3[:, col(c)], before, True, False)
                    mm(B[0][:, col(c)], g4[:, col(c)], ident, False, True)
                if not first:
                    pe.wait_ge(h_read, s)
                T.transpose(B[3][0:LOW, 0:P], low_tile[:], ident).then_inc(u4_psum, 1)

            def project(s, half, lo=0, hi=UC + 1):
                if half == 0 and lo == 0:
                    pe.wait_ge(u4_sb, 2 * s + 2)
                bank = B[1 + half][:]
                for c in range(lo, hi):
                    if c < UC:
                        last = mm(bank, ut[:, c, :], whigh[:, c, col(half, 512)], c == 0, False)
                    else:
                        last = mm(bank, lowt[:], wlow[:, col(half, 512)], False, True)
                if hi == UC + 1:
                    last.then_inc(y_psum, 1)

            def accumulate(s, half):
                pe.wait_ge(z_sb, 2 * s + (half + 1))
                for c in range(4 * half, 4 * half + 4):
                    last = mm(B[3][:, P:P + DIM], upto, z[:, c, :], c == 0, c == CHANNELS - 1)
                if half == 1:
                    last.then_inc(h_psum, 1)

            def iteration(t, sig, first=False):
                if sig:
                    features(t + 1)
                pe.wait_ge(xn_ready, t + 1)
                T.transpose(B[4][:, 0:P], xn[:], ident).then_inc(xT_psum, 1)
                if sig:
                    project(t + 1, 0)
                pe.wait_ge(xT_sb, t + 1)
                if not first:
                    pe.wait_ge(lg_sb, t)
                for c in range(PAIRS):
                    last = mm(B[5][:, col(c)], wqkvT[:, col(c)], xT[:])
                last.then_inc(q_psum, 1)
                for c in range(PAIRS):
                    last = mm(B[6][:, col(c)], wqkvT[:, col(PAIRS + c)], xT[:])
                last.then_inc(k_psum, 1)
                mm(B[7][:], xT[:], wqkvT[:, 2 * INNER:]).then_inc(v_psum, 1)
                if sig:
                    project(t + 1, 1, 0, 1)
                pe.wait_ge(q_sb, 2 * t + 2)
                pe.wait_ge(k_sb, t + 1)
                T.matmul(B[4][:], ident_b[:], mask[:], start=True, stop=False)
                for c in range(PAIRS):
                    for s in range(2):
                        last = mm(B[4][:, col(2 * c + s, LEN)], qz[:, c, s, :, :].rearrange("p h q -> p (h q)"),
                                  kT[:, c, col(s, LEN)], False, c == PAIRS - 1 and s == 1)
                last.then_inc(s_psum, 1)
                if sig:
                    project(t + 1, 1, 1, UC + 1)
                pe.wait_ge(pn_ready, t + 1)
                for c in range(PAIRS):
                    last = T.transpose(B[5][:, col(c)], pn[:, 2 * c:2 * c + 2, :].rearrange("p s k -> p (s k)"), ident)
                last.then_inc(p_psum, 1)
                if sig:
                    accumulate(t + 1, 0)
                pe.wait_ge(v_sb, t + 1)
                pe.wait_ge(pA_sb, t + 1)
                pe.wait_ge(pB_sb, t + 1)
                for c in range(PAIRS):
                    for hd in range(2):
                        last = mm(B[6][col(hd, HEAD_DIM), col(c)], vv[:, col(2 * c + hd, HEAD_DIM)],
                                  pz[:, c, :, hd, :])
                last.then_inc(o_psum, 1)
                if sig:
                    accumulate(t + 1, 1)
                pe.wait_ge(o_sb, t + 1)
                for c in range(PAIRS):
                    last = mm(B[7][:, 0:DIM], oT[:, c, :], woutT[:, c, :], c == 0, c == PAIRS - 1)
                last.then_inc(att_psum, 1)
                pe.wait_ge(x2_ready, t + 1)
                T.transpose(B[4][:, 0:P], x2n[:], ident).then_inc(x2T_psum, 1)
                pe.wait_ge(x2T_sb, 2 * t + 1)
                mm(B[5][:, 0:EXPERTS], x2t[:], gateT[:]).then_inc(lg_psum, 1)

            pe.wait_ge(small, SMALL_STEPS)
            pe.wait_ge(ld_sig, 32)
            pe.wait_ge(norm_mm, 3)
            pe.wait_ge(norm_step, NORM_STEPS)
            pe.wait_ge(consts_cast, 2)
            features(0, True)
            project(0, 0)
            project(0, 1)
            accumulate(0, 0)
            accumulate(0, 1)
            iteration(0, True, True)
            with pe.Fori(1, TILES - 1) as i:
                iteration(i, True)
            iteration(TILES - 1, False)

            pe.wait_ge(ld_ffn, 64)
            pe.wait_ge(x2T_sb, 2 * TILES)

            def up(g, first=False):
                for c in range(HC):
                    if not first:
                        pe.wait_ge(gelu_done, g * HC + (c + 1 - HC))
                    mm(B[c][:], sw1[:, col(c)], x2T[:, bass.ds(g * GROUP * P, GROUP * P)]).then_inc(up_psum, 1)

            def down(g, k, first=False):
                pe.wait_ge(gelu_done, (g + 1) * HC)
                if not first:
                    pe.wait_ge(added, g - 1)
                for t in range(GROUP):
                    for c in range(HC):
                        last = mm(B[4 + k][:, col(t)], gh[:, k, c, col(t)], sw2[:, c, :], c == 0, c == HC - 1)
                last.then_inc(down_psum, 1)

            up(0, True)
            pe.wait_ge(route, 5)
            mm(B[6][:, 0:TILES * EXPERTS], below, oh[:].rearrange("p t e -> p (t e)"))
            mm(B[7][:, 0:TILES * EXPERTS], ones, oh[:].rearrange("p t e -> p (t e)")).then_inc(rank_psum, 1)
            up(1)
            down(0, 0, True)
            up(2)
            down(1, 1, True)
            with pe.Fori(2, GROUPS - 3, 2) as g:
                up(g + 1)
                down(g, 0)
                up(g + 2)
                down(g + 1, 1)
            up(GROUPS - 1)
            down(GROUPS - 2, 0)
            down(GROUPS - 1, 1)

            def expert(j):
                return pe.value_load(exp_i[0:1, bass.ds(j, 1)], min_val=0, max_val=EXPERTS - 1)

            def rows_in_columns(j, k, first=False):
                pe.wait_ge(rows_in[k], (j - k) * 8 + 16)
                if not first:
                    pe.wait_ge(rT_sb, j)
                T.transpose(B[0][:, 0:P], rows[:, k, 0:DIM], ident).then_inc(rT_psum, 1)

            def expert_up(j, k, first=False):
                e = expert(j)
                pe.wait_ge(rT_sb, j + 1)
                if not first:
                    pe.wait_ge(hid_done, j - 1)
                mm(B[1 + 2 * k][:], rowsT[:, k, :], w13[:, bass.ds(e, 1), 0:HIDDEN].rearrange("p o i -> p (o i)"))
                mm(B[2 + 2 * k][:], rowsT[:, k, :], w13[:, bass.ds(e, 1), HIDDEN:].rearrange("p o i -> p (o i)")) \
                    .then_inc(eu_psum, 1)

            def hidden_in_columns(j, k, first=False):
                pe.wait_ge(hid_done, j + 1)
                if not first:
                    pe.wait_ge(hT_sb, j)
                for c in range(HC):
                    last = T.transpose(B[5][:, col(c)], hid[:, k, col(c)], ident)
                last.then_inc(hT_psum, 1)

            def expert_down(j, k, first=False):
                e = expert(j)
                pe.wait_ge(hT_sb, j + 1)
                if not first:
                    pe.wait_ge(y_done, j)
                for c in range(HC):
                    last = mm(B[6][:, 0:DIM], hidT[:, k, c, :],
                              w2[:, bass.ds(e, 1), c, :].rearrange("p o d -> p (o d)"), c == 0, c == HC - 1)
                last.then_inc(ed_psum, 1)

            pe.wait_ge(pos_ready, 2)
            pe.wait_ge(added, GROUPS)
            rows_in_columns(0, 0, True)
            rows_in_columns(1, 1)
            expert_up(0, 0, True)
            expert_up(1, 1, True)
            hidden_in_columns(0, 0, True)
            rows_in_columns(2, 0)
            expert_up(2, 0)
            hidden_in_columns(1, 1)
            rows_in_columns(3, 1)
            expert_down(0, 0, True)
            with pe.Fori(2, SORTED - 4, 2) as j:
                for k in range(2):
                    expert_up(j + (k + 1), 1 - k)
                    hidden_in_columns(j + k, k)
                    rows_in_columns(j + (k + 2), k)
                    expert_down(j + (k - 1), 1 - k)
            for j in range(SORTED - 3, SORTED + 1):
                if j + 1 < SORTED:
                    expert_up(j + 1, (j + 1) % 2)
                if j < SORTED:
                    hidden_in_columns(j, j % 2)
                if j + 2 < SORTED:
                    rows_in_columns(j + 2, j % 2)
                expert_down(j - 1, (j - 1) % 2)


_IN = ["x_next", "x_prev", "w_low", "w_high", "tok_b", "wqkv_t", "wqkv", "u_qkv", "wout_t", "wout", "u_out",
       "b_out", "scalars", "gate_t", "w13_t", "w2_t", "sw1_t", "sw2_t", "square", "mask_c", "steps"]


def kernel(x, L0_tok_W, L0_tok_b, L0_attn_w_qkv, L0_attn_u_qkv, L0_attn_sigma_qkv, L0_attn_w_out,
           L0_attn_b_out, L0_attn_u_out, L0_attn_sigma_out, L0_attn_temperature, L0_ffn_gate_w,
           L0_ffn_w1, L0_ffn_w2, L0_ffn_w3, L0_ffn_sw1, L0_ffn_sw2):
    import numpy as np
    import concourse.bacc as bacc
    from concourse.bass_utils import run_bass_kernel_spmd

    time = np.arange(LEN, dtype=np.float32) * (np.float32(1) / np.float32(LEN - 1))
    path = np.concatenate([np.broadcast_to(time[None, :, None], (SEQS, LEN, 1)), np.asarray(x)], axis=-1)

    def tokens(a):
        padded = np.zeros((SEQS, LEN, CHANNELS), np.float32)
        padded[:, :LEN - 1] = a
        return padded.reshape(TILES, P, CHANNELS).transpose(1, 0, 2)

    def on_all(a):
        a = np.asarray(a)
        return np.broadcast_to(a.reshape(1, -1), (P, a.size))

    w = np.asarray(L0_tok_W).reshape(DIM, LOW + C3, CHANNELS).transpose(1, 2, 0).reshape(LOW + C3, -1)
    w1, w2, w3 = np.asarray(L0_ffn_w1), np.asarray(L0_ffn_w2), np.asarray(L0_ffn_w3)
    wqkv, wout = np.asarray(L0_attn_w_qkv), np.asarray(L0_attn_w_out)
    n = np.arange(P)
    same = n[:, None] // LEN == n[None, :] // LEN
    key = np.arange(C3) % LEN
    masked = (key[None, :] == n[:, None] % LEN) | (key[None, :] == LEN - 1)
    arrays = {
        "x_next": tokens(path[:, 1:]),
        "x_prev": tokens(path[:, :-1]),
        "w_low": w[:LOW],
        "w_high": w[LOW:].reshape(UC, P, -1).transpose(1, 0, 2),
        "tok_b": on_all(L0_tok_b),
        "wqkv_t": wqkv.T,
        "wqkv": wqkv.reshape(-1, P, DIM).transpose(1, 0, 2),
        "u_qkv": np.asarray(L0_attn_u_qkv).reshape(P, 1),
        "wout_t": wout.T.reshape(PAIRS, P, DIM).transpose(1, 0, 2),
        "wout": wout,
        "u_out": np.asarray(L0_attn_u_out).reshape(PAIRS, P).T,
        "b_out": on_all(L0_attn_b_out),
        "scalars": np.stack([np.broadcast_to(np.asarray(s), (P,)) for s in
                             (L0_attn_sigma_qkv, L0_attn_sigma_out, L0_attn_temperature)], axis=1),
        "gate_t": np.asarray(L0_ffn_gate_w).T,
        "w13_t": np.concatenate([w1, w3], axis=1).transpose(2, 0, 1),
        "w2_t": w2.reshape(EXPERTS, DIM, HC, P).transpose(3, 0, 2, 1),
        "sw1_t": np.asarray(L0_ffn_sw1).T,
        "sw2_t": np.asarray(L0_ffn_sw2).T.reshape(HC, P, DIM).transpose(1, 0, 2),
        "square": np.stack([n[:, None] == n[None, :], same & (n[:, None] < n[None, :]),
                            same & (n[:, None] <= n[None, :]), n[:, None] < n[None, :],
                            np.ones((P, P), bool)], axis=1).astype(np.float32),
        "mask_c": np.where(masked, np.float32(-3e38), np.float32(0)),
        "steps": on_all(np.concatenate([EXPERTS - np.arange(EXPERTS), P * np.arange(TILES),
                                        np.arange(SORTED)]).astype(np.float32)),
    }
    arrays = {k: np.ascontiguousarray(a) for k, a in arrays.items()}
    nc = bacc.Bacc("TRN2", target_bir_lowering=False, num_devices=1)
    args = [nc.dram_tensor(k, arrays[k].shape, F32, kind="ExternalInput").ap() for k in _IN]
    out = nc.dram_tensor("out", (TILES * P, DIM), F32, kind="ExternalOutput").ap()
    build(nc, *args, out)
    r = run_bass_kernel_spmd(nc, [arrays], core_ids=[0])
    return r.results[0]["out"].reshape(SEQS, LEN, DIM)[:, :LEN - 1]
```

```python
from contextlib import ExitStack

import concourse.bass as bass
from concourse import mybir

F32 = mybir.dt.float32
F32R = mybir.dt.float32r
BF16 = mybir.dt.bfloat16
I32 = mybir.dt.int32
U32 = mybir.dt.uint32
ALU = mybir.AluOpType
ACT = mybir.ActivationFunctionType
AX = mybir.AxisListType.X

P = 128
SEQS, LEN, CHANNELS = 64, 64, 8
TILES = SEQS * LEN // P
DIM = 128
HEADS, HEAD_DIM = 8, 64
PAIRS = HEADS // 2
INNER = HEADS * HEAD_DIM
EXPERTS, HIDDEN = 8, 512
HC = HIDDEN // P
SORTED = TILES + EXPERTS - 1
ROW = DIM + 1
C2 = CHANNELS * CHANNELS
C3 = C2 * CHANNELS
LOW = 1 + CHANNELS + C2
UC = C3 // P
EPS = 1e-5
NO_TOKEN = 1 << 20

GROUP = 4
GROUPS = TILES // GROUP
FILL = SORTED // 3
SMALL_STEPS, NORM_STEPS, ROUTE_STEPS = 15, 11, 21
SQUARED_STEP = 7


def spread(ap, axis, shape):
    return ap.unsqueeze(axis).to_broadcast(shape)


def build(nc, x_next, x_prev, w_low, w_high, tok_b, wqkv_t, wqkv, u_qkv, wout_t, wout, u_out, b_out,
          scalars, gate_t, w13_t, w2_t, sw1_t, sw2_t, square, mask_c, steps, out):
    with ExitStack() as ctx:
        def sb(name, shape, dt=F32):
            return ctx.enter_context(nc.sbuf_tensor(name, shape, dt))

        def sem(name):
            return ctx.enter_context(nc.semaphore(name))

        x2T_dram = nc.dram_tensor("x2_columns", [P, TILES * P], F32, kind="Internal").ap()
        sorted_rows = nc.dram_tensor("sorted_rows", [SORTED * P, ROW], F32, kind="Internal").ap()

        x2 = sb("x2", [P, TILES, ROW])
        h = sb("h", [P, TILES, DIM])
        w13 = sb("w13", [P, EXPERTS, 2 * HIDDEN])
        whigh = sb("whigh", [P, 2, UC, CHANNELS * DIM], F32R)
        wlow = sb("wlow", [LOW, 2, CHANNELS * DIM], F32R)
        tokb = sb("tokb", [P, DIM])
        wqkvT = sb("wqkvT", [P, 2, 3 * INNER], F32R)
        def parts(flat, *sizes):
            at = 0
            for size in sizes:
                yield flat[:, at:at + size]
                at += size

        in_c = TILES * CHANNELS
        whigh_in, wqkvT_in, wqkv_sb, wlow_in = parts(
            w13[:].rearrange("p e n -> p (e n)"), UC * CHANNELS * DIM, 3 * INNER, 3 * INNER, CHANNELS * DIM)
        whigh_in = whigh_in.rearrange("p (c n) -> p c n", c=UC)
        wqkv_sb = wqkv_sb.rearrange("p (c d) -> p c d", d=DIM)
        wlow_in = wlow_in[0:LOW, :]
        e2, xn_in, xp_in, wout_sb, sw1_in, sw2_in = parts(
            h[:].rearrange("p t d -> p (t d)"), TILES * C2, in_c, in_c, INNER, HIDDEN, HIDDEN)
        e2 = e2.rearrange("p (t a) -> p t a", a=C2)
        xn_in, xp_in = (t.rearrange("p (t c) -> p t c", c=CHANNELS) for t in (xn_in, xp_in))
        fill, t3, t4 = parts(x2[:].rearrange("p t r -> p (t r)"), FILL * ROW, in_c, in_c)
        fill = fill.rearrange("p (t r) -> p t r", r=ROW)
        t3, t4 = (t.rearrange("p (t c) -> p t c", c=CHANNELS) for t in (t3, t4))
        uq = sb("uq", [P, 1])
        woutT = sb("woutT", [P, PAIRS, DIM])
        uo = sb("uo", [P, PAIRS])
        bout = sb("bout", [P, DIM])
        scal = sb("scal", [P, 3])
        gateT = sb("gateT", [P, EXPERTS])
        sw1 = sb("sw1", [P, 2, HIDDEN], F32R)
        sw2 = sb("sw2", [P, 2, HC, DIM], F32R)
        sq = sb("sq", [P, 5, P])
        ident, before, upto, below, ones = (sq[:, n, :] for n in range(5))
        before_r = sb("before_r", [P, P], F32R)
        upto_r = sb("upto_r", [P, P], F32R)
        ident_b = sb("ident_b", [P, P], BF16)
        mask = sb("mask", [P, C3], BF16)
        stepc = sb("stepc", [P, EXPERTS + TILES + SORTED])
        rev_expert = stepc[:, 0:EXPERTS]
        tile_edges = stepc[:, EXPERTS:EXPERTS + TILES]
        tile_index = stepc[:, EXPERTS + TILES:]

        v = sb("v", [P, TILES, CHANNELS])
        vh = sb("vh", [P, TILES, CHANNELS])
        levels = sb("levels", [P, TILES * (LOW + C2)])
        low = levels[:, 0:TILES * LOW].rearrange("p (t a) -> p t a", a=LOW)
        g3 = levels[:, TILES * LOW:].rearrange("p (t a) -> p t a", a=C2)

        e3 = sb("e3", [P, C3])
        e3h = sb("e3h", [P, C3], F32R)
        e3l = sb("e3l", [P, C3], F32R)
        g4 = sb("g4", [P, C3])
        low_tile = sb("low_tile", [P, LOW])
        uth = sb("uth", [P, UC, P], F32R)
        utl = sb("utl", [P, UC, P], F32R)
        lowth = sb("lowth", [LOW, P], F32R)
        lowtl = sb("lowtl", [LOW, P], F32R)
        z = sb("z", [P, CHANNELS, DIM])
        maskf = z[:].rearrange("p c d -> p (c d)")[:, 0:C3]
        z4 = sb("z4", [P, 4, DIM])
        z1 = sb("z1", [P, DIM])
        z1h = sb("z1h", [P, DIM], F32R)
        z1l = sb("z1l", [P, DIM], F32R)

        xn = sb("xn", [P, DIM])
        xTh = sb("xTh", [P, P], F32R)
        xTl = sb("xTl", [P, P], F32R)
        qz = sb("qz", [P, PAIRS, 2, 2, LEN])
        kT = sb("kT", [P, PAIRS, P])
        vv = sb("vv", [P, HEADS, HEAD_DIM + 1])
        rowmax = sb("rowmax", [P, HEADS])
        prob = sb("prob", [P, HEADS, LEN])
        rinv = sb("rinv", [P, HEADS])
        pz = sb("pz", [P, PAIRS, 2, 2, LEN])
        on = sb("on", [P, HEADS, HEAD_DIM])
        oT = sb("oT", [P, PAIRS, P])
        stats = sb("stats", [P, 2, 6])
        meanvar = sb("meanvar", [P, 2, 2])
        rstd = sb("rstd", [P, 2, 2])
        powers = sb("powers", [P, 2])
        scrap = sb("scrap", [P, 1])
        x2t = sb("x2t", [P, P])
        x2n = sb("x2n", [P, DIM])
        logits = sb("logits", [P, TILES, EXPERTS])

        wu = sb("wu", [P, 3 * INNER // P + 1])
        wtwu = sb("wtwu", [P, 1 + PAIRS])
        sqs = sb("sqs", [P, 32])
        nrm = sb("nrm", [P, 4])
        fac = sb("fac", [P, 8])

        def taker(*hosts):
            parts = [[t, 0] for t in hosts]

            def take(*shape):
                size = 1
                for n in shape:
                    size *= n
                for part in parts:
                    flat, at = part
                    if at + size <= flat.shape[1]:
                        part[1] = at + size
                        ap = flat[:, at:at + size]
                        names = "abcd"[:len(shape)]
                        if len(shape) == 1:
                            return ap
                        return ap.rearrange(f"p ({' '.join(names)}) -> p {' '.join(names)}",
                                            **dict(zip(names, shape)))
                raise AssertionError("no room")
            return take

        def flat4(t):
            return t[:].rearrange("p a b c d -> p (a b c d)")

        tail = sb("tail", [P, 2 * HIDDEN])[:]
        late = taker(levels[:, EXPERTS * HC * DIM:], e3[:], g4[:], vv[:].rearrange("p a b -> p (a b)"),
                     on[:].rearrange("p a b -> p (a b)"), oT[:].rearrange("p a b -> p (a b)"),
                     kT[:].rearrange("p a b -> p (a b)"), prob[:].rearrange("p a b -> p (a b)"),
                     z4[:].rearrange("p a b -> p (a b)"))
        late_wide = taker(z[:].rearrange("p c d -> p (c d)"), flat4(qz), flat4(pz), tail)
        w2 = levels[:, 0:EXPERTS * HC * DIM].rearrange("p (e c d) -> p e c d", e=EXPERTS, c=HC)

        oh = late(TILES, EXPERTS)
        pick = late(TILES, EXPERTS)
        best = sb("best", [P, 2, TILES])
        tot = late(EXPERTS, TILES)
        incl = late(EXPERTS, TILES)
        zeros = late(EXPERTS * TILES)
        rt = sb("rt", [P, 8, EXPERTS])
        off = late(EXPERTS, TILES)
        over = late(EXPERTS, TILES)
        pos_f = late(TILES)
        pos = sb("pos", [P, TILES], U32)
        upt = late(SORTED, EXPERTS)
        exp_f = late(SORTED)
        exp_i = sb("exp_i", [P, SORTED], I32)

        wh = whigh[:].rearrange("p s c n -> p (s c n)")
        half = HC * GROUP * P
        ghh = [wh[:, (2 * k) * half:(2 * k + 1) * half].rearrange("p (c t) -> p c t", c=HC) for k in range(2)]
        ghl = [wh[:, (2 * k + 1) * half:(2 * k + 2) * half].rearrange("p (c t) -> p c t", c=HC) for k in range(2)]
        gelu = late_wide(2, GROUP * P)
        xg_in = sb("xg_in", [P, 2, GROUP * P])
        late_r = taker(wqkvT[:].rearrange("p s n -> p (s n)"))
        xgh = late_r(2, GROUP * P)
        xgl = [late_r(GROUP * P), uth[:].rearrange("p c t -> p (c t)")]
        rows = late(2, ROW)
        ids = sb("ids", [P, SORTED], U32)
        rowsT = late(2, P)
        act = late_wide(2, HIDDEN)
        hid = late_wide(2, HIDDEN)
        hidT = late_wide(2, HC, P)
        y = late(2, DIM)

        b56 = ctx.enter_context(nc.psum_tensor("bank56", [P, 2, 512], F32))
        B = {n: ctx.enter_context(nc.psum_tensor(f"bank{n}", [P, 512], F32)) for n in (0, 1, 2, 3, 4, 7)}
        B[5], B[6] = b56[:, 0, :], b56[:, 1, :]
        heads_out = b56[:, :, 0:4 * (HEAD_DIM + 1)].rearrange("p b (h e) -> p b h e", h=4)

        ld_x, ld_c, ld_sn, ld_att, ld_ffn, ld_sw = (
            sem(f"loaded_{n}") for n in ("x", "const", "norms", "attention", "experts", "shared"))
        ld_sig = [sem(f"loaded_signature{c}") for c in range(UC + 1)]
        filled, fill_sent = sem("fill_written"), sem("fill_sent")
        consts_cast = sem("consts_cast")
        pads_zeroed = sem("pads_zeroed")
        ids_written = sem("ids_written")
        w_hi, w_lo = sem("signature_weights_hi"), sem("signature_weights_lo")
        q_hi, q_lo = sem("qkv_weights_hi"), sem("qkv_weights_lo")
        sw_hi, sw_lo = sem("shared_weights_hi"), sem("shared_weights_lo")
        small, s1_psum, s2_psum = sem("small_levels"), sem("s1_psum"), sem("s2_psum")
        norm_root, norm_mm, norm_step, exp_temp = (sem("norm_root"), sem("norm_matmul"), sem("norm_step"),
                                                   sem("exp_temperature"))
        e3_ready, e3_hi, e3_lo, low_ready = sem("e3_ready"), sem("e3_hi"), sem("e3_lo"), sem("low_ready")
        u4_psum, u4_hi, u4_lo = sem("u4_psum"), sem("u4_hi"), sem("u4_lo")
        y_psum, z_sb, tree, h_psum, h_read = sem("y_psum"), sem("z_sb"), sem("tree"), sem("h_psum"), sem("h_read")
        ln1, ln2, xn_ready, xT_psum = sem("ln1"), sem("ln2"), sem("xn_ready"), sem("xT_psum")
        xT_hi, xT_lo = sem("xT_hi"), sem("xT_lo")
        q_psum, k_psum, v_psum = sem("q_psum"), sem("k_psum"), sem("v_psum")
        q_sb, k_sb, v_sb = sem("q_sb"), sem("k_sb"), sem("v_sb")
        s_psum, soft, shifted, exp_done = sem("scores_psum"), sem("row_max"), sem("shifted"), sem("exp_done")
        p_psum, pA_sb, pB_sb = sem("probT_psum"), sem("probT_first_seq"), sem("probT_second_seq")
        o_psum, o_inv, on_ready, oT_psum, o_sb = (sem("o_psum"), sem("o_inverse"), sem("o_normalised"),
                                                  sem("oT_psum"), sem("o_sb"))
        h_biased, att_psum, h2_done = sem("h_biased"), sem("attention_psum"), sem("h2_done")
        x2_ready, x2T_psum, x2T_sb, x2_kept = sem("x2_ready"), sem("x2T_psum"), sem("x2T_sb"), sem("x2_kept")
        lg_psum, lg_sb = sem("logits_psum"), sem("logits_sb")
        rooted = [sem("ln1_rooted"), sem("ln2_rooted")]
        powers_set = sem("powers_set")
        route, rank_psum, pos_ready, scattered = (sem("route_step"), sem("rank_psum"), sem("pos_ready"),
                                                  sem("scattered"))
        xg_hi, xg_lo, gelu_done = sem("x_group_hi"), sem("x_group_lo"), sem("gelu_done")
        gh_hi, gh_lo = sem("gelu_hi"), sem("gelu_lo")
        up_psum, down_psum, added = sem("up_psum"), sem("down_psum"), sem("added")
        x2T_sent = sem("x2T_sent")
        xg_loaded = [sem(f"x_group_loaded{n}") for n in range(2)]
        out_sent = [sem(f"out_sent{n}") for n in range(GROUPS)]
        rows_in = [sem(f"rows_in{n}") for n in range(2)]
        id_kept = sem("id_kept")
        rT_psum, rT_sb = sem("rowsT_psum"), sem("rowsT_sb")
        eu_psum, silu_done, hid_done = sem("expert_up_psum"), sem("silu_done"), sem("hid_done")
        hT_psum, hT_sb, ed_psum, y_done = (sem("hidT_psum"), sem("hidT_sb"), sem("expert_down_psum"),
                                           sem("y_done"))
        y_sent = [sem(f"y_sent{n}") for n in range(2)]

        block = ctx.enter_context(nc.Block())

        @block.sync
        def _(sp):
            sp.dma_start(xn_in, x_next).then_inc(ld_x, 16)
            sp.dma_start(xp_in, x_prev).then_inc(ld_x, 16)
            sp.dma_start(sq[:], square).then_inc(ld_c, 16)
            sp.dma_start(maskf[:], mask_c).then_inc(ld_c, 16)
            sp.dma_start(stepc[:], steps).then_inc(ld_c, 16)
            sp.dma_start(tokb[:], tok_b).then_inc(ld_c, 16)
            for c in range(UC):
                sp.dma_start(whigh_in[:, c, :], w_high[:, c, :]).then_inc(ld_sig[c], 16)
            sp.dma_start(wlow_in, w_low).then_inc(ld_sig[UC], 16)
            sp.dma_start(wqkvT_in, wqkv_t).then_inc(ld_att, 16)
            sp.dma_start(woutT[:], wout_t).then_inc(ld_att, 16)
            sp.dma_start(bout[:], b_out).then_inc(ld_att, 16)
            sp.dma_start(gateT[:], gate_t).then_inc(ld_att, 16)
            sp.dma_start(wqkv_sb, wqkv).then_inc(ld_sn, 16)
            sp.dma_start(wout_sb, wout).then_inc(ld_sn, 16)
            sp.dma_start(uq[:], u_qkv).then_inc(ld_sn, 16)
            sp.dma_start(uo[:], u_out).then_inc(ld_sn, 16)
            sp.dma_start(scal[:], scalars).then_inc(ld_sn, 16)
            sp.dma_start(sw1_in, sw1_t).then_inc(ld_sw, 16)
            sp.dma_start(sw2_in.rearrange("p (c d) -> p c d", c=HC), sw2_t).then_inc(ld_sw, 16)
            sp.wait_ge(filled, 1)
            for n in range(SORTED // FILL):
                sp.dma_start(sorted_rows[n * FILL * P:(n + 1) * FILL * P, :].rearrange("(t p) r -> p t r", p=P),
                             fill).then_inc(fill_sent, 16)
            sp.wait_ge(w_lo, UC + 1)
            sp.wait_ge(q_lo, 1)
            sp.wait_ge(norm_mm, 2)
            sp.dma_start(w13[:], w13_t).then_inc(ld_ffn, 16)

            def spill(t):
                sp.wait_ge(x2T_sb, t + 1)
                sp.dma_start(x2T_dram[:, bass.ds(t * P, P)], x2t[:]).then_inc(x2T_sent, 16)

            def load_group(g):
                sp.dma_start(xg_in[:, g % 2, :], x2T_dram[:, g * GROUP * P:(g + 1) * GROUP * P]) \
                    .then_inc(xg_loaded[g % 2], 16)

            with sp.Fori(0, 2 * GROUP) as t:
                spill(t)
            sp.wait_ge(x2T_sent, 16 * 2 * GROUP)
            load_group(0)
            load_group(1)
            with sp.Fori(2 * GROUP, TILES) as t:
                spill(t)
            sp.wait_ge(lg_psum, TILES)
            sp.dma_start(w2, w2_t).then_inc(ld_ffn, 16)
            sp.wait_ge(x2T_sent, 16 * TILES)
            for g in range(GROUPS):
                if g + 2 < GROUPS:
                    sp.wait_ge(xg_lo, g + 1)
                    load_group(g + 2)
                sp.wait_ge(added, g + 1)
                sp.dma_start(out[g * GROUP * P:(g + 1) * GROUP * P, :].rearrange("(t p) d -> p t d", p=P),
                             h[:, g * GROUP:(g + 1) * GROUP, :]).then_inc(out_sent[g], 16)
                if g == GROUPS - 3:
                    sp.wait_ge(scattered, 16 * TILES)
                    for j in range(2):
                        sp.dma_start(rows[:, j, :], sorted_rows[j * P:(j + 1) * P, :]).then_inc(rows_in[j], 16)
            with sp.Fori(2, SORTED - 2, 2) as j:
                for k in range(2):
                    sp.wait_ge(rT_psum, j + (k - 1))
                    sp.wait_ge(id_kept, j + (k - 1))
                    sp.dma_start(rows[:, k, :], sorted_rows[bass.ds((j + k) * P, P), :]).then_inc(rows_in[k], 16)
            sp.wait_ge(rT_psum, SORTED - 2)
            sp.wait_ge(id_kept, SORTED - 2)
            sp.dma_start(rows[:, 0, :], sorted_rows[(SORTED - 1) * P:SORTED * P, :]).then_inc(rows_in[0], 16)

        @block.gpsimd
        def _(pool):
            nc.gpsimd.memset(powers[:, 0:1], -0.5).then_inc(powers_set, 1)
            nc.gpsimd.memset(powers[:, 1:2], 0.5).then_inc(powers_set, 1)
            pool.wait_ge(powers_set, 2)
            nc.gpsimd.memset(qz[:], 0.0).then_inc(pads_zeroed, 1)
            nc.gpsimd.memset(pz[:], 0.0).then_inc(pads_zeroed, 1)
            nc.gpsimd.memset(vv[:, :, HEAD_DIM:], 1.0).then_inc(pads_zeroed, 1)
            nc.gpsimd.memset(fill[:, :, 0:DIM], 0.0)
            nc.gpsimd.memset(fill[:, :, DIM:ROW].bitcast(I32), NO_TOKEN).then_inc(filled, 1)
            G = nc.gpsimd

            def level3(s, first=False):
                if not first:
                    pool.wait_ge(u4_psum, s)
                shape = [P, 1, C2, CHANNELS]

                def by3(t):
                    return t[:].rearrange("p (o a c) -> p o a c", o=1, c=CHANNELS)
                G.tensor_tensor(by3(e3), spread(low[:, bass.ds(s, 1), 1 + CHANNELS:LOW], 3, shape),
                                spread(v[:, bass.ds(s, 1), :], 2, shape), ALU.mult).then_inc(e3_ready, 1)
                G.tensor_tensor(by3(g4), spread(g3[:, bass.ds(s, 1), :], 3, shape),
                                spread(vh[:, bass.ds(s, 1), :], 2, shape), ALU.mult)

            def level3_rest(s):
                pool.wait_ge(e3_hi, s + 1)
                G.tensor_tensor(e3l[:], e3[:], e3h[:].bitcast(F32), ALU.subtract).then_inc(e3_lo, 1)

            def add_channels(s):
                pool.wait_ge(z_sb, 2 * s + 2)
                G.tensor_tensor(z4[:], z[:, 0:4, :], z[:, 4:8, :], ALU.add).then_inc(tree, 1)
                pool.wait_ge(tree, 5 * s + 1)
                G.tensor_tensor(z4[:, 0:2, :], z4[:, 0:2, :], z4[:, 2:4, :], ALU.add).then_inc(tree, 1)
                pool.wait_ge(tree, 5 * s + 2)
                G.tensor_tensor(z1[:], z4[:, 0, :], z4[:, 1, :], ALU.add).then_inc(tree, 1)
                G.tensor_tensor(z1h[:], z4[:, 0, :], z4[:, 1, :], ALU.add).then_inc(tree, 1)
                pool.wait_ge(tree, 5 * s + 4)
                G.tensor_tensor(z1l[:], z1[:], z1h[:].bitcast(F32), ALU.subtract).then_inc(tree, 1)

            def root(n, done, t):
                pool.wait_ge(done, 3 * t + 3)
                G.tensor_tensor(rstd[:, n, 1:2], rstd[:, n, 0:1], powers[:, 0:1], ALU.pow) \
                    .then_inc(rooted[n], 1)

            def iteration(i, f, acc, prev=True):
                if f:
                    level3(i + 3)
                if prev:
                    root(1, ln2, i - 1)
                if acc:
                    add_channels(i + 1)
                if f:
                    level3_rest(i + 3)
                if acc:
                    root(0, ln1, i + 1)

            pool.wait_ge(small, SMALL_STEPS)
            level3(0, True)
            pool.wait_ge(norm_step, SQUARED_STEP)
            G.tensor_tensor(fac[:, 2:4], fac[:, 2:4], powers[:, 1:2].to_broadcast([P, 2]), ALU.pow) \
                .then_inc(norm_root, 1)
            level3_rest(0)
            level3(1)
            level3_rest(1)
            add_channels(0)
            root(0, ln1, 0)
            level3(2)
            level3_rest(2)
            iteration(0, True, True, False)
            with pool.Fori(1, TILES - 3) as i:
                iteration(i, True, True)
            iteration(TILES - 3, False, True)
            iteration(TILES - 2, False, True)
            iteration(TILES - 1, False, False)
            root(1, ln2, TILES - 1)

            nc.gpsimd.iota(x2[:, :, DIM:ROW].bitcast(I32), pattern=[[P, TILES], [1, 1]], base=0,
                           channel_multiplier=1).then_inc(ids_written, 1)
            pool.wait_ge(pos_ready, 1)
            pool.wait_ge(x2_kept, TILES)
            pool.wait_ge(ids_written, 1)
            for t in range(TILES):
                nc.gpsimd.indirect_dma_start(
                    out=sorted_rows[:, :], out_offset=bass.IndirectOffsetOnAxis(ap=pos[:, t:t + 1], axis=0),
                    in_=x2[:, t, :], in_offset=None).then_inc(scattered, 16)
            for g in range(GROUPS):
                pool.wait_ge(out_sent[g], 16)
            for j in range(SORTED):
                pool.wait_ge(y_done, j + 1)
                nc.gpsimd.indirect_dma_start(
                    out=out[:, :], out_offset=bass.IndirectOffsetOnAxis(ap=ids[:, j:j + 1], axis=0),
                    in_=y[:, j % 2, :], in_offset=None, bounds_check=TILES * P - 1, oob_is_err=False,
                    compute_op=ALU.add).then_inc(y_sent[j % 2], 16)
            pool.wait_ge(y_sent[0], 16 * ((SORTED + 1) // 2))
            pool.wait_ge(y_sent[1], 16 * (SORTED // 2))

        @block.scalar
        def _(a):
            A = nc.scalar
            for c in range(UC):
                a.wait_ge(ld_sig[c], 16)
                A.copy(whigh[:, 0, c, :], whigh_in[:, c, :]).then_inc(w_hi, 1)
            a.wait_ge(ld_sig[UC], 16)
            A.copy(wlow[:, 0, :], wlow_in).then_inc(w_hi, 1)
            a.wait_ge(ld_att, 64)
            A.copy(wqkvT[:, 0, :], wqkvT_in).then_inc(q_hi, 1)

            a.wait_ge(ld_sn, 80)
            A.activation(fac[:, 0:1], scal[:, 2:3], ACT.Exp).then_inc(exp_temp, 1)

            def level3_hi(s):
                a.wait_ge(e3_ready, s + 1)
                A.copy(e3h[:], e3[:]).then_inc(e3_hi, 1)

            def low_features(s, first=False):
                if not first:
                    a.wait_ge(u4_psum, s)
                A.copy(low_tile[:], low[:, bass.ds(s, 1), :].rearrange("p o a -> p (o a)")).then_inc(low_ready, 1)

            def features_hi(s):
                a.wait_ge(u4_psum, s + 1)
                A.copy(uth[:].rearrange("p c t -> p (c t)"), B[0][:]).then_inc(u4_hi, 1)
                A.copy(lowth[:], B[3][0:LOW, 0:P]).then_inc(u4_hi, 1)

            def x_hi(t):
                a.wait_ge(xT_psum, t + 1)
                A.copy(xTh[:], B[4][:, 0:P]).then_inc(xT_hi, 1)

            def x2_transposed(t, first=False):
                a.wait_ge(x2T_psum, t + 1)
                if not first:
                    a.wait_ge(x2T_sent, 16 * t)
                A.copy(x2t[:], B[4][:, 0:P]).then_inc(x2T_sb, 1)

            def keep_x2(t):
                a.wait_ge(x2_ready, t + 1)
                A.copy(x2[:, bass.ds(t, 1), 0:DIM].rearrange("p o d -> p (o d)"), x2n[:]).then_inc(x2_kept, 1)

            def iteration(i, f, acc, prev=True, second=False):
                a.wait_ge(q_psum, i + 1)
                for half_ in range(2):
                    part = slice(half_ * HEAD_DIM, (half_ + 1) * HEAD_DIM)
                    A.activation(qz[part, :, :, half_, :],
                                 B[5][part, :].rearrange("p (c s q) -> p c s q", c=PAIRS, s=2),
                                 ACT.Copy, scale=fac[part, 1:2]).then_inc(q_sb, 1)
                a.wait_ge(v_psum, i + 1)
                A.copy(vv[:, :, 0:HEAD_DIM], B[7][:].rearrange("p (h e) -> p h e", h=HEADS)).then_inc(v_sb, 1)
                if f:
                    level3_hi(i + 3)
                    low_features(i + 3)
                a.wait_ge(shifted, i + 1)
                A.activation(prob[:], prob[:], ACT.Exp).then_inc(exp_done, 1)
                if prev:
                    keep_x2(i - 1)
                a.wait_ge(p_psum, i + 1)
                A.copy(pz[0:LEN, :, :, 0, :],
                       B[5][0:LEN, :].rearrange("k (c h q) -> k c h q", c=PAIRS, h=2)).then_inc(pA_sb, 1)
                if prev:
                    x2_transposed(i - 1, second)
                a.wait_ge(oT_psum, i + 1)
                A.copy(oT[:].rearrange("p c t -> p (c t)"), B[7][:]).then_inc(o_sb, 1)
                if acc:
                    x_hi(i + 1)
                if f:
                    features_hi(i + 3)

            level3_hi(0)
            low_features(0, True)
            level3_hi(1)
            features_hi(0)
            low_features(1)
            a.wait_ge(norm_step, NORM_STEPS)
            a.wait_ge(pads_zeroed, 3)
            x_hi(0)
            features_hi(1)
            level3_hi(2)
            low_features(2)
            features_hi(2)
            a.wait_ge(ld_sw, 32)
            A.copy(sw1[:, 0, :], sw1_in).then_inc(sw_hi, 1)
            A.copy(sw2[:, 0, :, :].rearrange("p c d -> p (c d)"), sw2_in).then_inc(sw_hi, 1)

            a.wait_ge(fill_sent, 16 * (SORTED // FILL))
            iteration(0, True, True, False)
            iteration(1, True, True, True, True)
            with a.Fori(2, TILES - 3) as i:
                iteration(i, True, True)
            iteration(TILES - 3, False, True)
            iteration(TILES - 2, False, True)
            iteration(TILES - 1, False, False)
            keep_x2(TILES - 1)
            x2_transposed(TILES - 1)

            def x_group_hi(g, k, first=False):
                if not first:
                    a.wait_ge(up_psum, (g - 1) * HC)
                a.wait_ge(xg_loaded[k], (g - k) * 8 + 16)
                A.copy(xgh[:, k, :], xg_in[:, k, :]).then_inc(xg_hi, 1)

            def gelus(g, k):
                for c in range(HC):
                    a.wait_ge(up_psum, g * HC + (c + 1))
                    if not (isinstance(g, int) and g == 0 and c < 2):
                        a.wait_ge(gh_lo, g * HC + (c - 1))
                    A.activation(gelu[:, c % 2, :], B[c][:], ACT.Gelu).then_inc(gelu_done, 1)

            x_group_hi(0, 0, True)
            x_group_hi(1, 1, True)
            gelus(0, 0)
            gelus(1, 1)
            x_group_hi(2, 0)
            with a.Fori(2, GROUPS - 2, 2) as g:
                for k in range(2):
                    x_group_hi(g + (k + 1), 1 - k)
                    gelus(g + k, k)
            x_group_hi(GROUPS - 1, 1)
            gelus(GROUPS - 2, 0)
            gelus(GROUPS - 1, 1)

            def silu(j, k):
                a.wait_ge(eu_psum, j + 1)
                nc.scalar.activation(act[:, k, :], B[1 + 2 * k][:], ACT.Silu).then_inc(silu_done, 1)

            def rows_transposed(j, k):
                a.wait_ge(rT_psum, j + 1)
                nc.scalar.copy(rowsT[:, k, :], B[0][:, 0:P]).then_inc(rT_sb, 1)

            def result(j, k, reused=True):
                a.wait_ge(ed_psum, j + 1)
                if reused:
                    a.wait_ge(y_sent[k], (j - k) * 8)
                nc.scalar.copy(y[:, k, :], B[6][:, 0:DIM]).then_inc(y_done, 1)

            rows_transposed(0, 0)
            rows_transposed(1, 1)
            silu(0, 0)
            for j in range(3):
                silu(j + 1, (j + 1) % 2)
                rows_transposed(j + 2, j % 2)
                if j >= 1:
                    result(j - 1, (j - 1) % 2, False)
            with a.Fori(3, SORTED - 3, 2) as i:
                for k in range(2):
                    silu(i + (k + 1), k)
                    rows_transposed(i + (k + 2), 1 - k)
                    result(i + (k - 1), k)
            silu(SORTED - 1, 0)
            for j in range(SORTED - 3, SORTED):
                result(j, j % 2)

        @block.vector
        def _(d):
            V = nc.vector
            d.wait_ge(ld_x, 32)
            n_small = 0

            def step(ins):
                nonlocal n_small
                ins.then_inc(small, 1)
                n_small += 1
                d.wait_ge(small, n_small)

            lev = [P, TILES, CHANNELS, CHANNELS]

            def outer(out_, left, right):
                return V.tensor_tensor(out_.rearrange("p t (a c) -> p t a c", c=CHANNELS), spread(left, 3, lev),
                                       spread(right, 2, lev), ALU.mult)

            s1 = B[1][:, 0:TILES * CHANNELS].rearrange("p (t c) -> p t c", c=CHANNELS)
            step(V.tensor_tensor(v[:], xn_in, xp_in, ALU.subtract))
            V.memset(low[:, :, 0:1], 1.0)
            V.tensor_scalar(vh[:], v[:], 0.5, None, ALU.mult)
            d.wait_ge(s1_psum, 1)
            f2 = low[:, :, 1:1 + CHANNELS]
            step(V.scalar_tensor_tensor(f2, v[:], 0.5, s1, ALU.mult, ALU.add))
            step(outer(e2[:], f2, v[:]))
            V.scalar_tensor_tensor(t3[:], v[:], 1.0 / 3.0, s1, ALU.mult, ALU.add)
            step(V.scalar_tensor_tensor(t4[:], v[:], 0.25, s1, ALU.mult, ALU.add))
            step(outer(low[:, :, 1 + CHANNELS:LOW], t3[:], vh[:]))
            step(V.tensor_scalar(t3[:], v[:], 1.0 / 3.0, None, ALU.mult))
            step(outer(g3[:], t4[:], t3[:]))
            d.wait_ge(s2_psum, 1)
            per = 512 // C2
            for n in range(TILES // per):
                s2 = B[2 + n][:].rearrange("p (t c) -> p t c", c=C2)
                ts = slice(n * per, (n + 1) * per)
                for into in (low[:, ts, 1 + CHANNELS:LOW], g3[:, ts, :]):
                    step(V.tensor_tensor(into, into, s2, ALU.add))
            assert n_small == SMALL_STEPS

            d.wait_ge(ld_c, 64)
            V.tensor_copy(before_r[:], before).then_inc(consts_cast, 1)
            V.tensor_copy(upto_r[:], upto).then_inc(consts_cast, 1)
            V.tensor_copy(ident_b[:], ident).then_inc(consts_cast, 1)
            V.tensor_copy(mask[:], maskf).then_inc(consts_cast, 1)

            def remainder(out_, x_, hi, done):
                return V.tensor_tensor(out_, x_, hi.bitcast(F32), ALU.subtract).then_inc(done, 1)

            for c in range(UC):
                d.wait_ge(w_hi, c + 1)
                remainder(whigh[:, 1, c, :], whigh_in[:, c, :], whigh[:, 0, c, :], w_lo)
            d.wait_ge(w_hi, UC + 1)
            remainder(wlow[:, 1, :], wlow_in, wlow[:, 0, :], w_lo)
            d.wait_ge(q_hi, 1)
            remainder(wqkvT[:, 1, :], wqkvT_in, wqkvT[:, 0, :], q_lo)
            nq = 3 * INNER // P
            n_norm = 0

            def nstep(ins):
                nonlocal n_norm
                ins.then_inc(norm_step, 1)
                n_norm += 1
                d.wait_ge(norm_step, n_norm)

            d.wait_ge(norm_mm, 1)
            nstep(V.tensor_copy(wu[:], B[6][:, 0:nq + 1]))
            d.wait_ge(norm_mm, 2)
            nstep(V.tensor_copy(wtwu[:], B[7][:, 0:1 + PAIRS]))
            V.tensor_tensor(sqs[:, 0:nq], wu[:, 0:nq], wu[:, 0:nq], ALU.mult)
            V.tensor_tensor(sqs[:, nq:nq + 1], wu[:, nq:nq + 1], wu[:, nq:nq + 1], ALU.mult)
            nstep(V.tensor_tensor(sqs[:, 16:17 + PAIRS], wtwu[:], wtwu[:], ALU.mult))
            V.reduce_sum(nrm[:, 0:1], sqs[:, 0:nq], axis=AX)
            V.tensor_copy(nrm[:, 1:2], sqs[:, 16:17])
            V.tensor_copy(nrm[:, 2:3], sqs[:, nq:nq + 1])
            nstep(V.reduce_sum(nrm[:, 3:4], sqs[:, 17:17 + PAIRS], axis=AX))
            d.wait_ge(norm_mm, 3)
            nstep(V.tensor_copy(sqs[:, 0:4], B[6][:, 32:36]))
            nstep(V.reciprocal(fac[:, 6:8], sqs[:, 1:4:2]))
            nstep(V.tensor_tensor(fac[:, 2:4], sqs[:, 0:4:2], fac[:, 6:8], ALU.mult))
            d.wait_ge(norm_root, 1)
            nstep(V.tensor_tensor(fac[:, 4:6], fac[:, 2:4], scal[:, 0:2], ALU.mult))
            d.wait_ge(exp_temp, 1)
            nstep(V.tensor_tensor(fac[:, 1:2], fac[:, 4:5], fac[:, 4:5], ALU.mult))
            nstep(V.tensor_tensor(fac[:, 1:2], fac[:, 1:2], fac[:, 0:1], ALU.mult))
            nstep(V.tensor_tensor(fac[:, 6:7], fac[:, 4:5], fac[:, 5:6], ALU.mult))
            assert n_norm == NORM_STEPS

            def one(ap):
                return ap.rearrange("p o c -> p (o c)")

            def carry():
                V.tensor_copy(scrap[:], ones[:, 0:1])

            def layer_norm(n, done, t, src, dst):
                V.bn_stats(stats[:, n, :], src).then_inc(done, 1)
                d.wait_ge(done, 3 * t + 1)
                carry()
                V.bn_aggr(meanvar[:, n, :], stats[:, n, :]).then_inc(done, 1)
                d.wait_ge(done, 3 * t + 2)
                V.tensor_scalar(rstd[:, n, 0:1], meanvar[:, n, 1:2], EPS, None, ALU.add).then_inc(done, 1)
                d.wait_ge(rooted[n], t + 1)
                return V.tensor_scalar(dst, src, meanvar[:, n, 0:1], rstd[:, n, 1:2], ALU.subtract, ALU.mult)

            def weigh(s, half, first=False):
                cs = slice(half * 4, half * 4 + 4)
                d.wait_ge(y_psum, 2 * s + (half + 1))
                if half == 0 and not first:
                    d.wait_ge(tree, 5 * s - 4)
                V.tensor_tensor(z[:, cs, :], B[1 + half][:].rearrange("p (c d) -> p c d", c=4),
                                spread(v[:, bass.ds(s, 1), cs].rearrange("p o c -> p (o c)"), 2, [P, 4, DIM]),
                                ALU.mult).then_inc(z_sb, 1)

            def tile_h(t):
                return one(h[:, bass.ds(t, 1), :])

            def first_norm(t):
                d.wait_ge(h_psum, t + 1)
                V.tensor_tensor(tile_h(t), B[3][:, P:P + DIM], tokb[:], ALU.add).then_inc(h_read, 1)
                d.wait_ge(h_read, t + 1)
                carry()
                layer_norm(0, ln1, t, tile_h(t), xn[:]).then_inc(xn_ready, 1)
                V.tensor_tensor(tile_h(t), tile_h(t), bout[:], ALU.add).then_inc(h_biased, 1)

            def x_lo(t):
                d.wait_ge(xT_hi, t + 1)
                remainder(xTl[:], B[4][:, 0:P], xTh[:], xT_lo)

            def features_lo(s):
                d.wait_ge(u4_hi, 2 * s + 2)
                remainder(utl[:].rearrange("p c t -> p (c t)"), B[0][:], uth[:].rearrange("p c t -> p (c t)"),
                          u4_lo)
                remainder(lowtl[:], B[3][0:LOW, 0:P], lowth[:], u4_lo)

            def residual(t, first=False):
                d.wait_ge(att_psum, t + 1)
                d.wait_ge(h_biased, t + 1)
                V.scalar_tensor_tensor(tile_h(t), B[7][:, 0:DIM], fac[:, 6:7], tile_h(t), ALU.mult, ALU.add) \
                    .then_inc(h2_done, 1)

            def second_norm(t, first=False):
                if not first:
                    d.wait_ge(x2_kept, t)
                    d.wait_ge(x2T_psum, t)
                d.wait_ge(h2_done, t + 1)
                carry()
                layer_norm(1, ln2, t, tile_h(t), x2n[:]).then_inc(x2_ready, 1)

            def keep_logits(t):
                d.wait_ge(lg_psum, t + 1)
                V.tensor_copy(one(logits[:, bass.ds(t, 1), :]), B[4][:, P:P + EXPERTS]).then_inc(lg_sb, 1)

            def iteration(i, f, u, acc, prev=True, second=True):
                if acc:
                    weigh(i + 1, 1)
                if prev:
                    residual(i - 1)
                d.wait_ge(k_psum, i + 1)
                V.tensor_copy(kT[:].rearrange("p c t -> p (c t)"), B[6][:]).then_inc(k_sb, 1)
                if prev:
                    second_norm(i - 1, second)
                d.wait_ge(s_psum, i + 1)
                sc = B[4][:].rearrange("p (c k) -> p c k", k=LEN)
                V.tensor_reduce(rowmax[:], sc, AX, ALU.max).then_inc(soft, 1)
                d.wait_ge(soft, i + 1)
                V.tensor_tensor(prob[:], sc, spread(rowmax[:], 2, [P, HEADS, LEN]), ALU.subtract) \
                    .then_inc(shifted, 1)
                if acc:
                    first_norm(i + 1)
                if u:
                    weigh(i + 2, 0)
                d.wait_ge(p_psum, i + 1)
                V.tensor_copy(pz[LEN:P, :, :, 1, :],
                              B[5][LEN:P, :].rearrange("k (c h q) -> k c h q", c=PAIRS, h=2)).then_inc(pB_sb, 1)
                d.wait_ge(o_psum, i + 1)
                inv = rinv[:].rearrange("p (b h) -> p b h", b=2)
                V.reciprocal(inv.unsqueeze(3), heads_out[:, :, :, HEAD_DIM:]).then_inc(o_inv, 1)
                d.wait_ge(o_inv, i + 1)
                V.tensor_tensor(on[:].rearrange("p (b h) e -> p b h e", b=2), heads_out[:, :, :, 0:HEAD_DIM],
                                spread(inv, 3, [P, 2, 4, HEAD_DIM]), ALU.mult).then_inc(on_ready, 1)
                if prev:
                    keep_logits(i - 1)
                if acc:
                    x_lo(i + 1)
                if f:
                    features_lo(i + 3)

            features_lo(0)
            weigh(0, 0, True)
            weigh(0, 1)
            first_norm(0)
            x_lo(0)
            features_lo(1)
            weigh(1, 0)
            features_lo(2)
            d.wait_ge(sw_hi, 2)
            remainder(sw1[:, 1, :], sw1_in, sw1[:, 0, :], sw_lo)
            remainder(sw2[:, 1, :, :].rearrange("p c d -> p (c d)"), sw2_in, sw2[:, 0, :, :].rearrange("p c d -> p (c d)"), sw_lo)
            iteration(0, True, True, True, False)
            iteration(1, True, True, True, True, True)
            with d.Fori(2, TILES - 3) as i:
                iteration(i, True, True, True, True, False)
            iteration(TILES - 3, False, True, True, True, False)
            iteration(TILES - 2, False, False, True, True, False)
            iteration(TILES - 1, False, False, False, True, False)
            residual(TILES - 1)
            second_norm(TILES - 1)
            keep_logits(TILES - 1)

            def x_group_lo(g, k):
                d.wait_ge(xg_hi, g + 1)
                remainder(xgl[k], xg_in[:, k, :], xgh[:, k, :], xg_lo)

            x_group_lo(0, 0)
            x_group_lo(1, 1)

            n_route = 0

            def rstep(ins):
                nonlocal n_route
                ins.then_inc(route, 1)
                n_route += 1
                d.wait_ge(route, n_route)

            te = [P, TILES, EXPERTS]
            d.wait_ge(lg_sb, TILES)
            V.memset(zeros[:], 0.0)
            rstep(V.tensor_reduce(best[:, 0, :], logits[:], AX, ALU.max))
            rstep(V.tensor_tensor(pick[:], logits[:], spread(best[:, 0, :], 2, te), ALU.is_equal))
            rstep(V.tensor_tensor(pick[:], pick[:], spread(rev_expert, 1, te), ALU.mult))
            rstep(V.tensor_reduce(best[:, 1, :], pick[:], AX, ALU.max))
            rstep(V.tensor_tensor(oh[:], spread(rev_expert, 1, te), spread(best[:, 1, :], 2, te), ALU.is_equal))
            d.wait_ge(rank_psum, 1)
            te_bank = B[7][:, 0:TILES * EXPERTS].rearrange("p (t e) -> p e t", e=EXPERTS)
            rstep(V.tensor_copy(tot[:], te_bank))
            rstep(V.tensor_tensor_scan(incl[:].rearrange("p e t -> p (e t)"),
                                       tot[:].rearrange("p e t -> p (e t)"), zeros[:], 0.0, ALU.add, ALU.add))
            last = incl[:, :, TILES - 1]
            start, count, ntiles, end_t, base = (rt[:, n, :] for n in range(5))
            V.memset(start[:, 0:1], 0.0)
            rstep(V.tensor_copy(start[:, 1:EXPERTS], last[:, 0:EXPERTS - 1]))
            rstep(V.tensor_tensor(count, last, start, ALU.subtract))
            rstep(V.tensor_tensor(over[:], spread(count, 2, [P, EXPERTS, TILES]),
                                  spread(tile_edges, 1, [P, EXPERTS, TILES]), ALU.is_gt))
            rstep(V.reduce_sum(ntiles, over[:], axis=AX))
            rstep(V.tensor_tensor_scan(end_t, ntiles, zeros[:, 0:EXPERTS], 0.0, ALU.add, ALU.add))
            rstep(V.tensor_tensor(base, end_t, ntiles, ALU.subtract))
            rstep(V.scalar_tensor_tensor(base, base, float(P), start, ALU.mult, ALU.subtract))
            rstep(V.tensor_tensor(off[:], incl[:], tot[:], ALU.subtract))
            rstep(V.tensor_tensor(off[:], off[:], spread(base, 2, [P, EXPERTS, TILES]), ALU.add))
            rstep(V.tensor_tensor(pick[:], off[:].rearrange("p e t -> p t e"),
                                  B[6][:, 0:TILES * EXPERTS].rearrange("p (t e) -> p t e", e=EXPERTS), ALU.add))
            rstep(V.tensor_tensor(pick[:], pick[:], oh[:], ALU.mult))
            rstep(V.reduce_sum(pos_f[:], pick[:], axis=AX))
            V.tensor_copy(pos[:], pos_f[:]).then_inc(pos_ready, 1)
            se = [P, SORTED, EXPERTS]
            rstep(V.tensor_tensor(upt[:], spread(end_t, 1, se), spread(tile_index, 2, se), ALU.is_le))
            rstep(V.reduce_sum(exp_f[:], upt[:], axis=AX))
            V.tensor_scalar(exp_i[:], exp_f[:], float(EXPERTS - 1), None, ALU.min).then_inc(pos_ready, 1)
            assert n_route == ROUTE_STEPS

            def split_gelu(g, k):
                for c in range(HC):
                    d.wait_ge(gelu_done, g * HC + (c + 1))
                    V.tensor_copy(ghh[k][:, c, :], gelu[:, c % 2, :]).then_inc(gh_hi, 1)
                    d.wait_ge(gh_hi, g * HC + (c + 1))
                    remainder(ghl[k][:, c, :], gelu[:, c % 2, :], ghh[k][:, c, :], gh_lo)

            def add_shared(g, k):
                d.wait_ge(down_psum, g + 1)
                hg = h[:, bass.ds(g * GROUP, GROUP), :].rearrange("p t d -> p (t d)")
                V.tensor_tensor(hg, hg, B[4 + k][:], ALU.add).then_inc(added, 1)

            split_gelu(0, 0)
            split_gelu(1, 1)
            x_group_lo(2, 0)
            add_shared(0, 0)
            with d.Fori(2, GROUPS - 2, 2) as g:
                for k in range(2):
                    x_group_lo(g + (k + 1), 1 - k)
                    split_gelu(g + k, k)
                    add_shared(g + (k - 1), 1 - k)
            x_group_lo(GROUPS - 1, 1)
            split_gelu(GROUPS - 2, 0)
            add_shared(GROUPS - 3, 1)
            split_gelu(GROUPS - 1, 1)
            add_shared(GROUPS - 2, 0)
            add_shared(GROUPS - 1, 1)

            def keep_ids(j, k):
                d.wait_ge(rows_in[k], (j - k) * 8 + 16)
                V.tensor_copy(ids[:, bass.ds(j, 1)], rows[:, k, DIM:ROW].bitcast(U32)).then_inc(id_kept, 1)

            def gate(j, k):
                d.wait_ge(silu_done, j + 1)
                V.tensor_tensor(hid[:, k, :], act[:, k, :], B[2 + 2 * k][:], ALU.mult).then_inc(hid_done, 1)

            def hidden_transposed(j, k):
                d.wait_ge(hT_psum, j + 1)
                V.tensor_copy(hidT[:, k, :, :].rearrange("p c t -> p (c t)"), B[5][:]).then_inc(hT_sb, 1)

            keep_ids(0, 0)
            keep_ids(1, 1)
            gate(0, 0)
            hidden_transposed(0, 0)
            gate(1, 1)
            keep_ids(2, 0)
            with d.Fori(1, SORTED - 3, 2) as i:
                for k in range(2):
                    hidden_transposed(i + k, 1 - k)
                    gate(i + (k + 1), k)
                    keep_ids(i + (k + 2), 1 - k)
            hidden_transposed(SORTED - 2, 1)
            gate(SORTED - 1, 0)
            hidden_transposed(SORTED - 1, 0)

        @block.tensor
        def _(pe):
            T = nc.tensor

            def mm(out_, lhsT, rhs, start=True, stop=True):
                return T.matmul(out_, lhsT, rhs, start=start, stop=stop)

            def col(c, n=P):
                return slice(c * n, (c + 1) * n)

            pe.wait_ge(ld_c, 64)
            pe.wait_ge(small, 1)
            mm(B[1][:, 0:TILES * CHANNELS], before, v[:].rearrange("p t c -> p (t c)")).then_inc(s1_psum, 1)
            pe.wait_ge(small, 3)
            per = 512 // C2
            for n in range(TILES // per):
                last = mm(B[2 + n][:], before, e2[:, n * per:(n + 1) * per, :].rearrange("p t c -> p (t c)"))
            last.then_inc(s2_psum, 1)

            pe.wait_ge(ld_sn, 80)
            pe.wait_ge(ld_att, 64)
            nq = 3 * INNER // P
            for c in range(nq):
                mm(B[6][:, c:c + 1], wqkvT_in[:, col(c)], uq[:])
            for c in range(PAIRS):
                last = mm(B[6][:, nq:nq + 1], woutT[:, c, :], uo[:, c:c + 1], c == 0, c == PAIRS - 1)
            last.then_inc(norm_mm, 1)
            pe.wait_ge(norm_step, 1)
            for c in range(nq):
                mm(B[7][:, 0:1], wqkv_sb[:, c, :], wu[:, c:c + 1], c == 0, c == nq - 1)
            for c in range(PAIRS):
                last = mm(B[7][:, 1 + c:2 + c], wout_sb[:, col(c)], wu[:, nq:nq + 1])
            last.then_inc(norm_mm, 1)
            pe.wait_ge(norm_step, 4)
            mm(B[6][:, 32:36], ones, nrm[:]).then_inc(norm_mm, 1)

            def features(s, part):
                if part == 0:
                    pe.wait_ge(e3_lo, s + 1)
                for c in range(2 * part, 2 * part + 2):
                    T.matmul(B[0][:, col(c)], g4[:, col(c)], ident, is_transpose=True, start=True, stop=False)
                    mm(B[0][:, col(c)], e3h[:, col(c)], before_r[:], False, False)
                    mm(B[0][:, col(c)], e3l[:, col(c)], before_r[:], False, True)
                if part == 1:
                    pe.wait_ge(low_ready, s + 1)
                    T.transpose(B[3][0:LOW, 0:P], low_tile[:], ident).then_inc(u4_psum, 1)

            def project(s, lo, hi, first=False):
                if lo == 0:
                    if not first:
                        pe.wait_ge(z_sb, 2 * s - 1)
                    pe.wait_ge(u4_hi, 2 * s + 2)
                    pe.wait_ge(u4_lo, 2 * s + 2)
                for n in range(lo, hi):
                    half_, c = divmod(n, UC + 1)
                    bank, cols = B[1 + half_][:], col(half_, 512)
                    if c < UC:
                        uh, ul, wh_, wl_ = uth[:, c, :], utl[:, c, :], whigh[:, 0, c, cols], whigh[:, 1, c, cols]
                    else:
                        uh, ul, wh_, wl_ = lowth[:], lowtl[:], wlow[:, 0, cols], wlow[:, 1, cols]
                    mm(bank, uh, wh_, c == 0, False)
                    mm(bank, uh, wl_, False, False)
                    last = mm(bank, ul, wh_, False, c == UC)
                    if c == UC:
                        last.then_inc(y_psum, 1)

            def accumulate(s):
                pe.wait_ge(tree, 5 * s + 5)
                mm(B[3][:, P:P + DIM], upto_r[:], z1h[:], True, False)
                mm(B[3][:, P:P + DIM], upto_r[:], z1l[:], False, True).then_inc(h_psum, 1)

            def x_columns(t, first=False):
                pe.wait_ge(xn_ready, t + 1)
                if not first:
                    pe.wait_ge(lg_sb, t - 1)
                T.transpose(B[4][:, 0:P], xn[:], ident).then_inc(xT_psum, 1)

            def three(out_, lhs, rhs):
                mm(out_, lhs[0], rhs[0], True, False)
                mm(out_, lhs[0], rhs[1], False, False)
                return mm(out_, lhs[1], rhs[0], False, True)

            def x2_columns(t):
                pe.wait_ge(x2_ready, t + 1)
                T.transpose(B[4][:, 0:P], x2n[:], ident).then_inc(x2T_psum, 1)

            def router(t):
                pe.wait_ge(x2T_sb, t + 1)
                mm(B[4][:, P:P + EXPERTS], x2t[:], gateT[:]).then_inc(lg_psum, 1)

            def iteration(i, f, u, acc, prev=True, second=False):
                x = (xTh[:], xTl[:])
                pe.wait_ge(xT_hi, i + 1)
                pe.wait_ge(xT_lo, i + 1)
                for c in range(PAIRS):
                    last = three(B[5][:, col(c)], [wqkvT[:, n, col(c)] for n in range(2)], x)
                last.then_inc(q_psum, 1)
                for c in range(PAIRS):
                    last = three(B[6][:, col(c)], [wqkvT[:, n, col(PAIRS + c)] for n in range(2)], x)
                last.then_inc(k_psum, 1)
                if prev:
                    pe.wait_ge(h2_done, i)
                three(B[7][:], x, [wqkvT[:, n, 2 * INNER:] for n in range(2)]).then_inc(v_psum, 1)
                if u:
                    project(i + 2, 0, 2)
                pe.wait_ge(q_sb, 2 * i + 2)
                pe.wait_ge(k_sb, i + 1)
                T.matmul(B[4][:], ident_b[:], mask[:], start=True, stop=False)
                for c in range(PAIRS):
                    for s in range(2):
                        last = mm(B[4][:, col(2 * c + s, LEN)], qz[:, c, s, :, :].rearrange("p h q -> p (h q)"),
                                  kT[:, c, col(s, LEN)], False, c == PAIRS - 1 and s == 1)
                last.then_inc(s_psum, 1)
                if u:
                    project(i + 2, 2, 4)
                if acc:
                    accumulate(i + 1)
                if u:
                    if acc:
                        pe.wait_ge(z_sb, 2 * i + 4)
                    project(i + 2, 4, 6)
                pe.wait_ge(exp_done, i + 1)
                for c in range(PAIRS):
                    last = T.transpose(B[5][:, col(c)], prob[:, 2 * c:2 * c + 2, :].rearrange("p s k -> p (s k)"),
                                       ident)
                last.then_inc(p_psum, 1)
                if prev:
                    x2_columns(i - 1)
                if u:
                    project(i + 2, 6, 7)
                pe.wait_ge(v_sb, i + 1)
                pe.wait_ge(pA_sb, i + 1)
                pe.wait_ge(pB_sb, i + 1)
                for c in range(PAIRS):
                    for hd in range(2):
                        n = 2 * c + hd
                        last = mm(heads_out[:, n // 4, n % 4, :], pz[:, c, hd, :, :].rearrange("k s q -> k (s q)"), vv[:, n, :])
                last.then_inc(o_psum, 1)
                if prev:
                    router(i - 1)
                if u:
                    project(i + 2, 7, 8)
                if f:
                    features(i + 3, 0)
                pe.wait_ge(on_ready, i + 1)
                for c in range(PAIRS):
                    last = T.transpose(B[7][:, col(c)], on[:, 2 * c:2 * c + 2, :].rearrange("p s k -> p (s k)"),
                                       ident)
                last.then_inc(oT_psum, 1)
                if u:
                    project(i + 2, 8, 9)
                pe.wait_ge(o_sb, i + 1)
                for c in range(PAIRS):
                    last = mm(B[7][:, 0:DIM], oT[:, c, :], woutT[:, c, :], c == 0, c == PAIRS - 1)
                last.then_inc(att_psum, 1)
                if u:
                    project(i + 2, 9, 10)
                if acc:
                    if prev:
                        x_columns(i + 1)
                    else:
                        x_columns(i + 1, True)
                if f:
                    pe.wait_ge(h_read, i + 2)
                    features(i + 3, 1)

            pe.wait_ge(small, SMALL_STEPS)
            pe.wait_ge(norm_mm, 3)
            pe.wait_ge(norm_step, 5)
            pe.wait_ge(consts_cast, 4)
            features(0, 0)
            features(0, 1)
            pe.wait_ge(w_lo, UC + 1)
            pe.wait_ge(q_lo, 1)
            project(0, 0, 10, True)
            accumulate(0)
            pe.wait_ge(h_read, 1)
            features(1, 0)
            features(1, 1)
            x_columns(0, True)
            pe.wait_ge(z_sb, 2)
            project(1, 0, 10)
            features(2, 0)
            features(2, 1)
            iteration(0, True, True, True, False)
            with pe.Fori(1, TILES - 3) as i:
                iteration(i, True, True, True)
            iteration(TILES - 3, False, True, True)
            iteration(TILES - 2, False, False, True)
            iteration(TILES - 1, False, False, False)
            pe.wait_ge(lg_sb, TILES - 1)
            x2_columns(TILES - 1)
            router(TILES - 1)

            pe.wait_ge(sw_lo, 2)

            def up(g, k, first=False):
                pe.wait_ge(xg_lo, g + 1)
                for c in range(HC):
                    if not first:
                        pe.wait_ge(gelu_done, g * HC + (c + 1 - HC))
                    three(B[c][:], [sw1[:, n, col(c)] for n in range(2)], (xgh[:, k, :], xgl[k])) \
                        .then_inc(up_psum, 1)

            def down(g, k, first=False):
                pe.wait_ge(gh_lo, (g + 1) * HC)
                if not first:
                    pe.wait_ge(added, g - 1)
                for t in range(GROUP):
                    for c in range(HC):
                        out_, gh_h, gh_l = B[4 + k][:, col(t)], ghh[k][:, c, col(t)], ghl[k][:, c, col(t)]
                        mm(out_, gh_h, sw2[:, 0, c, :], c == 0, False)
                        mm(out_, gh_h, sw2[:, 1, c, :], False, False)
                        last = mm(out_, gh_l, sw2[:, 0, c, :], False, c == HC - 1)
                last.then_inc(down_psum, 1)

            up(0, 0, True)
            pe.wait_ge(route, 5)
            mm(B[6][:, 0:TILES * EXPERTS], below, oh[:].rearrange("p t e -> p (t e)"))
            mm(B[7][:, 0:TILES * EXPERTS], ones, oh[:].rearrange("p t e -> p (t e)")).then_inc(rank_psum, 1)
            up(1, 1)
            down(0, 0, True)
            up(2, 0)
            down(1, 1, True)
            with pe.Fori(2, GROUPS - 3, 2) as g:
                up(g + 1, 1)
                down(g, 0)
                up(g + 2, 0)
                down(g + 1, 1)
            up(GROUPS - 1, 1)
            down(GROUPS - 2, 0)
            down(GROUPS - 1, 1)

            def expert(j):
                return pe.value_load(exp_i[0:1, bass.ds(j, 1)], min_val=0, max_val=EXPERTS - 1)

            def rows_in_columns(j, k, first=False):
                pe.wait_ge(rows_in[k], (j - k) * 8 + 16)
                if not first:
                    pe.wait_ge(rT_sb, j)
                T.transpose(B[0][:, 0:P], rows[:, k, 0:DIM], ident).then_inc(rT_psum, 1)

            def expert_up(j, k, first=False):
                e = expert(j)
                pe.wait_ge(rT_sb, j + 1)
                if not first:
                    pe.wait_ge(hid_done, j - 1)
                mm(B[1 + 2 * k][:], rowsT[:, k, :], w13[:, bass.ds(e, 1), 0:HIDDEN].rearrange("p o i -> p (o i)"))
                mm(B[2 + 2 * k][:], rowsT[:, k, :], w13[:, bass.ds(e, 1), HIDDEN:].rearrange("p o i -> p (o i)")) \
                    .then_inc(eu_psum, 1)

            def hidden_in_columns(j, k, first=False):
                pe.wait_ge(hid_done, j + 1)
                if not first:
                    pe.wait_ge(hT_sb, j)
                for c in range(HC):
                    last = T.transpose(B[5][:, col(c)], hid[:, k, col(c)], ident)
                last.then_inc(hT_psum, 1)

            def expert_down(j, k, first=False):
                e = expert(j)
                pe.wait_ge(hT_sb, j + 1)
                if not first:
                    pe.wait_ge(y_done, j)
                for c in range(HC):
                    last = mm(B[6][:, 0:DIM], hidT[:, k, c, :],
                              w2[:, bass.ds(e, 1), c, :].rearrange("p o d -> p (o d)"), c == 0, c == HC - 1)
                last.then_inc(ed_psum, 1)

            pe.wait_ge(pos_ready, 2)
            pe.wait_ge(added, GROUPS)
            pe.wait_ge(ld_ffn, 32)
            rows_in_columns(0, 0, True)
            rows_in_columns(1, 1)
            expert_up(0, 0, True)
            expert_up(1, 1, True)
            hidden_in_columns(0, 0, True)
            rows_in_columns(2, 0)
            expert_up(2, 0)
            hidden_in_columns(1, 1)
            rows_in_columns(3, 1)
            expert_down(0, 0, True)
            with pe.Fori(2, SORTED - 4, 2) as j:
                for k in range(2):
                    expert_up(j + (k + 1), 1 - k)
                    hidden_in_columns(j + k, k)
                    rows_in_columns(j + (k + 2), k)
                    expert_down(j + (k - 1), 1 - k)
            for j in range(SORTED - 3, SORTED + 1):
                if j + 1 < SORTED:
                    expert_up(j + 1, (j + 1) % 2)
                if j < SORTED:
                    hidden_in_columns(j, j % 2)
                if j + 2 < SORTED:
                    rows_in_columns(j + 2, j % 2)
                expert_down(j - 1, (j - 1) % 2)


_IN = ["x_next", "x_prev", "w_low", "w_high", "tok_b", "wqkv_t", "wqkv", "u_qkv", "wout_t", "wout", "u_out",
       "b_out", "scalars", "gate_t", "w13_t", "w2_t", "sw1_t", "sw2_t", "square", "mask_c", "steps"]


def kernel(x, L0_tok_W, L0_tok_b, L0_attn_w_qkv, L0_attn_u_qkv, L0_attn_sigma_qkv, L0_attn_w_out,
           L0_attn_b_out, L0_attn_u_out, L0_attn_sigma_out, L0_attn_temperature, L0_ffn_gate_w,
           L0_ffn_w1, L0_ffn_w2, L0_ffn_w3, L0_ffn_sw1, L0_ffn_sw2):
    import numpy as np
    import concourse.bacc as bacc
    from concourse.bass_utils import run_bass_kernel_spmd

    time = np.arange(LEN, dtype=np.float32) * (np.float32(1) / np.float32(LEN - 1))
    path = np.concatenate([np.broadcast_to(time[None, :, None], (SEQS, LEN, 1)), np.asarray(x)], axis=-1)

    def tokens(a):
        padded = np.zeros((SEQS, LEN, CHANNELS), np.float32)
        padded[:, :LEN - 1] = a
        return padded.reshape(TILES, P, CHANNELS).transpose(1, 0, 2)

    def on_all(a):
        a = np.asarray(a)
        return np.broadcast_to(a.reshape(1, -1), (P, a.size))

    w = np.asarray(L0_tok_W).reshape(DIM, LOW + C3, CHANNELS).transpose(1, 2, 0).reshape(LOW + C3, -1)
    w1, w2, w3 = np.asarray(L0_ffn_w1), np.asarray(L0_ffn_w2), np.asarray(L0_ffn_w3)
    wqkv, wout = np.asarray(L0_attn_w_qkv), np.asarray(L0_attn_w_out)
    n = np.arange(P)
    same = n[:, None] // LEN == n[None, :] // LEN
    key = np.arange(C3) % LEN
    masked = (key[None, :] == n[:, None] % LEN) | (key[None, :] == LEN - 1)
    arrays = {
        "x_next": tokens(path[:, 1:]),
        "x_prev": tokens(path[:, :-1]),
        "w_low": w[:LOW],
        "w_high": w[LOW:].reshape(UC, P, -1).transpose(1, 0, 2),
        "tok_b": on_all(L0_tok_b),
        "wqkv_t": wqkv.T,
        "wqkv": wqkv.reshape(-1, P, DIM).transpose(1, 0, 2),
        "u_qkv": np.asarray(L0_attn_u_qkv).reshape(P, 1),
        "wout_t": wout.T.reshape(PAIRS, P, DIM).transpose(1, 0, 2),
        "wout": wout,
        "u_out": np.asarray(L0_attn_u_out).reshape(PAIRS, P).T,
        "b_out": on_all(L0_attn_b_out),
        "scalars": np.stack([np.broadcast_to(np.asarray(s), (P,)) for s in
                             (L0_attn_sigma_qkv, L0_attn_sigma_out, L0_attn_temperature)], axis=1),
        "gate_t": np.asarray(L0_ffn_gate_w).T,
        "w13_t": np.concatenate([w1, w3], axis=1).transpose(2, 0, 1),
        "w2_t": w2.reshape(EXPERTS, DIM, HC, P).transpose(3, 0, 2, 1),
        "sw1_t": np.asarray(L0_ffn_sw1).T,
        "sw2_t": np.asarray(L0_ffn_sw2).T.reshape(HC, P, DIM).transpose(1, 0, 2),
        "square": np.stack([n[:, None] == n[None, :], same & (n[:, None] < n[None, :]),
                            same & (n[:, None] <= n[None, :]), n[:, None] < n[None, :],
                            np.ones((P, P), bool)], axis=1).astype(np.float32),
        "mask_c": np.where(masked, np.float32(-3e38), np.float32(0)),
        "steps": on_all(np.concatenate([EXPERTS - np.arange(EXPERTS), P * np.arange(TILES),
                                        np.arange(SORTED)]).astype(np.float32)),
    }
    arrays = {k: np.ascontiguousarray(a) for k, a in arrays.items()}
    nc = bacc.Bacc("TRN2", target_bir_lowering=False, num_devices=1)
    args = [nc.dram_tensor(k, arrays[k].shape, F32, kind="ExternalInput").ap() for k in _IN]
    out = nc.dram_tensor("out", (TILES * P, DIM), F32, kind="ExternalOutput").ap()
    build(nc, *args, out)
    r = run_bass_kernel_spmd(nc, [arrays], core_ids=[0])
    return r.results[0]["out"].reshape(SEQS, LEN, DIM)[:, :LEN - 1]
```

```python
from contextlib import ExitStack

import concourse.bass as bass
from concourse import mybir

F32 = mybir.dt.float32
F32R = mybir.dt.float32r
BF16 = mybir.dt.bfloat16
I32 = mybir.dt.int32
U32 = mybir.dt.uint32
ALU = mybir.AluOpType
ACT = mybir.ActivationFunctionType
AX = mybir.AxisListType.X

P = 128
SEQS, LEN, CHANNELS = 64, 64, 8
TILES = SEQS * LEN // P
DIM = 128
HEADS, HEAD_DIM = 8, 64
PAIRS = HEADS // 2
INNER = HEADS * HEAD_DIM
EXPERTS, HIDDEN = 8, 512
HC = HIDDEN // P
SORTED = TILES + EXPERTS - 1
ROW = DIM + 1
C2 = CHANNELS * CHANNELS
C3 = C2 * CHANNELS
FEW = 1 + CHANNELS
LOW = FEW + C2
FEW_STEP = 16
STACKED = C2 + 2 * FEW_STEP + FEW
UC = C3 // P
EPS = 1e-5
NO_TOKEN = 1 << 20

SUM_BANKS = (3, 2, 4, 5)
E2_STEPS = (7, 9, 10, 11)
FIRST_GROUP_STEPS, SECOND_GROUP_STEPS = 13, 16
EXPERT_UNROLL = 8
GROUP = 4
GROUPS = TILES // GROUP
LAST, LAST_BUT_ONE = TILES - 1, TILES - 2
FILL = SORTED // 3
SMALL_STEPS, NORM_STEPS, ROUTE_STEPS = 20, 10, 21
SQUARED_STEP = 6


def spread(ap, axis, shape):
    return ap.unsqueeze(axis).to_broadcast(shape)


def is_tile(i, t):
    return isinstance(i, int) and i == t


def build(nc, x_next, x_prev, w_low, w_high, tok_b, wqkv, u_qkv, wout_t, wout, u_out, b_out,
          scalars, gate_t, w13_t, w2_t, sw1_t, sw2_t, square, mask_c, steps, out):
    with ExitStack() as ctx:
        def sb(name, shape, dt=F32):
            return ctx.enter_context(nc.sbuf_tensor(name, shape, dt))

        def sem(name):
            return ctx.enter_context(nc.semaphore(name))

        x2T_dram = nc.dram_tensor("x2_columns", [P, TILES * P], F32, kind="Internal").ap()
        sorted_rows = nc.dram_tensor("sorted_rows", [SORTED * P, ROW], F32, kind="Internal").ap()

        tail = sb("tail", [P, 2 * HIDDEN])[:]

        x2 = sb("x2", [P, TILES, ROW])
        h = sb("h", [P, TILES, DIM])
        w13 = sb("w13", [P, EXPERTS, 2 * HIDDEN])
        whigh = sb("whigh", [P, 2, UC, CHANNELS * DIM], F32R)
        wlow = sb("wlow", [P, 2, CHANNELS * DIM], F32R)
        tokb = sb("tokb", [P, DIM])
        qkw = sb("qkw", [P, HEADS, DIM])
        vow = sb("vow", [P, 2, HEADS * DIM], F32R)
        def parts(flat, *sizes):
            at = 0
            for size in sizes:
                yield flat[:, at:at + size]
                at += size

        in_c = TILES * CHANNELS
        whigh_in, wqkv_sb, wlow_in = parts(
            w13[:].rearrange("p e n -> p (e n)"), UC * CHANNELS * DIM, 3 * INNER, 2 * CHANNELS * DIM)
        whigh_in = whigh_in.rearrange("p (c n) -> p c n", c=UC)
        wqkv_sb = wqkv_sb.rearrange("p (c d) -> p c d", d=DIM)
        wlow_in = wlow_in.rearrange("p (s n) -> p s n", s=2)
        e2, xn_in, xp_in, wout_sb, sw1_in = parts(
            h[:].rearrange("p t d -> p (t d)"), TILES * C2, in_c, in_c, INNER, HIDDEN)
        wu_terms, wtwu = e2[:, 0:4 * INNER], e2[:, 2 * INNER:4 * INNER]
        e2 = e2.rearrange("p (t a) -> p t a", a=C2)
        xn_in, xp_in = (t.rearrange("p (t c) -> p t c", c=CHANNELS) for t in (xn_in, xp_in))
        fill, t3, t4, v3 = parts(x2[:].rearrange("p t r -> p (t r)"), FILL * ROW, in_c, in_c, in_c)
        fill = fill.rearrange("p (t r) -> p t r", r=ROW)
        t3, t4, v3 = (t.rearrange("p (t c) -> p t c", c=CHANNELS) for t in (t3, t4, v3))
        uq = sb("uq", [P, DIM])
        woutT = sb("woutT", [P, PAIRS, DIM])
        uo = tail[:, 0:INNER]
        bout = sb("bout", [P, DIM])
        scal = sb("scal", [P, 3])
        gateT = sb("gateT", [P, EXPERTS])
        sw1 = sb("sw1", [P, 2, HIDDEN], F32R)
        sw2 = sb("sw2", [P, HC, DIM])
        sq = sb("sq", [P, 5, P])
        ident, before, upto, below, ones = (sq[:, n, :] for n in range(5))
        before_r = sb("before_r", [P, P], F32R)
        ident_b = sb("ident_b", [P, P], BF16)
        mask = sb("mask", [P, C3], BF16)
        stepc = sb("stepc", [P, EXPERTS + TILES + SORTED])
        rev_expert = stepc[:, 0:EXPERTS]
        tile_edges = stepc[:, EXPERTS:EXPERTS + TILES]
        tile_index = stepc[:, EXPERTS + TILES:]

        v = sb("v", [P, TILES, CHANNELS])
        vh = sb("vh", [P, TILES, CHANNELS])
        levels = sb("levels", [P, TILES * (LOW + C2)])
        low = levels[:, 0:TILES * LOW].rearrange("p (t a) -> p t a", a=LOW)
        g3 = levels[:, TILES * LOW:].rearrange("p (t a) -> p t a", a=C2)

        e3 = sb("e3", [P, C3])
        e3h = sb("e3h", [P, C3], F32R)
        e3l = sb("e3l", [P, C3], F32R)
        g4 = sb("g4", [P, C3])
        u4 = sb("u4", [P, C3])
        low_tile = sb("low_tile", [P, 2 * P])
        uth = sb("uth", [P, UC, P], F32R)
        utl = sb("utl", [P, UC, P], F32R)
        lowt = sb("lowt", [P, 2, P], F32R)
        z = sb("z", [P, CHANNELS, DIM])
        maskf = z[:].rearrange("p c d -> p (c d)")[:, 0:C3]
        z4 = sb("z4", [P, 4, DIM])
        z1 = sb("z1", [P, DIM])

        xn = sb("xn", [P, DIM])
        xT = sb("xT", [P, P])
        xTh = sb("xTh", [P, P], F32R)
        xTl = sb("xTl", [P, P], F32R)
        xqk = sb("xqk", [P, PAIRS, 2, 2, LEN])
        xvo = sb("xvo", [P, HEADS, DIM])
        rowmax = sb("rowmax", [P, HEADS])
        prob = sb("prob", [P, HEADS, LEN])
        rinv = sb("rinv", [P, 2, HEADS])
        pz = sb("pz", [P, PAIRS, 2, 2, LEN])
        stats = sb("stats", [P, 2, 6])
        meanvar = sb("meanvar", [P, 2, 2])
        rstd = sb("rstd", [P, 2, 2])
        powers = sb("powers", [P, 2])
        scrap = sb("scrap", [P, 1])
        x2t = sb("x2t", [P, P])
        x2n = sb("x2n", [P, DIM])
        logits = sb("logits", [P, TILES, EXPERTS])

        wu = sb("wu", [P, 3 * INNER // P + 1])
        sqs = sb("sqs", [P, 3 * INNER // P + 1])
        nrm = sb("nrm", [P, 4])
        fac = sb("fac", [P, 8])

        def taker(*hosts):
            parts = [[t, 0] for t in hosts]

            def take(*shape):
                size = 1
                for n in shape:
                    size *= n
                for part in parts:
                    flat, at = part
                    if at + size <= flat.shape[1]:
                        part[1] = at + size
                        ap = flat[:, at:at + size]
                        names = "abcd"[:len(shape)]
                        if len(shape) == 1:
                            return ap
                        return ap.rearrange(f"p ({' '.join(names)}) -> p {' '.join(names)}",
                                            **dict(zip(names, shape)))
                raise AssertionError("no room")
            return take

        late = taker(levels[:, EXPERTS * HC * DIM:], e3[:], g4[:], xvo[:].rearrange("p a b -> p (a b)"),
                     prob[:].rearrange("p a b -> p (a b)"), z4[:].rearrange("p a b -> p (a b)"))
        wide = (z[:].rearrange("p c d -> p (c d)"), xqk[:].rearrange("p a b c d -> p (a b c d)"),
                pz[:].rearrange("p a b c d -> p (a b c d)"), tail)
        late_wide = taker(*wide)
        w2 = levels[:, 0:EXPERTS * HC * DIM].rearrange("p (e c d) -> p e c d", e=EXPERTS, c=HC)

        oh = late(TILES, EXPERTS)
        pick = late(TILES, EXPERTS)
        best = sb("best", [P, 2, TILES])
        tot = late(EXPERTS, TILES)
        incl = late(EXPERTS, TILES)
        zeros = late(EXPERTS * TILES)
        rt = sb("rt", [P, 8, EXPERTS])
        off = late(EXPERTS, TILES)
        over = late(EXPERTS, TILES)
        pos_f = late(TILES)
        pos = sb("pos", [P, TILES], U32)
        upt = late(SORTED, EXPERTS)
        exp_f = late(SORTED)
        exp_i = sb("exp_i", [P, SORTED], I32)

        gelu_take = taker(tail, *wide[:3])
        gelu = [[gelu_take(GROUP * P) for c in range(HC)] for k in range(2)]
        xg_in = sb("xg_in", [P, 2, GROUP * P])
        late_r = taker(vow[:].rearrange("p s n -> p (s n)"))
        xgh = [uth[:].rearrange("p c t -> p (c t)"), late_r(GROUP * P)]
        xgl = [utl[:].rearrange("p c t -> p (c t)"), late_r(GROUP * P)]
        w1h, w1l = (whigh[:, n].rearrange("p c n -> p (c n)").rearrange("p (e i) -> p e i", e=EXPERTS)
                    for n in range(2))
        rowsTh, rowsTl = late_r(2, P), late_r(2, P)
        rows = late(2, ROW)
        ids = sb("ids", [P, SORTED], U32)
        rowsT = late(2, P)
        act = late_wide(2, HIDDEN)
        hid = late_wide(2, HIDDEN)
        hidT = late_wide(2, HC, P)
        y = late(2, DIM)

        B = [ctx.enter_context(nc.psum_tensor(f"bank{n}", [P, 512], F32)) for n in range(8)]

        ld_x, ld_sq, ld_c, ld_w, ld_sn, ld_w13, ld_w2, ld_sw = (
            sem(f"loaded_{n}") for n in ("x", "square", "const", "attention", "norms", "w13", "w2",
                                       "shared"))
        ld_sig = [sem(f"loaded_signature{c}") for c in range(UC + 1)]
        filled, fill_sent = sem("fill_written"), sem("fill_sent")
        consts_cast = sem("consts_cast")
        pads_zeroed = sem("pads_zeroed")
        ids_written = sem("ids_written")
        w_hi, w_lo, w_lo_pool = (sem("signature_weights_hi"), sem("signature_weights_lo"),
                                 sem("signature_weights_lo_by_gpsimd"))
        ww_psum, ww_hi, ww_lo, qkw_sb = (sem("weight_products_psum"), sem("value_out_weights_hi"),
                                         sem("value_out_weights_lo"), sem("query_key_weights"))
        sw_hi, sw_lo = sem("shared_weights_hi"), sem("shared_weights_lo")
        small, s1_psum, s2_psum = sem("small_levels"), sem("s1_psum"), sem("s2_psum")
        g3_outer, wu_ready = sem("g3_outer"), sem("wu_terms")
        recip = sem("norm_reciprocal")
        norm_root, norm_mm, norm_step, exp_temp = (sem("norm_root"), sem("norm_matmul"), sem("norm_step"),
                                                   sem("exp_temperature"))
        before_cast = sem("before_cast")
        e3_ready, e3_hi, e3_lo, g4_ready, low_ready = (sem("e3_ready"), sem("e3_hi"), sem("e3_lo"),
                                                       sem("g4_ready"), sem("low_ready"))
        s3_psum, u4_sb = sem("s3_psum"), sem("u4_sb")
        u4_psum, u4_hi, u4_lo = sem("u4_psum"), sem("u4_hi"), sem("u4_lo")
        y_psum, z_sb, tree, h_psum, h_read = sem("y_psum"), sem("z_sb"), sem("tree"), sem("h_psum"), sem("h_read")
        ln1, ln2, xn_ready, xT_psum = sem("ln1"), sem("ln2"), sem("xn_ready"), sem("xT_psum")
        xT_hi, xT_lo = sem("xT_hi"), sem("xT_lo")
        g_psum, g_sb, vo_psum, vo_sb = sem("xqk_psum"), sem("xqk_sb"), sem("xvo_psum"), sem("xvo_sb")
        s_psum, soft, shifted, exp_done = sem("scores_psum"), sem("row_max"), sem("shifted"), sem("exp_done")
        summed, normalised = sem("row_sums"), sem("probabilities")
        p_psum, pA_sb, pB_sb = sem("probT_psum"), sem("probT_first_seq"), sem("probT_second_seq")
        h_biased, att_psum, h2_done = sem("h_biased"), sem("attention_psum"), sem("h2_done")
        x2_ready, x2T_psum, x2T_sb, x2_kept = sem("x2_ready"), sem("x2T_psum"), sem("x2T_sb"), sem("x2_kept")
        lg_psum, lg_sb = sem("logits_psum"), sem("logits_sb")
        rooted = [sem("ln1_rooted"), sem("ln2_rooted")]
        powers_set = sem("powers_set")
        route, rank_psum, pos_ready, scattered = (sem("route_step"), sem("rank_psum"), sem("pos_ready"),
                                                  sem("scattered"))
        xg_hi, xg_lo, gelu_done = sem("x_group_hi"), sem("x_group_lo"), sem("gelu_done")
        up_psum, down_psum, added = sem("up_psum"), sem("down_psum"), sem("added")
        x2T_sent = sem("x2T_sent")
        xg_loaded = [sem(f"x_group_loaded{n}") for n in range(2)]
        out_sent = [sem(f"out_sent{n}") for n in range(GROUPS)]
        rows_in = [sem(f"rows_in{n}") for n in range(2)]
        id_kept = sem("id_kept")
        rT_psum, rT_hi, rT_lo = sem("rowsT_psum"), sem("rowsT_hi"), sem("rowsT_lo")
        w1_hi, w1_lo = sem("w1_hi"), sem("w1_lo")
        eu_psum, silu_done, hid_done = sem("expert_up_psum"), sem("silu_done"), sem("hid_done")
        hT_psum, hT_sb, ed_psum, y_done = (sem("hidT_psum"), sem("hidT_sb"), sem("expert_down_psum"),
                                           sem("y_done"))
        y_sent = [sem(f"y_sent{n}") for n in range(2)]

        block = ctx.enter_context(nc.Block())

        @block.sync
        def _(sp):
            sp.dma_start(xn_in, x_next).then_inc(ld_x, 16)
            sp.dma_start(xp_in, x_prev).then_inc(ld_x, 16)
            sp.dma_start(sq[:], square).then_inc(ld_sq, 16)
            for c in range(UC):
                sp.dma_start(whigh_in[:, c, :], w_high[:, c, :]).then_inc(ld_sig[c], 16)
            sp.dma_start(wqkv_sb, wqkv).then_inc(ld_w, 16)
            sp.dma_start(woutT[:], wout_t).then_inc(ld_w, 16)
            sp.dma_start(wlow_in, w_low).then_inc(ld_sig[UC], 16)
            sp.dma_start(wout_sb, wout).then_inc(ld_sn, 16)
            sp.dma_start(uq[:], u_qkv).then_inc(ld_sn, 16)
            sp.dma_start(uo, u_out).then_inc(ld_sn, 16)
            sp.dma_start(scal[:], scalars).then_inc(ld_sn, 16)
            sp.dma_start(maskf[:], mask_c).then_inc(ld_c, 16)
            sp.dma_start(stepc[:], steps).then_inc(ld_c, 16)
            sp.dma_start(tokb[:], tok_b).then_inc(ld_c, 16)
            sp.dma_start(bout[:], b_out).then_inc(ld_c, 16)
            sp.dma_start(gateT[:], gate_t).then_inc(ld_c, 16)
            sp.dma_start(sw1_in, sw1_t).then_inc(ld_sw, 16)
            sp.dma_start(sw2[:], sw2_t).then_inc(ld_sw, 16)
            sp.wait_ge(filled, 1)
            for n in range(SORTED // FILL):
                sp.dma_start(sorted_rows[n * FILL * P:(n + 1) * FILL * P, :].rearrange("(t p) r -> p t r", p=P),
                             fill).then_inc(fill_sent, 16)
            sp.wait_ge(w_lo, UC - 1)
            sp.wait_ge(w_lo_pool, 2)
            sp.wait_ge(norm_mm, 1)
            sp.wait_ge(ww_psum, 4)
            sp.dma_start(w13[:], w13_t).then_inc(ld_w13, 16)

            def spill(t):
                sp.wait_ge(x2T_sb, t + 1)
                sp.dma_start(x2T_dram[:, bass.ds(t * P, P)], x2t[:]).then_inc(x2T_sent, 16)

            def load_group(g):
                sp.dma_start(xg_in[:, g % 2, :], x2T_dram[:, g * GROUP * P:(g + 1) * GROUP * P]) \
                    .then_inc(xg_loaded[g % 2], 16)

            with sp.Fori(0, 2 * GROUP) as t:
                spill(t)
            sp.wait_ge(x2T_sent, 16 * 2 * GROUP)
            load_group(0)
            load_group(1)
            with sp.Fori(2 * GROUP, TILES - 2) as t:
                spill(t)
            for g in range(2):
                sp.wait_ge(xg_lo, g + 1)
                load_group(g + 2)
                spill(TILES - 2 + g)
            sp.dma_start(w2, w2_t).then_inc(ld_w2, 16)
            sp.wait_ge(x2T_sent, 16 * TILES)
            for g in range(GROUPS):
                if g + 4 < GROUPS:
                    sp.wait_ge(xg_lo, g + 3)
                    load_group(g + 4)
                sp.wait_ge(added, g + 1)
                sp.dma_start(out[g * GROUP * P:(g + 1) * GROUP * P, :].rearrange("(t p) d -> p t d", p=P),
                             h[:, g * GROUP:(g + 1) * GROUP, :]).then_inc(out_sent[g], 16)
                if g == GROUPS - 3:
                    sp.wait_ge(scattered, 16 * TILES)
                    for j in range(2):
                        sp.dma_start(rows[:, j, :], sorted_rows[j * P:(j + 1) * P, :]).then_inc(rows_in[j], 16)
            with sp.Fori(2, SORTED - 2, 2) as j:
                for k in range(2):
                    sp.wait_ge(rT_psum, j + (k - 1))
                    sp.wait_ge(id_kept, j + (k - 1))
                    sp.dma_start(rows[:, k, :], sorted_rows[bass.ds((j + k) * P, P), :]).then_inc(rows_in[k], 16)
            sp.wait_ge(rT_psum, SORTED - 2)
            sp.wait_ge(id_kept, SORTED - 2)
            sp.dma_start(rows[:, 0, :], sorted_rows[(SORTED - 1) * P:SORTED * P, :]).then_inc(rows_in[0], 16)

        @block.gpsimd
        def _(pool):
            nc.gpsimd.memset(powers[:, 0:1], -0.5).then_inc(powers_set, 1)
            nc.gpsimd.memset(powers[:, 1:2], 0.5).then_inc(powers_set, 1)
            pool.wait_ge(powers_set, 2)
            nc.gpsimd.memset(low_tile[:], 0.0).then_inc(pads_zeroed, 1)
            nc.gpsimd.memset(pz[:], 0.0).then_inc(pads_zeroed, 1)
            nc.gpsimd.memset(fill[:, :, 0:DIM], 0.0)
            nc.gpsimd.memset(fill[:, :, DIM:ROW].bitcast(I32), NO_TOKEN).then_inc(filled, 1)
            G = nc.gpsimd

            def by3(t):
                return t[:].rearrange("p (o a c) -> p o a c", o=1, c=CHANNELS)

            def level3(s, first=False):
                if not first:
                    pool.wait_ge(s3_psum, s)
                G.tensor_tensor(by3(e3), spread(low[:, bass.ds(s, 1), 1 + CHANNELS:LOW], 3, [P, 1, C2, CHANNELS]),
                                spread(v[:, bass.ds(s, 1), :], 2, [P, 1, C2, CHANNELS]), ALU.mult) \
                    .then_inc(e3_ready, 1)

            def level3_rest(s, first=False):
                if not first:
                    pool.wait_ge(u4_sb, s)
                G.tensor_tensor(by3(g4), spread(g3[:, bass.ds(s, 1), :], 3, [P, 1, C2, CHANNELS]),
                                spread(vh[:, bass.ds(s, 1), :], 2, [P, 1, C2, CHANNELS]), ALU.mult) \
                    .then_inc(g4_ready, 1)
                pool.wait_ge(e3_hi, s + 1)
                G.tensor_tensor(e3l[:], e3[:], e3h[:].bitcast(F32), ALU.subtract).then_inc(e3_lo, 1)

            def add_channels(s):
                pool.wait_ge(z_sb, 2 * s + 2)
                G.tensor_tensor(z4[:], z[:, 0:4, :], z[:, 4:8, :], ALU.add).then_inc(tree, 1)
                pool.wait_ge(tree, 3 * s + 1)
                G.tensor_tensor(z4[:, 0:2, :], z4[:, 0:2, :], z4[:, 2:4, :], ALU.add).then_inc(tree, 1)
                pool.wait_ge(tree, 3 * s + 2)
                G.tensor_tensor(z1[:], z4[:, 0, :], z4[:, 1, :], ALU.add).then_inc(tree, 1)

            def root(n, done, t):
                pool.wait_ge(done, 3 * t + 3)
                G.tensor_tensor(rstd[:, n, 1:2], rstd[:, n, 0:1], powers[:, 0:1], ALU.pow) \
                    .then_inc(rooted[n], 1)

            def iteration(i, f, u, acc):
                if f:
                    level3(i + 3)
                if acc:
                    root(0, ln1, i + 1)
                if f:
                    level3_rest(i + 3)
                if u:
                    add_channels(i + 2)
                root(1, ln2, i)

            def remainder(out_, x_, hi):
                G.tensor_tensor(out_, x_, hi.bitcast(F32), ALU.subtract).then_inc(w_lo_pool, 1)

            pool.wait_ge(small, 5)
            per = 512 // C2
            for ts in (slice(0, per), slice(per, TILES)):
                shape = [P, ts.stop - ts.start, CHANNELS, CHANNELS]
                G.tensor_tensor(g3[:, ts, :].rearrange("p t (a c) -> p t a c", c=CHANNELS),
                                spread(t4[:, ts, :], 3, shape), spread(v3[:, ts, :], 2, shape), ALU.mult) \
                    .then_inc(g3_outer, 1)
            pool.wait_ge(small, FIRST_GROUP_STEPS)
            level3(0, True)
            level3_rest(0, True)
            pool.wait_ge(w_hi, UC)
            remainder(whigh[:, 1, UC - 1, :], whigh_in[:, UC - 1, :], whigh[:, 0, UC - 1, :])
            level3(1)
            level3_rest(1)
            pool.wait_ge(w_hi, UC + 1)
            lo_rows = slice(0, C2 + FEW)
            remainder(wlow[lo_rows, 1, :], wlow_in[lo_rows, 1, :], wlow[lo_rows, 1, :])
            pool.wait_ge(ld_w, 32)
            pool.wait_ge(ld_sn, 64)
            pool.wait_ge(s2_psum, 4)
            G.tensor_tensor(wu_terms[:, 0:3 * INNER].rearrange("p (c d) -> p c d", d=DIM), wqkv_sb,
                            spread(uq[:], 1, [P, 3 * INNER // P, DIM]), ALU.mult)
            G.tensor_tensor(wu_terms[:, 3 * INNER:], wout_sb, uo, ALU.mult).then_inc(wu_ready, 1)
            add_channels(0)
            level3(2)
            level3_rest(2)
            root(0, ln1, 0)
            pool.wait_ge(norm_step, SQUARED_STEP)
            G.tensor_tensor(fac[:, 2:4], fac[:, 2:4], powers[:, 1:2].to_broadcast([P, 2]), ALU.pow) \
                .then_inc(norm_root, 1)
            pool.wait_ge(small, SMALL_STEPS)
            add_channels(1)
            with pool.Fori(0, TILES - 3) as i:
                iteration(i, True, True, True)
            iteration(TILES - 3, False, True, True)
            iteration(TILES - 2, False, False, True)
            iteration(TILES - 1, False, False, False)

            nc.gpsimd.iota(x2[:, :, DIM:ROW].bitcast(I32), pattern=[[P, TILES], [1, 1]], base=0,
                           channel_multiplier=1).then_inc(ids_written, 1)
            pool.wait_ge(pos_ready, 1)
            pool.wait_ge(x2_kept, TILES)
            pool.wait_ge(ids_written, 1)
            for t in range(TILES):
                nc.gpsimd.indirect_dma_start(
                    out=sorted_rows[:, :], out_offset=bass.IndirectOffsetOnAxis(ap=pos[:, t:t + 1], axis=0),
                    in_=x2[:, t, :], in_offset=None).then_inc(scattered, 16)
            for g in range(GROUPS):
                pool.wait_ge(out_sent[g], 16)
            for j in range(SORTED):
                pool.wait_ge(y_done, j + 1)
                nc.gpsimd.indirect_dma_start(
                    out=out[:, :], out_offset=bass.IndirectOffsetOnAxis(ap=ids[:, j:j + 1], axis=0),
                    in_=y[:, j % 2, :], in_offset=None, bounds_check=TILES * P - 1, oob_is_err=False,
                    compute_op=ALU.add).then_inc(y_sent[j % 2], 16)
            pool.wait_ge(y_sent[0], 16 * ((SORTED + 1) // 2))
            pool.wait_ge(y_sent[1], 16 * (SORTED // 2))

        @block.scalar
        def _(a):
            A = nc.scalar
            a.wait_ge(ld_sq, 16)
            A.copy(before_r[:], before).then_inc(before_cast, 1)
            for c in range(UC):
                a.wait_ge(ld_sig[c], 16)
                A.copy(whigh[:, 0, c, :], whigh_in[:, c, :]).then_inc(w_hi, 1)
            def level3_hi(s):
                a.wait_ge(e3_ready, s + 1)
                A.copy(e3h[:], e3[:]).then_inc(e3_hi, 1)

            def low_features(s, first=False):
                if not first:
                    a.wait_ge(u4_psum, s)
                A.copy(low_tile[:, 0:3 * C2].rearrange("p (n a) -> p n a", n=3),
                       low[:, bass.ds(s, 1), FEW:].to_broadcast([P, 3, C2])).then_inc(low_ready, 1)
                A.copy(low_tile[:, 3 * C2:3 * C2 + 3 * FEW_STEP].rearrange("p (n a) -> p n a", n=3)[:, :, 0:FEW],
                       low[:, bass.ds(s, 1), 0:FEW].to_broadcast([P, 3, FEW])).then_inc(low_ready, 1)

            def features_hi(s):
                a.wait_ge(u4_psum, s + 1)
                A.copy(uth[:].rearrange("p c t -> p (c t)"), B[0][:]).then_inc(u4_hi, 1)
                A.copy(lowt[:], B[3][:].rearrange("p (n t) -> p n t", t=P)[:, 0:4:3, :]).then_inc(u4_hi, 1)

            def x_hi(t):
                a.wait_ge(xT_psum, t + 1)
                A.copy(xTh[:], B[3][:, 2 * P:3 * P]).then_inc(xT_hi, 1)
                A.copy(xT[:], B[3][:, 2 * P:3 * P]).then_inc(xT_hi, 1)

            def x2_transposed(t, first=False):
                a.wait_ge(x2T_psum, t + 1)
                if not first:
                    a.wait_ge(x2T_sent, 16 * t)
                A.copy(x2t[:], B[4][:, 0:P]).then_inc(x2T_sb, 1)

            def keep_x2(t):
                a.wait_ge(x2_ready, t + 1)
                A.copy(x2[:, bass.ds(t, 1), 0:DIM].rearrange("p o d -> p (o d)"), x2n[:]).then_inc(x2_kept, 1)

            def iteration(i, f, acc, prev=True, second=False):
                for n in range(2):
                    a.wait_ge(g_psum, 2 * i + (n + 1))
                    A.activation(xqk[:, 2 * n:2 * n + 2].rearrange("p c s h q -> p (c s h q)"), B[5 + n][:],
                                 ACT.Copy, scale=fac[:, 1:2]).then_inc(g_sb, 1)
                for n in range(2):
                    a.wait_ge(vo_psum, 2 * i + (n + 1))
                    A.copy(xvo[:, 4 * n:4 * n + 4, :].rearrange("p h d -> p (h d)"), B[7 - 2 * n][:]) \
                        .then_inc(vo_sb, 1)
                if is_tile(i, LAST):
                    x_group_hi(1, 1)
                if f:
                    low_features(i + 3)
                if prev:
                    keep_x2(i - 1)
                if f:
                    level3_hi(i + 3)
                a.wait_ge(shifted, i + 1)
                A.activation(prob[:], prob[:], ACT.Exp).then_inc(exp_done, 1)
                if acc:
                    x_hi(i + 1)
                if is_tile(i, LAST):
                    gelus(0, 0, range(HC - 1, HC))
                a.wait_ge(p_psum, i + 1)
                A.copy(pz[0:LEN, :, :, 0, :],
                       B[6][0:LEN, :].rearrange("k (c h q) -> k c h q", c=PAIRS, h=2)).then_inc(pA_sb, 1)
                if prev:
                    x2_transposed(i - 1, second)
                if f:
                    features_hi(i + 3)
                if is_tile(i, LAST_BUT_ONE):
                    a.wait_ge(tree, 3 * TILES - 2)
                    gelus(0, 0, range(HC - 1))
                if is_tile(i, LAST):
                    gelus(1, 1, range(2))
                    a.wait_ge(up_psum, HC)
                    x_group_hi(2, 0)

            level3_hi(0)
            a.wait_ge(small, FIRST_GROUP_STEPS)
            a.wait_ge(pads_zeroed, 1)
            low_features(0, True)
            features_hi(0)
            for n in range(2):
                a.wait_ge(ww_psum, n + 1)
                A.copy(qkw[:, 4 * n:4 * n + 4, :].rearrange("p h d -> p (h d)"), B[6 + n][:]).then_inc(qkw_sb, 1)
            a.wait_ge(ld_sig[UC], 16)
            A.copy(wlow[:], wlow_in).then_inc(w_hi, 1)
            a.wait_ge(ld_sn, 64)
            A.activation(fac[:, 0:1], scal[:, 2:3], ACT.Exp).then_inc(exp_temp, 1)
            level3_hi(1)
            low_features(1)
            features_hi(1)
            for n in range(2):
                a.wait_ge(ww_psum, n + 3)
                A.copy(vow[:, 0, n * 512:(n + 1) * 512], B[5 - n][:]).then_inc(ww_hi, 1)
            level3_hi(2)
            low_features(2)
            x_hi(0)
            features_hi(2)
            a.wait_ge(norm_step, NORM_STEPS)
            a.wait_ge(pads_zeroed, 2)
            a.wait_ge(small, SMALL_STEPS)

            a.wait_ge(fill_sent, 16 * (SORTED // FILL))
            iteration(0, True, True, False)
            a.wait_ge(ld_sw, 32)
            A.copy(sw1[:, 0, :], sw1_in).then_inc(sw_hi, 1)
            iteration(1, True, True, True, True)
            with a.Fori(2, TILES - 3) as i:
                iteration(i, True, True)
            iteration(TILES - 3, False, True)

            def x_group_hi(g, k):
                a.wait_ge(xg_loaded[k], (g - k) * 8 + 16)
                A.copy(xgh[k], xg_in[:, k, :]).then_inc(xg_hi, 1)

            def gelus(g, k, chunks=range(HC)):
                for c in chunks:
                    a.wait_ge(up_psum, g * HC + (c + 1))
                    A.activation(gelu[k][c], B[c][:], ACT.Gelu).then_inc(gelu_done, 1)

            a.wait_ge(y_psum, 2 * TILES)
            x_group_hi(0, 0)
            iteration(TILES - 2, False, True)
            iteration(TILES - 1, False, False)
            keep_x2(TILES - 1)
            x2_transposed(TILES - 1)
            a.wait_ge(att_psum, TILES)
            gelus(1, 1, range(2, HC))
            x_group_hi(3, 1)
            a.wait_ge(ld_w13, 16)
            with a.Fori(2, GROUPS - 3, 2) as g:
                for k in range(2):
                    a.wait_ge(down_psum, g + (k - 1))
                    gelus(g + k, k)
                    x_group_hi(g + (k + 2), k)
                    for m in range(2):
                        e = (g + (k - 2)) * 2 + m
                        A.copy(w1h[:, bass.ds(e, 1), :].rearrange("p o n -> p (o n)"),
                               w13[:, bass.ds(e, 1), 0:HIDDEN].rearrange("p o n -> p (o n)")).then_inc(w1_hi, 1)
            for k in range(2):
                a.wait_ge(down_psum, GROUPS - 3 + k)
                gelus(GROUPS - 2 + k, k)

            def silu(j, k):
                a.wait_ge(eu_psum, j + 1)
                nc.scalar.activation(act[:, k, :], B[1 + 2 * k][:], ACT.Silu).then_inc(silu_done, 1)

            def rows_transposed(j, k):
                a.wait_ge(rT_psum, j + 1)
                nc.scalar.copy(rowsTh[:, k, :], B[7 * k][:, 0:P]).then_inc(rT_hi, 1)
                nc.scalar.copy(rowsT[:, k, :], B[7 * k][:, 0:P]).then_inc(rT_hi, 1)

            def result(j, k, reused=True):
                a.wait_ge(ed_psum, j + 1)
                if reused:
                    a.wait_ge(y_sent[k], (j - k) * 8)
                nc.scalar.copy(y[:, k, :], B[6][:, 0:DIM]).then_inc(y_done, 1)

            rows_transposed(0, 0)
            rows_transposed(1, 1)
            silu(0, 0)
            for j in range(3):
                silu(j + 1, (j + 1) % 2)
                rows_transposed(j + 2, j % 2)
                if j >= 1:
                    result(j - 1, (j - 1) % 2, False)
            with a.Fori(3, SORTED - 3, 2) as i:
                for k in range(2):
                    silu(i + (k + 1), k)
                    rows_transposed(i + (k + 2), 1 - k)
                    result(i + (k - 1), k)
            silu(SORTED - 1, 0)
            for j in range(SORTED - 3, SORTED):
                result(j, j % 2)

        @block.vector
        def _(d):
            V = nc.vector
            n_small = 0

            def step(ins):
                nonlocal n_small
                ins.then_inc(small, 1)
                n_small += 1
                return n_small

            def after(n):
                d.wait_ge(small, n)

            def remainder(out_, x_, hi, done):
                return V.tensor_tensor(out_, x_, hi.bitcast(F32), ALU.subtract).then_inc(done, 1)

            def outer(out_, left, right):
                shape = [P, left.shape[1], CHANNELS, CHANNELS]
                return V.tensor_tensor(out_.rearrange("p t (a c) -> p t a c", c=CHANNELS), spread(left, 3, shape),
                                       spread(right, 2, shape), ALU.mult)

            s1 = B[1][:, 0:TILES * CHANNELS].rearrange("p (t c) -> p t c", c=CHANNELS)
            f2 = low[:, :, 1:1 + CHANNELS]
            per = 512 // C2
            groups = [slice(n * per, (n + 1) * per) for n in range(TILES // per)]
            V.memset(low[:, :, 0:1], 1.0)
            V.memset(nrm[:], 0.0)
            d.wait_ge(ld_x, 32)
            after(step(V.tensor_tensor(v[:], xn_in, xp_in, ALU.subtract)))
            step(V.tensor_scalar(vh[:], v[:], 0.5, None, ALU.mult))
            v3_made = step(V.tensor_scalar(v3, v[:], 1.0 / 3.0, None, ALU.mult))
            d.wait_ge(s1_psum, 1)
            f2_made = step(V.scalar_tensor_tensor(f2, v[:], 0.5, s1, ALU.mult, ALU.add))
            t4_made = step(V.scalar_tensor_tensor(t4, v[:], 0.25, s1, ALU.mult, ALU.add))
            assert max(v3_made, t4_made) == 5
            t3_made = step(V.scalar_tensor_tensor(t3, v[:], 1.0 / 3.0, s1, ALU.mult, ALU.add))
            def low_outer(ts):
                return step(outer(low[:, ts, 1 + CHANNELS:LOW], t3[:, ts, :], vh[:, ts, :]))

            after(f2_made)
            for n, ts in enumerate(groups):
                made = step(outer(e2[:, ts, :], f2[:, ts, :], v[:, ts, :]))
                assert made == E2_STEPS[n]
                if n == 0:
                    after(t3_made)
                    first_made = low_outer(ts)

            def add_s2(n):
                s2 = B[SUM_BANKS[n]][:].rearrange("p (t c) -> p t c", c=C2)
                d.wait_ge(s2_psum, n + 1)
                step(V.tensor_tensor(low[:, groups[n], 1 + CHANNELS:LOW], low[:, groups[n], 1 + CHANNELS:LOW], s2,
                                     ALU.add))
                d.wait_ge(g3_outer, 1 if n == 0 else 2)
                step(V.tensor_tensor(g3[:, groups[n], :], g3[:, groups[n], :], s2, ALU.add))

            def level4(s):
                d.wait_ge(s3_psum, s + 1)
                d.wait_ge(g4_ready, s + 1)
                V.tensor_tensor(u4[:], B[0][:], g4[:], ALU.add).then_inc(u4_sb, 1)

            after(first_made)
            add_s2(0)
            assert n_small == FIRST_GROUP_STEPS
            rest_made = low_outer(slice(per, TILES))
            for c in range(UC - 1):
                if c == UC - 2:
                    level4(0)
                d.wait_ge(w_hi, c + 1)
                remainder(whigh[:, 1, c, :], whigh_in[:, c, :], whigh[:, 0, c, :], w_lo)

            def one(ap):
                return ap.rearrange("p o c -> p (o c)")

            def carry():
                V.tensor_copy(scrap[:], ones[:, 0:1])

            def layer_norm(n, done, t, src, dst):
                V.bn_stats(stats[:, n, :], src).then_inc(done, 1)
                d.wait_ge(done, 3 * t + 1)
                carry()
                V.bn_aggr(meanvar[:, n, :], stats[:, n, :]).then_inc(done, 1)
                d.wait_ge(done, 3 * t + 2)
                V.tensor_scalar(rstd[:, n, 0:1], meanvar[:, n, 1:2], EPS, None, ALU.add).then_inc(done, 1)

                def finish():
                    d.wait_ge(rooted[n], t + 1)
                    return V.tensor_scalar(dst, src, meanvar[:, n, 0:1], rstd[:, n, 1:2], ALU.subtract, ALU.mult)
                return finish

            def weigh(s, half, first=False):
                cs = slice(half * 4, half * 4 + 4)
                d.wait_ge(y_psum, 2 * s + (half + 1))
                if half == 0 and not first:
                    d.wait_ge(tree, 3 * s - 2)
                V.tensor_tensor(z[:, cs, :], B[1 + half][:].rearrange("p (c d) -> p c d", c=4),
                                spread(v[:, bass.ds(s, 1), cs].rearrange("p o c -> p (o c)"), 2, [P, 4, DIM]),
                                ALU.mult).then_inc(z_sb, 1)

            def tile_h(t):
                return one(h[:, bass.ds(t, 1), :])

            def first_norm(t):
                d.wait_ge(h_psum, t + 1)
                V.tensor_tensor(tile_h(t), B[3][:, P:P + DIM], tokb[:], ALU.add).then_inc(h_read, 1)
                d.wait_ge(h_read, t + 1)
                carry()
                layer_norm(0, ln1, t, tile_h(t), xn[:])().then_inc(xn_ready, 1)
                V.tensor_tensor(tile_h(t), tile_h(t), bout[:], ALU.add).then_inc(h_biased, 1)

            def x_lo(t):
                d.wait_ge(xT_hi, 2 * t + 2)
                remainder(xTl[:], B[3][:, 2 * P:3 * P], xTh[:], xT_lo)

            def features_lo(s):
                d.wait_ge(u4_hi, 2 * s + 2)
                remainder(utl[:].rearrange("p c t -> p (c t)"), B[0][:], uth[:].rearrange("p c t -> p (c t)"),
                          u4_lo)
                rows_ = slice(C2, P)
                remainder(lowt[rows_, 0, :], B[3][rows_, 0:P], lowt[rows_, 0, :], u4_lo)
                rows_ = slice(C2 + 2 * FEW_STEP, STACKED)
                remainder(lowt[rows_, 1, :], B[3][rows_, 3 * P:], lowt[rows_, 1, :], u4_lo)

            def residual(t):
                d.wait_ge(att_psum, t + 1)
                d.wait_ge(h_biased, t + 1)
                V.scalar_tensor_tensor(tile_h(t), B[7][:, 0:DIM], fac[:, 6:7], tile_h(t), ALU.mult, ALU.add) \
                    .then_inc(h2_done, 1)

            def second_norm(t, first=False):
                if not first:
                    d.wait_ge(x2_kept, t)
                    d.wait_ge(x2T_psum, t)
                d.wait_ge(h2_done, t + 1)
                carry()
                finish = layer_norm(1, ln2, t, tile_h(t), x2n[:])
                return lambda: finish().then_inc(x2_ready, 1)

            def keep_logits(t):
                d.wait_ge(lg_psum, t + 1)
                V.tensor_copy(one(logits[:, bass.ds(t, 1), :]), B[4][:, P:P + EXPERTS]).then_inc(lg_sb, 1)

            def x_group_lo(g, k):
                d.wait_ge(xg_hi, g + 1)
                remainder(xgl[k], xg_in[:, k, :], xgh[k], xg_lo)

            def iteration(i, f, u, acc, prev=True):
                if is_tile(i, LAST_BUT_ONE):
                    x_group_lo(0, 0)
                if acc:
                    first_norm(i + 1)
                if is_tile(i, LAST):
                    x_group_lo(1, 1)
                d.wait_ge(s_psum, i + 1)
                sc = B[4][:].rearrange("p (c k) -> p c k", k=LEN)
                V.tensor_reduce(rowmax[:], sc, AX, ALU.max).then_inc(soft, 1)
                d.wait_ge(soft, i + 1)
                V.tensor_tensor(prob[:], sc, spread(rowmax[:], 2, [P, HEADS, LEN]), ALU.subtract) \
                    .then_inc(shifted, 1)
                d.wait_ge(exp_done, i + 1)
                V.reduce_sum(rinv[:, 0, :], prob[:], axis=AX).then_inc(summed, 1)
                d.wait_ge(summed, 2 * i + 1)
                V.reciprocal(rinv[:, 1, :], rinv[:, 0, :]).then_inc(summed, 1)
                d.wait_ge(summed, 2 * i + 2)
                V.tensor_tensor(prob[:], prob[:], spread(rinv[:, 1, :], 2, [P, HEADS, LEN]), ALU.mult) \
                    .then_inc(normalised, 1)
                if acc:
                    x_lo(i + 1)
                d.wait_ge(p_psum, i + 1)
                V.tensor_copy(pz[LEN:P, :, :, 1, :],
                              B[6][LEN:P, :].rearrange("k (c h q) -> k c h q", c=PAIRS, h=2)).then_inc(pB_sb, 1)
                if u:
                    weigh(i + 2, 0)
                if f:
                    level4(i + 3)
                if prev:
                    keep_logits(i - 1)
                residual(i)
                if u:
                    weigh(i + 2, 1)
                finish = second_norm(i, not prev)
                if f:
                    features_lo(i + 3)
                finish()

            features_lo(0)
            after(rest_made)
            add_s2(1)
            assert n_small == SECOND_GROUP_STEPS
            add_s2(2)
            add_s2(3)
            assert n_small == SMALL_STEPS
            d.wait_ge(ld_c, 80)
            V.tensor_copy(ident_b[:], ident).then_inc(consts_cast, 1)
            V.tensor_copy(mask[:], maskf).then_inc(consts_cast, 1)

            nq = 3 * INNER // P
            n_norm = 0

            def nstep(ins):
                nonlocal n_norm
                ins.then_inc(norm_step, 1)
                n_norm += 1
                d.wait_ge(norm_step, n_norm)

            d.wait_ge(consts_cast, 2)
            weigh(0, 0, True)
            weigh(0, 1)
            level4(1)
            features_lo(1)
            d.wait_ge(wu_ready, 1)
            V.reduce_sum(wu[:, 0:nq], wu_terms[:, 0:3 * INNER].rearrange("p (c d) -> p c d", d=DIM), axis=AX)
            nstep(V.reduce_sum(wu[:, nq:nq + 1], wu_terms[:, 3 * INNER:], axis=AX))
            for n in range(2):
                d.wait_ge(ww_hi, n + 1)
                cols = slice(n * 512, (n + 1) * 512)
                remainder(vow[:, 1, cols], B[5 - n][:], vow[:, 0, cols], ww_lo)
            nstep(V.tensor_tensor(sqs[:], wu[:], wu[:], ALU.mult))
            V.reduce_sum(nrm[:, 0:1], sqs[:, 0:nq], axis=AX)
            V.tensor_copy(nrm[:, 2:3], sqs[:, nq:nq + 1])
            first_norm(0)
            d.wait_ge(norm_mm, 1)
            row = slice(0, 1)
            V.tensor_copy(wtwu[row, 0:DIM], B[6][row, 0:DIM])
            nstep(V.tensor_copy(wtwu[row, INNER:], B[7][row, :]))
            V.tensor_tensor(wtwu[row, 0:DIM], wtwu[row, 0:DIM], wtwu[row, 0:DIM], ALU.mult)
            nstep(V.tensor_tensor(wtwu[row, INNER:], wtwu[row, INNER:], wtwu[row, INNER:], ALU.mult))
            V.reduce_sum(nrm[row, 1:2], wtwu[row, 0:DIM], axis=AX)
            nstep(V.reduce_sum(nrm[row, 3:4], wtwu[row, INNER:], axis=AX))
            level4(2)
            d.wait_ge(norm_mm, 2)
            V.reciprocal(fac[:, 6:8], B[6][:, 256:260][:, 1:4:2]).then_inc(recip, 1)
            d.wait_ge(recip, 1)
            nstep(V.tensor_tensor(fac[:, 2:4], B[6][:, 256:260][:, 0:4:2], fac[:, 6:8], ALU.mult))
            x_lo(0)
            weigh(1, 0)
            d.wait_ge(norm_root, 1)
            nstep(V.tensor_tensor(fac[:, 4:6], fac[:, 2:4], scal[:, 0:2], ALU.mult))
            d.wait_ge(exp_temp, 1)
            nstep(V.tensor_tensor(fac[:, 1:2], fac[:, 4:5], fac[:, 4:5], ALU.mult))
            nstep(V.tensor_tensor(fac[:, 1:2], fac[:, 1:2], fac[:, 0:1], ALU.mult))
            nstep(V.tensor_tensor(fac[:, 6:7], fac[:, 4:5], fac[:, 5:6], ALU.mult))
            assert n_norm == NORM_STEPS
            weigh(1, 1)
            features_lo(2)
            iteration(0, True, True, True, False)
            d.wait_ge(sw_hi, 1)
            remainder(sw1[:, 1, :], sw1_in, sw1[:, 0, :], sw_lo)
            with d.Fori(1, TILES - 3) as i:
                iteration(i, True, True, True)
            iteration(TILES - 3, False, True, True)
            iteration(TILES - 2, False, False, True)
            V.memset(zeros[:], 0.0)
            iteration(TILES - 1, False, False, False)
            keep_logits(TILES - 1)

            x_group_lo(2, 0)

            def add_shared(g, k):
                d.wait_ge(down_psum, g + 1)
                hg = h[:, bass.ds(g * GROUP, GROUP), :].rearrange("p t d -> p (t d)")
                V.tensor_tensor(hg, hg, B[5 + k][:], ALU.add).then_inc(added, 1)

            n_route = 0

            def rstep(ins):
                nonlocal n_route
                ins.then_inc(route, 1)
                n_route += 1
                d.wait_ge(route, n_route)

            te = [P, TILES, EXPERTS]
            d.wait_ge(lg_sb, TILES)
            rstep(V.tensor_reduce(best[:, 0, :], logits[:], AX, ALU.max))
            rstep(V.tensor_tensor(pick[:], logits[:], spread(best[:, 0, :], 2, te), ALU.is_equal))
            rstep(V.tensor_tensor(pick[:], pick[:], spread(rev_expert, 1, te), ALU.mult))
            rstep(V.tensor_reduce(best[:, 1, :], pick[:], AX, ALU.max))
            rstep(V.tensor_tensor(oh[:], spread(rev_expert, 1, te), spread(best[:, 1, :], 2, te), ALU.is_equal))
            d.wait_ge(rank_psum, 1)
            te_bank = B[7][:, 0:TILES * EXPERTS].rearrange("p (t e) -> p e t", e=EXPERTS)
            rstep(V.tensor_copy(tot[:], te_bank))
            rstep(V.tensor_tensor_scan(incl[:].rearrange("p e t -> p (e t)"),
                                       tot[:].rearrange("p e t -> p (e t)"), zeros[:], 0.0, ALU.add, ALU.add))
            last = incl[:, :, TILES - 1]
            start, count, ntiles, end_t, base = (rt[:, n, :] for n in range(5))
            V.memset(start[:, 0:1], 0.0)
            rstep(V.tensor_copy(start[:, 1:EXPERTS], last[:, 0:EXPERTS - 1]))
            rstep(V.tensor_tensor(count, last, start, ALU.subtract))
            rstep(V.tensor_tensor(over[:], spread(count, 2, [P, EXPERTS, TILES]),
                                  spread(tile_edges, 1, [P, EXPERTS, TILES]), ALU.is_gt))
            rstep(V.reduce_sum(ntiles, over[:], axis=AX))
            rstep(V.tensor_tensor_scan(end_t, ntiles, zeros[:, 0:EXPERTS], 0.0, ALU.add, ALU.add))
            rstep(V.tensor_tensor(base, end_t, ntiles, ALU.subtract))
            rstep(V.scalar_tensor_tensor(base, base, float(P), start, ALU.mult, ALU.subtract))
            rstep(V.tensor_tensor(off[:], incl[:], tot[:], ALU.subtract))
            rstep(V.tensor_tensor(off[:], off[:], spread(base, 2, [P, EXPERTS, TILES]), ALU.add))
            rstep(V.tensor_tensor(pick[:], off[:].rearrange("p e t -> p t e"),
                                  B[4][:, 0:TILES * EXPERTS].rearrange("p (t e) -> p t e", e=EXPERTS), ALU.add))
            rstep(V.tensor_tensor(pick[:], pick[:], oh[:], ALU.mult))
            rstep(V.reduce_sum(pos_f[:], pick[:], axis=AX))
            V.tensor_copy(pos[:], pos_f[:]).then_inc(pos_ready, 1)
            x_group_lo(3, 1)
            add_shared(0, 0)
            se = [P, SORTED, EXPERTS]
            rstep(V.tensor_tensor(upt[:], spread(end_t, 1, se), spread(tile_index, 2, se), ALU.is_le))
            rstep(V.reduce_sum(exp_f[:], upt[:], axis=AX))
            V.tensor_scalar(exp_i[:], exp_f[:], float(EXPERTS - 1), None, ALU.min).then_inc(pos_ready, 1)
            assert n_route == ROUTE_STEPS

            with d.Fori(2, GROUPS - 3, 2) as g:
                for k in range(2):
                    x_group_lo(g + (k + 2), k)
                    add_shared(g + (k - 1), 1 - k)
                    for m in range(2):
                        e = (g + (k - 2)) * 2 + m
                        d.wait_ge(w1_hi, e + 1)
                        lo, w, hi = (x[:, bass.ds(e, 1), 0:HIDDEN].rearrange("p o n -> p (o n)")
                                     for x in (w1l, w13, w1h))
                        remainder(lo, w, hi, w1_lo)
            add_shared(GROUPS - 3, 1)
            add_shared(GROUPS - 2, 0)
            add_shared(GROUPS - 1, 1)

            def keep_ids(j, k):
                d.wait_ge(rows_in[k], (j - k) * 8 + 16)
                V.tensor_copy(ids[:, bass.ds(j, 1)], rows[:, k, DIM:ROW].bitcast(U32)).then_inc(id_kept, 1)

            def gate(j, k):
                d.wait_ge(silu_done, j + 1)
                V.tensor_tensor(hid[:, k, :], act[:, k, :], B[2 + 2 * k][:], ALU.mult).then_inc(hid_done, 1)

            def rows_lo(j, k):
                d.wait_ge(rT_hi, 2 * j + 2)
                remainder(rowsTl[:, k, :], B[7 * k][:, 0:P], rowsTh[:, k, :], rT_lo)

            def hidden_transposed(j, k):
                d.wait_ge(hT_psum, j + 1)
                V.tensor_copy(hidT[:, k, :, :].rearrange("p c t -> p (c t)"), B[5][:]).then_inc(hT_sb, 1)

            keep_ids(0, 0)
            keep_ids(1, 1)
            rows_lo(0, 0)
            rows_lo(1, 1)
            gate(0, 0)
            hidden_transposed(0, 0)
            rows_lo(2, 0)
            gate(1, 1)
            keep_ids(2, 0)
            with d.Fori(1, SORTED - 3, 2) as i:
                for k in range(2):
                    hidden_transposed(i + k, 1 - k)
                    rows_lo(i + (k + 2), 1 - k)
                    gate(i + (k + 1), k)
                    keep_ids(i + (k + 2), 1 - k)
            hidden_transposed(SORTED - 2, 1)
            gate(SORTED - 1, 0)
            hidden_transposed(SORTED - 1, 0)

        @block.tensor
        def _(pe):
            T = nc.tensor

            def mm(out_, lhsT, rhs, start=True, stop=True):
                return T.matmul(out_, lhsT, rhs, start=start, stop=stop)

            def col(c, n=P):
                return slice(c * n, (c + 1) * n)

            def place(hd):
                return hd % 2 * PAIRS + hd // 2

            pe.wait_ge(ld_sq, 16)
            pe.wait_ge(small, 1)
            mm(B[1][:, 0:TILES * CHANNELS], before, v[:].rearrange("p t c -> p (t c)")).then_inc(s1_psum, 1)
            per = 512 // C2
            for n in range(TILES // per):
                pe.wait_ge(small, E2_STEPS[n])
                mm(B[SUM_BANKS[n]][:], before, e2[:, n * per:(n + 1) * per, :].rearrange("p t c -> p (t c)")) \
                    .then_inc(s2_psum, 1)

            def weight_products(banks, left, right):
                for n in range(2):
                    rows_ = slice(n * HEAD_DIM, (n + 1) * HEAD_DIM)
                    for c in range(PAIRS):
                        last = mm(banks[n][:, col(c)], wqkv_sb[rows_, left + c, :], right[rows_, c, :])
                    last.then_inc(ww_psum, 1)

            def norm_columns():
                nq = 3 * INNER // P
                pe.wait_ge(norm_step, 1)
                pe.wait_ge(qkw_sb, 2)
                for c in range(nq):
                    mm(B[6][0:1, 0:DIM], wu[:, c:c + 1], wqkv_sb[:, c, :], c == 0, c == nq - 1)
                mm(B[7][0:1, :], wu[:, nq:nq + 1], wout_sb).then_inc(norm_mm, 1)

            def sum_level3(s):
                pe.wait_ge(e3_lo, s + 1)
                mm(B[0][:], before_r[:], e3h[:], True, False)
                mm(B[0][:], before_r[:], e3l[:], False, True).then_inc(s3_psum, 1)

            def features(s, read=True):
                pe.wait_ge(u4_sb, s + 1)
                for c in range(UC):
                    T.transpose(B[0][:, col(c)], u4[:, col(c)], ident)
                pe.wait_ge(low_ready, 2 * s + 2)
                if read:
                    pe.wait_ge(xT_lo, s - 1)
                T.transpose(B[3][:, 0:P], low_tile[:, 0:P], ident)
                T.transpose(B[3][:, 3 * P:], low_tile[:, P:], ident).then_inc(u4_psum, 1)

            def project(s, lo, hi, first=False):
                if lo == 0:
                    if not first:
                        pe.wait_ge(z_sb, 2 * s)
                    pe.wait_ge(u4_hi, 2 * s + 2)
                    pe.wait_ge(u4_lo, 3 * s + 3)
                for n in range(lo, hi):
                    half_, c = divmod(n, UC + 1)
                    if first:
                        pe.wait_ge(w_lo if c < UC - 1 else w_lo_pool, c + 1 if c < UC - 1 else c - UC + 2)
                    bank, cols = B[1 + half_][:], col(half_, 512)
                    if c < UC:
                        mm(bank, uth[:, c, :], whigh[:, 0, c, cols], c == 0, False)
                        mm(bank, uth[:, c, :], whigh[:, 1, c, cols], False, False)
                        mm(bank, utl[:, c, :], whigh[:, 0, c, cols], False, False)
                    else:
                        mm(bank, lowt[:, 0, :], wlow[:, 0, cols], False, False)
                        mm(bank, lowt[0:STACKED, 1, :], wlow[0:STACKED, 1, cols], False, True).then_inc(y_psum, 1)

            def accumulate(s):
                pe.wait_ge(tree, 3 * s + 3)
                mm(B[3][:, P:P + DIM], upto, z1[:]).then_inc(h_psum, 1)

            def x_columns(t):
                pe.wait_ge(xn_ready, t + 1)
                T.transpose(B[3][:, 2 * P:3 * P], xn[:], ident).then_inc(xT_psum, 1)

            def three(out_, lhs, rhs):
                mm(out_, lhs[0], rhs[0], True, False)
                mm(out_, lhs[0], rhs[1], False, False)
                return mm(out_, lhs[1], rhs[0], False, True)

            def x2_columns(t):
                pe.wait_ge(x2_ready, t + 1)
                T.transpose(B[4][:, 0:P], x2n[:], ident).then_inc(x2T_psum, 1)

            def router(t):
                pe.wait_ge(x2T_sb, t + 1)
                mm(B[4][:, P:P + EXPERTS], x2t[:], gateT[:]).then_inc(lg_psum, 1)

            def up(g, k, chunks=range(HC), first=False):
                pe.wait_ge(xg_lo, g + 1)
                for c in chunks:
                    if not first:
                        pe.wait_ge(gelu_done, g * HC + (c + 1 - HC))
                    three(B[c][:], [sw1[:, n, col(c)] for n in range(2)], (xgh[k], xgl[k])) \
                        .then_inc(up_psum, 1)

            def down(g, k, tiles=range(GROUP), first=False):
                pe.wait_ge(gelu_done, (g + 1) * HC)
                if not first:
                    pe.wait_ge(added, g - 1)
                for t in tiles:
                    for c in range(HC):
                        last = mm(B[5 + k][:, col(t)], gelu[k][c][:, col(t)], sw2[:, c, :],
                                  c == 0, c == HC - 1)
                if GROUP - 1 in tiles:
                    last.then_inc(down_psum, 1)

            def iteration(i, f, u, acc, prev=True):
                x = (xTh[:], xTl[:])
                pe.wait_ge(xT_hi, 2 * i + 2)
                if prev:
                    pe.wait_ge(vo_sb, 2 * i)
                for hd in range(HEADS):
                    by_pair = B[5 + hd // 4][:].rearrange("p (c s h q) -> p c h s q", c=2, s=2, h=2)
                    last = mm(by_pair[:, hd // 2 % 2, hd % 2, :, :], qkw[:, place(hd), :], xT[:])
                    if hd % 4 == 3:
                        last.then_inc(g_psum, 1)
                pe.wait_ge(xT_lo, i + 1)
                if prev:
                    pe.wait_ge(h2_done, i)
                three(B[7][:], x, [vow[:, n, 0:512] for n in range(2)]).then_inc(vo_psum, 1)
                pe.wait_ge(g_sb, 2 * i + 1)
                three(B[5][:], x, [vow[:, n, 512:] for n in range(2)]).then_inc(vo_psum, 1)
                if u:
                    project(i + 2, 0, 1)
                if acc:
                    accumulate(i + 1)
                pe.wait_ge(g_sb, 2 * i + 2)
                T.matmul(B[4][:], ident_b[:], mask[:], start=True, stop=False)
                for c in range(PAIRS):
                    for s in range(2):
                        last = mm(B[4][:, col(2 * c + s, LEN)],
                                  xqk[:, c, s, :, :].rearrange("p h q -> p (h q)"),
                                  xT[:, col(s, LEN)], False, c == PAIRS - 1 and s == 1)
                last.then_inc(s_psum, 1)
                if u:
                    project(i + 2, 1, 5)
                if is_tile(i, LAST_BUT_ONE):
                    pe.wait_ge(z_sb, 2 * TILES)
                    pe.wait_ge(sw_lo, 1)
                    up(0, 0, range(HC - 1), True)
                if is_tile(i, LAST):
                    up(0, 0, range(HC - 1, HC), True)
                    up(1, 1, range(HC - 1))
                if acc:
                    x_columns(i + 1)
                if u:
                    project(i + 2, 5, 8)
                pe.wait_ge(normalised, i + 1)
                for c in range(PAIRS):
                    last = T.transpose(B[6][:, col(c)], prob[:, 2 * c:2 * c + 2, :].rearrange("p s k -> p (s k)"),
                                       ident)
                last.then_inc(p_psum, 1)
                if prev:
                    x2_columns(i - 1)
                if u:
                    project(i + 2, 8, 9)
                if f:
                    sum_level3(i + 3)
                if is_tile(i, LAST):
                    down(0, 0, range(1), True)
                pe.wait_ge(vo_sb, 2 * i + 2)
                pe.wait_ge(pA_sb, i + 1)
                pe.wait_ge(pB_sb, i + 1)
                for hd in range(HEADS):
                    last = mm(B[7][:, 0:DIM], pz[:, hd // 2, hd % 2, :, :].rearrange("k s q -> k (s q)"),
                              xvo[:, place(hd), :], hd == 0, hd == HEADS - 1)
                last.then_inc(att_psum, 1)
                if prev:
                    router(i - 1)
                if is_tile(i, LAST):
                    down(0, 0, range(1, GROUP), True)
                if u:
                    project(i + 2, 9, 10)
                if f:
                    features(i + 3)

            pe.wait_ge(before_cast, 1)
            sum_level3(0)
            features(0, False)
            pe.wait_ge(ld_w, 32)
            weight_products(B[6:8], 0, wqkv_sb[:, PAIRS:2 * PAIRS, :])
            for lo in (0, UC + 1, UC, 2 * UC + 1):
                if lo == UC + 1:
                    pe.wait_ge(small, SECOND_GROUP_STEPS)
                project(0, lo, lo + (UC if lo % (UC + 1) == 0 else 1), True)
            sum_level3(1)
            features(1, False)
            pe.wait_ge(small, SMALL_STEPS)
            weight_products((B[5], B[4]), 2 * PAIRS, woutT)
            project(1, 0, UC + 1)
            accumulate(0)
            norm_columns()
            sum_level3(2)
            project(1, UC + 1, 8)
            x_columns(0)
            pe.wait_ge(norm_step, 5)
            mm(B[6][:, 256:260], ones, nrm[:]).then_inc(norm_mm, 1)
            project(1, 8, 10)
            features(2)
            pe.wait_ge(consts_cast, 2)
            pe.wait_ge(ww_lo, 2)
            pe.wait_ge(norm_step, 6)
            iteration(0, True, True, True, False)
            with pe.Fori(1, TILES - 3) as i:
                iteration(i, True, True, True)
            iteration(TILES - 3, False, True, True)
            iteration(TILES - 2, False, False, True)
            iteration(TILES - 1, False, False, False)
            pe.wait_ge(lg_sb, TILES - 1)
            x2_columns(TILES - 1)
            up(1, 1, range(HC - 1, HC))
            router(TILES - 1)
            up(2, 0)
            pe.wait_ge(route, 5)
            mm(B[4][:, 0:TILES * EXPERTS], below, oh[:].rearrange("p t e -> p (t e)"))
            mm(B[7][:, 0:TILES * EXPERTS], ones, oh[:].rearrange("p t e -> p (t e)")).then_inc(rank_psum, 1)
            down(1, 1, first=True)
            with pe.Fori(2, GROUPS - 3, 2) as g:
                up(g + 1, 1)
                down(g, 0)
                up(g + 2, 0)
                down(g + 1, 1)
            up(GROUPS - 1, 1)
            down(GROUPS - 2, 0)
            down(GROUPS - 1, 1)

            def expert(j):
                return pe.value_load(exp_i[0:1, bass.ds(j, 1)], min_val=0, max_val=EXPERTS - 1)

            def rows_in_columns(j, k, first=False):
                pe.wait_ge(rows_in[k], (j - k) * 8 + 16)
                if not first:
                    pe.wait_ge(rT_lo, j - 1)
                T.transpose(B[7 * k][:, 0:P], rows[:, k, 0:DIM], ident).then_inc(rT_psum, 1)

            def expert_up(j, k, e, first=False):
                if not first:
                    pe.wait_ge(hid_done, j - 1)
                pe.wait_ge(rT_hi, 2 * j + 2)
                hi, lo, w3 = (w[:, bass.ds(e, 1), cols].rearrange("p o i -> p (o i)") for w, cols in
                              ((w1h, col(0, HIDDEN)), (w1l, col(0, HIDDEN)), (w13, col(1, HIDDEN))))
                mm(B[2 + 2 * k][:], rowsT[:, k, :], w3)
                pe.wait_ge(rT_lo, j + 1)
                three(B[1 + 2 * k][:], (rowsTh[:, k, :], rowsTl[:, k, :]), (hi, lo)).then_inc(eu_psum, 1)

            def hidden_in_columns(j, k, first=False):
                pe.wait_ge(hid_done, j + 1)
                if not first:
                    pe.wait_ge(hT_sb, j)
                for c in range(HC):
                    last = T.transpose(B[5][:, col(c)], hid[:, k, col(c)], ident)
                last.then_inc(hT_psum, 1)

            def expert_down(j, k, e, first=False):
                pe.wait_ge(hT_sb, j + 1)
                if not first:
                    pe.wait_ge(y_done, j)
                for c in range(HC):
                    last = mm(B[6][:, 0:DIM], hidT[:, k, c, :],
                              w2[:, bass.ds(e, 1), c, :].rearrange("p o d -> p (o d)"), c == 0, c == HC - 1)
                last.then_inc(ed_psum, 1)

            pe.wait_ge(pos_ready, 2)
            pe.wait_ge(added, GROUPS)
            pe.wait_ge(ld_w2, 16)
            pe.wait_ge(w1_lo, EXPERTS)
            rows_in_columns(0, 0, True)
            rows_in_columns(1, 1, True)
            expert_up(0, 0, expert(0), True)
            expert_up(1, 1, expert(1), True)
            hidden_in_columns(0, 0, True)
            rows_in_columns(2, 0)
            expert_up(2, 0, expert(2))
            hidden_in_columns(1, 1)
            rows_in_columns(3, 1)
            expert_down(0, 0, expert(0), True)
            done = SORTED - 3 - (SORTED - 3 - 2) % EXPERT_UNROLL
            with pe.Fori(2, done - EXPERT_UNROLL + 1, EXPERT_UNROLL) as j:
                e = {1: expert(j + 1)}
                for n in range(EXPERT_UNROLL):
                    k = n % 2
                    expert_up(j + (n + 1), 1 - k, e[n + 1])
                    if n < 2:
                        e[n - 1] = expert(j + (n - 1))
                    if n < EXPERT_UNROLL - 1:
                        e[n + 2] = expert(j + (n + 2))
                    hidden_in_columns(j + n, k)
                    rows_in_columns(j + (n + 2), k)
                    expert_down(j + (n - 1), 1 - k, e[n - 1])
            for j in range(done, SORTED + 1):
                if j + 1 < SORTED:
                    expert_up(j + 1, (j + 1) % 2, expert(j + 1))
                if j < SORTED:
                    hidden_in_columns(j, j % 2)
                if j + 2 < SORTED:
                    rows_in_columns(j + 2, j % 2)
                expert_down(j - 1, (j - 1) % 2, expert(j - 1))


_IN = ["x_next", "x_prev", "w_low", "w_high", "tok_b", "wqkv", "u_qkv", "wout_t", "wout", "u_out",
       "b_out", "scalars", "gate_t", "w13_t", "w2_t", "sw1_t", "sw2_t", "square", "mask_c", "steps"]


def kernel(x, L0_tok_W, L0_tok_b, L0_attn_w_qkv, L0_attn_u_qkv, L0_attn_sigma_qkv, L0_attn_w_out,
           L0_attn_b_out, L0_attn_u_out, L0_attn_sigma_out, L0_attn_temperature, L0_ffn_gate_w,
           L0_ffn_w1, L0_ffn_w2, L0_ffn_w3, L0_ffn_sw1, L0_ffn_sw2):
    import numpy as np
    import concourse.bacc as bacc
    from concourse.bass_utils import run_bass_kernel_spmd

    time = np.arange(LEN, dtype=np.float32) * (np.float32(1) / np.float32(LEN - 1))
    path = np.concatenate([np.broadcast_to(time[None, :, None], (SEQS, LEN, 1)), np.asarray(x)], axis=-1)

    def tokens(a):
        padded = np.zeros((SEQS, LEN, CHANNELS), np.float32)
        padded[:, :LEN - 1] = a
        return padded.reshape(TILES, P, CHANNELS).transpose(1, 0, 2)

    def on_all(a):
        a = np.asarray(a)
        return np.broadcast_to(a.reshape(1, -1), (P, a.size))

    w = np.asarray(L0_tok_W).reshape(DIM, LOW + C3, CHANNELS).transpose(1, 2, 0).reshape(LOW + C3, -1)
    gap = np.zeros((FEW_STEP - FEW, w.shape[1]), np.float32)
    w1, w2, w3 = np.asarray(L0_ffn_w1), np.asarray(L0_ffn_w2), np.asarray(L0_ffn_w3)
    wqkv, wout = np.asarray(L0_attn_w_qkv), np.asarray(L0_attn_w_out)
    n = np.arange(P)
    same = n[:, None] // LEN == n[None, :] // LEN
    key = np.arange(C3) % LEN
    masked = (key[None, :] == n[:, None] % LEN) | (key[None, :] == LEN - 1)
    arrays = {
        "x_next": tokens(path[:, 1:]),
        "x_prev": tokens(path[:, :-1]),
        "w_low": np.stack([np.concatenate([w[FEW:LOW], w[FEW:LOW]]),
                           np.concatenate([w[FEW:LOW], w[:FEW], gap, w[:FEW], gap, w[:FEW],
                                           np.zeros((P - STACKED, w.shape[1]), np.float32)])], axis=1),
        "w_high": w[LOW:].reshape(UC, P, -1).transpose(1, 0, 2),
        "tok_b": on_all(L0_tok_b),
        "wqkv": wqkv.reshape(-1, P, DIM).transpose(1, 0, 2),
        "u_qkv": on_all(L0_attn_u_qkv),
        "wout_t": wout.T.reshape(PAIRS, P, DIM).transpose(1, 0, 2),
        "wout": wout,
        "u_out": on_all(L0_attn_u_out),
        "b_out": on_all(L0_attn_b_out),
        "scalars": np.stack([np.broadcast_to(np.asarray(s), (P,)) for s in
                             (L0_attn_sigma_qkv, L0_attn_sigma_out, L0_attn_temperature)], axis=1),
        "gate_t": np.asarray(L0_ffn_gate_w).T,
        "w13_t": np.concatenate([w1, w3], axis=1).transpose(2, 0, 1),
        "w2_t": w2.reshape(EXPERTS, DIM, HC, P).transpose(3, 0, 2, 1),
        "sw1_t": np.asarray(L0_ffn_sw1).T,
        "sw2_t": np.asarray(L0_ffn_sw2).T.reshape(HC, P, DIM).transpose(1, 0, 2),
        "square": np.stack([n[:, None] == n[None, :], same & (n[:, None] < n[None, :]),
                            same & (n[:, None] <= n[None, :]), n[:, None] < n[None, :],
                            np.ones((P, P), bool)], axis=1).astype(np.float32),
        "mask_c": np.where(masked, np.float32(-3e38), np.float32(0)),
        "steps": on_all(np.concatenate([EXPERTS - np.arange(EXPERTS), P * np.arange(TILES),
                                        np.arange(SORTED)]).astype(np.float32)),
    }
    arrays = {k: np.ascontiguousarray(a) for k, a in arrays.items()}
    nc = bacc.Bacc("TRN2", target_bir_lowering=False, num_devices=1)
    args = [nc.dram_tensor(k, arrays[k].shape, F32, kind="ExternalInput").ap() for k in _IN]
    out = nc.dram_tensor("out", (TILES * P, DIM), F32, kind="ExternalOutput").ap()
    build(nc, *args, out)
    r = run_bass_kernel_spmd(nc, [arrays], core_ids=[0])
    return r.results[0]["out"].reshape(SEQS, LEN, DIM)[:, :LEN - 1]
```
